# Optimizing a Trainium2 kernel written in Bass

```python
import numpy as np
import jax
import jax.numpy as jnp

def _softmax(x, axis=-1):
    return jax.nn.softmax(x, axis=axis)

def _gelu(x):
    return jax.nn.gelu(x, approximate=True)

def _silu(x):
    return jax.nn.silu(x)

def _sigmoid(x):
    return jax.nn.sigmoid(x)

def _layernorm(x, axis=-1, eps=1e-05):
    m = jnp.mean(x, axis=axis, keepdims=True)
    v = jnp.var(x, axis=axis, keepdims=True)
    return (x - m) / jnp.sqrt(v + eps)

def _scatter_add(tgt, idx, src, axis=0):
    return tgt.at[idx].add(src)

def _segment_sum(src, seg, n):
    return jax.ops.segment_sum(src, seg, n)
kernel_name = 'mk_gnn_resnorm_d4_gnn_r64_bca170'

def setup_inputs(seed: int=0):
    np.random.seed(seed)
    _w = jnp.asarray

    def _rec_inputs():
        import jax
        import jax.numpy as jnp
        _gk = jax.random.key(seed)
        x = -0.0003929 + 0.9999 * jax.random.normal(jax.random.fold_in(_gk, 1), (512, 512), jnp.float32)
        src = jax.random.randint(jax.random.fold_in(_gk, 2), (8192,), 0, 512, jnp.int32)
        dst = jax.random.randint(jax.random.fold_in(_gk, 3), (8192,), 0, 512, jnp.int32)
        _o = jnp.argsort(dst, stable=True)
        src = src[_o]
        dst = dst[_o]
        edge_attr_64 = 0.000189758 + 1.00013 * jax.random.normal(jax.random.fold_in(_gk, 13), (8192, 64), jnp.float32)
        edge_attr_8 = -4.48278e-06 + 1.00019 * jax.random.normal(jax.random.fold_in(_gk, 14), (8192, 8), jnp.float32)
        return (x, src, dst, edge_attr_64, edge_attr_8)
    x, src, dst, edge_attr_64, edge_attr_8 = _rec_inputs()

    def _L0_gnn_setup():
        import jax, jax.numpy as jnp
        import numpy as np
        L, C, H, E = (512, 512, 8, 16384)
        D = C // H
        HID = 1024
        EPS = 1e-05

        def _ln(x, g, b):
            mu = jnp.mean(x, axis=-1, keepdims=True)
            var = jnp.var(x, axis=-1, keepdims=True)
            return (x - mu) * jax.lax.rsqrt(var + EPS) * g + b

        def _sparse_attention(z, row, col, bias, Wq, bq, Wk, bk, Wv, bv, Wo, bo):
            q = (z @ Wq + bq).reshape(L, H, D)
            k = (z @ Wk + bk).reshape(L, H, D)
            v = (z @ Wv + bv).reshape(L, H, D)
            scale = 1.0 / jnp.sqrt(jnp.asarray(D, z.dtype))
            scores = jnp.einsum('ehd,ehd->eh', q[row], k[col]) * scale + bias
            m = jax.ops.segment_max(scores, row, num_segments=L)
            p = jnp.exp(scores - m[row])
            ssum = jax.ops.segment_sum(p, row, num_segments=L)
            alpha = p / ssum[row]
            out = jax.ops.segment_sum(alpha[:, :, None] * v[col], row, num_segments=L)
            return out.reshape(L, C) @ Wo + bo
        key = jax.random.key(seed)
        ks = jax.random.split(key, 12)
        s = 0.02
        inp = {'x': jax.random.normal(ks[0], (L, C), jnp.float32), 'row_index': jnp.sort(jax.random.randint(ks[1], (E,), 0, L)), 'col_index': jax.random.randint(ks[2], (E,), 0, L), 'att_bias': jax.random.normal(ks[3], (E, H), jnp.float32), 'Wq': jax.random.normal(ks[4], (C, C), jnp.float32) * s, 'bq': jnp.zeros((C,), jnp.float32), 'Wk': jax.random.normal(ks[5], (C, C), jnp.float32) * s, 'bk': jnp.zeros((C,), jnp.float32), 'Wv': jax.random.normal(ks[6], (C, C), jnp.float32) * s, 'bv': jnp.zeros((C,), jnp.float32), 'Wo': jax.random.normal(ks[7], (C, C), jnp.float32) * s, 'bo': jnp.zeros((C,), jnp.float32), 'ln1_g': jnp.ones((C,), jnp.float32), 'ln1_b': jnp.zeros((C,), jnp.float32), 'ln2_g': jnp.ones((C,), jnp.float32), 'ln2_b': jnp.zeros((C,), jnp.float32), 'W1': jax.random.normal(ks[8], (C, HID), jnp.float32) * s, 'b1': jnp.zeros((HID,), jnp.float32), 'W2': jax.random.normal(ks[9], (HID, C), jnp.float32) * s, 'b2': jnp.zeros((C,), jnp.float32)}
        return inp
    _L0_gnn_all = _L0_gnn_setup()
    _L0_gnn_in = {k: v for k, v in _L0_gnn_all.items() if k in ('Wq', 'bq', 'Wk', 'bk', 'Wv', 'bv', 'Wo', 'bo', 'ln1_g', 'ln1_b', 'ln2_g', 'ln2_b', 'W1', 'b1', 'W2', 'b2')}
    del _L0_gnn_all

    def _L1_gnn_setup():
        import jax, jax.numpy as jnp
        import numpy as np
        N = 10000
        E = 2500
        H = 4
        C = 256
        D_IN = 512
        D_OUT = 512
        NEG_SLOPE = 0.2

        def gat_conv(x, src, dst, W, a_src, a_dst, bias):
            n = x.shape[0]
            h = (x @ W).reshape(n, H, C)
            al_s = jnp.einsum('nhc,hc->nh', h, a_src)
            al_d = jnp.einsum('nhc,hc->nh', h, a_dst)
            e = jax.nn.leaky_relu(al_s[src] + al_d[dst], NEG_SLOPE)
            emax = jax.ops.segment_max(e, dst, num_segments=n)
            w = jnp.exp(e - emax[dst])
            denom = jax.ops.segment_sum(w, dst, num_segments=n)
            alpha = w / denom[dst]
            out = jax.ops.segment_sum(h[src] * alpha[:, :, None], dst, num_segments=n)
            return out.reshape(n, H * C) + bias
        key = jax.random.key(seed)
        ks = jax.random.split(key, 13)
        s = 0.05
        return {'x': jax.random.normal(ks[0], (N, D_IN), jnp.float32), 'edge_index': jax.random.randint(ks[1], (2, E), 0, N, dtype=jnp.int32), 'W1': jax.random.normal(ks[2], (D_IN, H * C), jnp.float32) * s, 'a_src1': jax.random.normal(ks[3], (H, C), jnp.float32) * s, 'a_dst1': jax.random.normal(ks[4], (H, C), jnp.float32) * s, 'b1': jnp.zeros((H * C,), jnp.float32), 'W2': jax.random.normal(ks[5], (H * C, H * C), jnp.float32) * s, 'a_src2': jax.random.normal(ks[6], (H, C), jnp.float32) * s, 'a_dst2': jax.random.normal(ks[7], (H, C), jnp.float32) * s, 'b2': jnp.zeros((H * C,), jnp.float32), 'Wfc': jax.random.normal(ks[8], (H * C, D_OUT), jnp.float32) * s, 'bfc': jnp.zeros((D_OUT,), jnp.float32)}
    _L1_gnn_all = _L1_gnn_setup()
    _L1_gnn_in = {k: v for k, v in _L1_gnn_all.items() if k in ('W1', 'a_src1', 'a_dst1', 'b1', 'W2', 'a_src2', 'a_dst2', 'b2', 'Wfc', 'bfc')}
    del _L1_gnn_all

    def _L2_gnn_setup():
        import jax, jax.numpy as jnp
        import numpy as np
        N_NODES = 50000
        N_EDGES = 12500
        NODE_IN = 512
        EDGE_IN = 64
        HID = 1024
        key = jax.random.key(seed)
        ks = jax.random.split(key, 6)
        x = jax.random.normal(ks[0], (N_NODES, NODE_IN), dtype=jnp.float32)
        edge_index = jax.random.randint(ks[1], (2, N_EDGES), 0, N_NODES, dtype=jnp.int64)
        edge_attr = jax.random.normal(ks[2], (N_EDGES, EDGE_IN), dtype=jnp.float32)
        u = jnp.zeros((1, 16), dtype=jnp.float32)
        batch = jnp.zeros((N_NODES,), dtype=jnp.int64)
        s1 = 1.0 / np.sqrt(NODE_IN + EDGE_IN)
        s2 = 1.0 / np.sqrt(HID)
        W1 = jax.random.normal(ks[3], (NODE_IN + EDGE_IN, HID), dtype=jnp.float32) * s1
        b1 = jnp.zeros((HID,), dtype=jnp.float32)
        W2 = jax.random.normal(ks[4], (HID, NODE_IN), dtype=jnp.float32) * s2
        b2 = jnp.zeros((NODE_IN,), dtype=jnp.float32)
        return {'x': x, 'edge_index': edge_index, 'edge_attr': edge_attr, 'u': u, 'batch': batch, 'W1': W1, 'b1': b1, 'W2': W2, 'b2': b2}
    _L2_gnn_all = _L2_gnn_setup()
    _L2_gnn_in = {k: v for k, v in _L2_gnn_all.items() if k in ('u', 'W1', 'b1', 'W2', 'b2')}
    del _L2_gnn_all

    def _L3_gnn_setup():
        import jax, jax.numpy as jnp
        import numpy as np
        N_NODES = 20000
        N_EDGES = 5000
        HIDDEN = 512
        EDGE_DIM = 64
        LN_EPS = 1e-05

        def mish(x):
            return x * jnp.tanh(jax.nn.softplus(x))
        key = jax.random.key(seed)
        ks = jax.random.split(key, 8)
        s = lambda fan_in: 1.0 / np.sqrt(fan_in)
        return {'x': jax.random.normal(ks[0], (N_NODES, HIDDEN), dtype=jnp.float32), 'edge_index': jax.random.randint(ks[1], (2, N_EDGES), 0, N_NODES, dtype=jnp.int64), 'edge_attr': jax.random.normal(ks[2], (N_EDGES, EDGE_DIM), dtype=jnp.float32), 'W1': jax.random.normal(ks[3], (2 * HIDDEN + EDGE_DIM, HIDDEN), dtype=jnp.float32) * s(2 * HIDDEN + EDGE_DIM), 'b1': jnp.zeros((HIDDEN,), dtype=jnp.float32), 'W2': jax.random.normal(ks[4], (HIDDEN, HIDDEN), dtype=jnp.float32) * s(HIDDEN), 'b2': jnp.zeros((HIDDEN,), dtype=jnp.float32), 'W3': jax.random.normal(ks[5], (2 * HIDDEN, HIDDEN), dtype=jnp.float32) * s(2 * HIDDEN), 'b3': jnp.zeros((HIDDEN,), dtype=jnp.float32), 'W4': jax.random.normal(ks[6], (HIDDEN, HIDDEN), dtype=jnp.float32) * s(HIDDEN), 'b4': jnp.zeros((HIDDEN,), dtype=jnp.float32), 'gamma': jnp.ones((HIDDEN,), dtype=jnp.float32), 'beta': jnp.zeros((HIDDEN,), dtype=jnp.float32)}
    _L3_gnn_all = _L3_gnn_setup()
    _L3_gnn_in = {k: v for k, v in _L3_gnn_all.items() if k in ('W1', 'b1', 'W2', 'b2', 'W3', 'b3', 'W4', 'b4', 'gamma', 'beta')}
    del _L3_gnn_all
    return {'x': x, 'src': src, 'dst': dst, 'edge_attr_64': edge_attr_64, 'edge_attr_8': edge_attr_8, 'L0_gnn_Wq': _L0_gnn_in['Wq'], 'L0_gnn_bq': _L0_gnn_in['bq'], 'L0_gnn_Wk': _L0_gnn_in['Wk'], 'L0_gnn_bk': _L0_gnn_in['bk'], 'L0_gnn_Wv': _L0_gnn_in['Wv'], 'L0_gnn_bv': _L0_gnn_in['bv'], 'L0_gnn_Wo': _L0_gnn_in['Wo'], 'L0_gnn_bo': _L0_gnn_in['bo'], 'L0_gnn_ln1_g': _L0_gnn_in['ln1_g'], 'L0_gnn_ln1_b': _L0_gnn_in['ln1_b'], 'L0_gnn_ln2_g': _L0_gnn_in['ln2_g'], 'L0_gnn_ln2_b': _L0_gnn_in['ln2_b'], 'L0_gnn_W1': _L0_gnn_in['W1'], 'L0_gnn_b1': _L0_gnn_in['b1'], 'L0_gnn_W2': _L0_gnn_in['W2'], 'L0_gnn_b2': _L0_gnn_in['b2'], 'L1_gnn_W1': _L1_gnn_in['W1'], 'L1_gnn_a_src1': _L1_gnn_in['a_src1'], 'L1_gnn_a_dst1': _L1_gnn_in['a_dst1'], 'L1_gnn_b1': _L1_gnn_in['b1'], 'L1_gnn_W2': _L1_gnn_in['W2'], 'L1_gnn_a_src2': _L1_gnn_in['a_src2'], 'L1_gnn_a_dst2': _L1_gnn_in['a_dst2'], 'L1_gnn_b2': _L1_gnn_in['b2'], 'L1_gnn_Wfc': _L1_gnn_in['Wfc'], 'L1_gnn_bfc': _L1_gnn_in['bfc'], 'L2_gnn_u': _L2_gnn_in['u'], 'L2_gnn_W1': _L2_gnn_in['W1'], 'L2_gnn_b1': _L2_gnn_in['b1'], 'L2_gnn_W2': _L2_gnn_in['W2'], 'L2_gnn_b2': _L2_gnn_in['b2'], 'L3_gnn_W1': _L3_gnn_in['W1'], 'L3_gnn_b1': _L3_gnn_in['b1'], 'L3_gnn_W2': _L3_gnn_in['W2'], 'L3_gnn_b2': _L3_gnn_in['b2'], 'L3_gnn_W3': _L3_gnn_in['W3'], 'L3_gnn_b3': _L3_gnn_in['b3'], 'L3_gnn_W4': _L3_gnn_in['W4'], 'L3_gnn_b4': _L3_gnn_in['b4'], 'L3_gnn_gamma': _L3_gnn_in['gamma'], 'L3_gnn_beta': _L3_gnn_in['beta']}

def reference(x, src, dst, edge_attr_64, edge_attr_8, L0_gnn_Wq, L0_gnn_bq, L0_gnn_Wk, L0_gnn_bk, L0_gnn_Wv, L0_gnn_bv, L0_gnn_Wo, L0_gnn_bo, L0_gnn_ln1_g, L0_gnn_ln1_b, L0_gnn_ln2_g, L0_gnn_ln2_b, L0_gnn_W1, L0_gnn_b1, L0_gnn_W2, L0_gnn_b2, L1_gnn_W1, L1_gnn_a_src1, L1_gnn_a_dst1, L1_gnn_b1, L1_gnn_W2, L1_gnn_a_src2, L1_gnn_a_dst2, L1_gnn_b2, L1_gnn_Wfc, L1_gnn_bfc, L2_gnn_u, L2_gnn_W1, L2_gnn_b1, L2_gnn_W2, L2_gnn_b2, L3_gnn_W1, L3_gnn_b1, L3_gnn_W2, L3_gnn_b2, L3_gnn_W3, L3_gnn_b3, L3_gnn_W4, L3_gnn_b4, L3_gnn_gamma, L3_gnn_beta):
    import jax
    import jax.numpy as jnp

    def _L0_gnn_ref(x, att_bias, Wq, bq, Wk, bk, Wv, bv, Wo, bo, ln1_g, ln1_b, ln2_g, ln2_b, W1, b1, W2, b2, row_index, col_index):
        import jax, jax.numpy as jnp
        import numpy as np
        L, C, H, E = (512, 512, 8, 16384)
        D = C // H
        HID = 1024
        EPS = 1e-05

        def _ln(x, g, b):
            mu = jnp.mean(x, axis=-1, keepdims=True)
            var = jnp.var(x, axis=-1, keepdims=True)
            return (x - mu) * jax.lax.rsqrt(var + EPS) * g + b

        def _sparse_attention(z, row, col, bias, Wq, bq, Wk, bk, Wv, bv, Wo, bo):
            q = (z @ Wq + bq).reshape(L, H, D)
            k = (z @ Wk + bk).reshape(L, H, D)
            v = (z @ Wv + bv).reshape(L, H, D)
            scale = 1.0 / jnp.sqrt(jnp.asarray(D, z.dtype))
            scores = jnp.einsum('ehd,ehd->eh', q[row], k[col]) * scale + bias
            m = jax.ops.segment_max(scores, row, num_segments=L)
            p = jnp.exp(scores - m[row])
            ssum = jax.ops.segment_sum(p, row, num_segments=L)
            alpha = p / ssum[row]
            out = jax.ops.segment_sum(alpha[:, :, None] * v[col], row, num_segments=L)
            return out.reshape(L, C) @ Wo + bo
        z = _ln(x, ln1_g, ln1_b)
        att = _sparse_attention(z, row_index, col_index, att_bias, Wq, bq, Wk, bk, Wv, bv, Wo, bo)
        x = x + att
        z = _ln(x, ln2_g, ln2_b)
        ff = jax.nn.silu(z @ W1 + b1) @ W2 + b2
        return x + ff

    def _L1_gnn_ref(x, edge_index, W1, a_src1, a_dst1, b1, W2, a_src2, a_dst2, b2, Wfc, bfc):
        import jax, jax.numpy as jnp
        import numpy as np
        N = 10000
        E = 2500
        H = 4
        C = 256
        D_IN = 512
        D_OUT = 512
        NEG_SLOPE = 0.2

        def gat_conv(x, src, dst, W, a_src, a_dst, bias):
            n = x.shape[0]
            h = (x @ W).reshape(n, H, C)
            al_s = jnp.einsum('nhc,hc->nh', h, a_src)
            al_d = jnp.einsum('nhc,hc->nh', h, a_dst)
            e = jax.nn.leaky_relu(al_s[src] + al_d[dst], NEG_SLOPE)
            emax = jax.ops.segment_max(e, dst, num_segments=n)
            w = jnp.exp(e - emax[dst])
            denom = jax.ops.segment_sum(w, dst, num_segments=n)
            alpha = w / denom[dst]
            out = jax.ops.segment_sum(h[src] * alpha[:, :, None], dst, num_segments=n)
            return out.reshape(n, H * C) + bias
        loop = jnp.arange(N, dtype=edge_index.dtype)
        src = jnp.concatenate([edge_index[0], loop])
        dst = jnp.concatenate([edge_index[1], loop])
        h = jax.nn.relu(gat_conv(x, src, dst, W1, a_src1, a_dst1, b1))
        h = jax.nn.relu(gat_conv(h, src, dst, W2, a_src2, a_dst2, b2))
        return h @ Wfc + bfc

    def _L2_gnn_ref(x, edge_index, edge_attr, u, batch, W1, b1, W2, b2):
        import jax, jax.numpy as jnp
        import numpy as np
        N_NODES = 50000
        N_EDGES = 12500
        NODE_IN = 512
        EDGE_IN = 64
        HID = 1024
        col = edge_index[1]
        summed = jax.ops.segment_sum(edge_attr, col, num_segments=x.shape[0])
        count = jax.ops.segment_sum(jnp.ones((edge_attr.shape[0],), dtype=x.dtype), col, num_segments=x.shape[0])
        agg = summed / jnp.maximum(count, 1.0)[:, None]
        h = jnp.concatenate([x, agg], axis=-1)
        h = jax.nn.relu(h @ W1 + b1)
        return x + h @ W2 + b2

    def _L3_gnn_ref(x, edge_index, edge_attr, W1, b1, W2, b2, W3, b3, W4, b4, gamma, beta):
        import jax, jax.numpy as jnp
        import numpy as np
        N_NODES = 20000
        N_EDGES = 5000
        HIDDEN = 512
        EDGE_DIM = 64
        LN_EPS = 1e-05

        def mish(x):
            return x * jnp.tanh(jax.nn.softplus(x))
        src, dst = (edge_index[0], edge_index[1])
        edge_feat = jnp.concatenate([x[src], x[dst], edge_attr], axis=-1)
        h = mish(edge_feat @ W1 + b1)
        messages = mish(h @ W2 + b2)
        agg = jax.ops.segment_sum(messages, dst, num_segments=x.shape[0])
        u = mish(jnp.concatenate([x, agg], axis=-1) @ W3 + b3)
        out = u @ W4 + b4
        y = x + out
        mu = jnp.mean(y, axis=-1, keepdims=True)
        var = jnp.mean(jnp.square(y - mu), axis=-1, keepdims=True)
        return (y - mu) * jax.lax.rsqrt(var + LN_EPS) * gamma + beta
    edge_index = jnp.stack([src, dst])
    batch0 = jnp.zeros((512,), jnp.int32)
    x = _layernorm(x + _L0_gnn_ref(x, edge_attr_8, L0_gnn_Wq, L0_gnn_bq, L0_gnn_Wk, L0_gnn_bk, L0_gnn_Wv, L0_gnn_bv, L0_gnn_Wo, L0_gnn_bo, L0_gnn_ln1_g, L0_gnn_ln1_b, L0_gnn_ln2_g, L0_gnn_ln2_b, L0_gnn_W1, L0_gnn_b1, L0_gnn_W2, L0_gnn_b2, src, dst), axis=-1)
    x = _layernorm(x + _L1_gnn_ref(x, edge_index, L1_gnn_W1, L1_gnn_a_src1, L1_gnn_a_dst1, L1_gnn_b1, L1_gnn_W2, L1_gnn_a_src2, L1_gnn_a_dst2, L1_gnn_b2, L1_gnn_Wfc, L1_gnn_bfc), axis=-1)
    x = _layernorm(x + _L2_gnn_ref(x, edge_index, edge_attr_64, L2_gnn_u, batch0, L2_gnn_W1, L2_gnn_b1, L2_gnn_W2, L2_gnn_b2), axis=-1)
    x = _layernorm(x + _L3_gnn_ref(x, edge_index, edge_attr_64, L3_gnn_W1, L3_gnn_b1, L3_gnn_W2, L3_gnn_b2, L3_gnn_W3, L3_gnn_b3, L3_gnn_W4, L3_gnn_b4, L3_gnn_gamma, L3_gnn_beta), axis=-1)
    return x

_drawn_inputs = setup_inputs


def setup_inputs(seed=0):
    import zlib

    import numpy as np

    out = dict(_drawn_inputs(seed))
    spreads = {'L0_gnn_bq': (0.0, 0.8),
     'L0_gnn_bk': (0.0, 2.0),
     'L0_gnn_bv': (0.0, 0.1),
     'L0_gnn_bo': (0.0, 0.1),
     'L0_gnn_ln1_g': (1.0, 0.6),
     'L0_gnn_ln1_b': (0.0, 0.617),
     'L0_gnn_ln2_g': (1.0, 0.6),
     'L0_gnn_ln2_b': (0.0, 0.706),
     'L0_gnn_b1': (0.0, 0.32),
     'L0_gnn_b2': (0.0, 0.1),
     'L1_gnn_b1': (0.0, 0.1),
     'L1_gnn_b2': (0.0, 0.1),
     'L1_gnn_bfc': (0.0, 0.1),
     'L2_gnn_u': (0.0, 0.1),
     'L2_gnn_b1': (0.0, 0.1),
     'L2_gnn_b2': (0.0, 0.1),
     'L3_gnn_b1': (0.0, 0.1),
     'L3_gnn_b2': (0.0, 0.1),
     'L3_gnn_b3': (0.0, 0.491),
     'L3_gnn_b4': (0.0, 0.375),
     'L3_gnn_gamma': (1.0, 0.2),
     'L3_gnn_beta': (0.0, 0.1)}
    factors = {'L0_gnn_Wq': 8.0,
     'L0_gnn_Wk': 8.0,
     'L1_gnn_a_dst1': 3.254,
     'L1_gnn_a_src2': 3.26,
     'L1_gnn_a_dst2': 8.0,
     'edge_attr_8': 3.172}
    for name, (base, spread) in spreads.items():
        noise = np.random.default_rng([zlib.crc32(name.encode()), seed]).standard_normal(out[name].shape)
        drawn = base * np.exp(spread * noise) if base else spread * noise
        out[name] = jnp.asarray(drawn.astype(out[name].dtype))
    for name, factor in factors.items():
        out[name] = (out[name] * factor).astype(out[name].dtype)
    return out
```

```python
from contextlib import ExitStack

import concourse.bass as bass
from concourse import mybir

F32 = mybir.dt.float32
F32R = mybir.dt.float32r
BF16 = mybir.dt.bfloat16
FP16 = mybir.dt.float16
I32 = mybir.dt.int32
ALU = mybir.AluOpType
ACT = mybir.ActivationFunctionType
AX = mybir.AxisListType
Offset = bass.IndirectOffsetOnAxis

P = 128
N = 512
C = 512
E = 8192
NT = N // P
CT = C // P
ET = E // P
H0, D0 = 8, 64
HID = 1024
HT = HID // P
H1, C1 = 4, 256
EA = 64
EPS = 1e-5
LN2 = 0.6931471805599453
BIG = 3.0e38
HALF_PI = 1.5707963267948966
GUARD_T = (64.0, 8.0)


class Ctx:

    def __init__(self, nc, io, stack):
        self.nc, self.io, self.stack = nc, io, stack
        self.phase_sems = []

    def sb(self, name, shape, dt=F32, stack=None):
        return (stack or self.stack).enter_context(self.nc.sbuf_tensor(name, shape, dt))

    def sem(self, name):
        s = self.nc.alloc_semaphore(name=name)
        self.phase_sems.append(s)
        return s

    def end_phase(self):
        self.nc.clear_and_free_semaphores(self.phase_sems)
        self.nc.all_engine_barrier()
        self.phase_sems = []


def row_b(vec):
    return vec.partition_broadcast(P)


def col(vec, tiles):
    return vec.rearrange("(k p) -> p k", p=P)


def rows(mat):
    return mat.rearrange("(k p) n -> p k n", p=P)


class Norm:

    def __init__(self, cx, tag, stack):
        self.stats = cx.sb(f"{tag}_stats", [P, NT, 6], F32, stack)
        self.mv = cx.sb(f"{tag}_mv", [P, NT, 2], F32, stack)
        self.var = cx.sb(f"{tag}_var", [P, NT], F32, stack)
        self.std = cx.sb(f"{tag}_std", [P, NT], F32, stack)
        self.rstd = cx.sb(f"{tag}_rstd", [P, NT], F32, stack)
        self.s_stats = cx.sem(f"{tag}_s_stats")
        self.s_aggr = cx.sem(f"{tag}_s_aggr")
        self.s_var = cx.sem(f"{tag}_s_var")
        self.s_std = cx.sem(f"{tag}_s_std")
        self.s_rstd = cx.sem(f"{tag}_s_rstd")
        self.s_out = cx.sem(f"{tag}_s_out")


def norm_vector(e, n, x, out, s_x):
    for i in range(NT):
        e.wait_ge(s_x, i + 1)
        e.bn_stats(n.stats[:, i, :], x[:, i, :]).then_inc(n.s_stats, 1)
    for i in range(NT):
        e.wait_ge(n.s_stats, i + 1)
        e.bn_aggr(n.mv[:, i, :], n.stats[:, i, :]).then_inc(n.s_aggr, 1)
    e.wait_ge(n.s_aggr, NT)
    e.tensor_scalar(n.var[:], n.mv[:, :, 1], EPS, None, ALU.add).then_inc(n.s_var, 1)
    e.wait_ge(n.s_std, 1)
    e.reciprocal(n.rstd[:], n.std[:]).then_inc(n.s_rstd, 1)
    e.wait_ge(n.s_rstd, 1)
    for i in range(NT):
        e.tensor_scalar(out[:, i, :], x[:, i, :], n.mv[:, i, 0:1], n.rstd[:, i:i + 1],
                        ALU.subtract, ALU.mult).then_inc(n.s_out, 1)


def norm_scalar(e, n):
    e.wait_ge(n.s_var, 1)
    e.activation(n.std[:], n.var[:], ACT.Sqrt).then_inc(n.s_std, 1)


def transposes(pe, cx, x, tiles, s_x, s_done, bank0=0, s_free=None):
    for c in range(tiles):
        for n in range(NT):
            if c == 0 and s_x is not None:
                pe.wait_ge(s_x, n + 1)
            t = pe.transpose(cx.ps[:, bank0 + c, n * P:(n + 1) * P], x[:, n, c * P:(c + 1) * P], cx.ident[:])
        t.then_inc(s_done, 1)


def product(pe, out, pairs):
    for k, (lhsT, rhs) in enumerate(pairs):
        m = pe.matmul(out, lhsT, rhs, start=(k == 0), stop=(k == len(pairs) - 1))
    return m


def setup(cx, st):
    nc, io = cx.nc, cx.io
    tmp = ExitStack()
    iota_i = cx.sb("iota_i", [P, N], I32, tmp)
    part_i = cx.sb("part_i", [P, NT], I32, tmp)
    part_f = cx.sb("part_f", [P, NT], F32, tmp)
    src_row = cx.sb("src_row", [P, E], I32, tmp)
    src_row_h = cx.sb("src_row_h", [P, E], FP16, tmp)
    s_in, s_const, s_f, s_row = cx.sem("s_in"), cx.sem("s_const"), cx.sem("s_f"), cx.sem("s_row")
    s_zero = cx.sem("s_zero")
    block = tmp.enter_context(nc.Block())

    @block.sync
    def _(sp):
        sp.dma_start(src_row[:], row_b(io["src"])).then_inc(s_row, 16)
        sp.dma_start(cx.x[:], rows(io["x"])).then_inc(s_in, 16)
        sp.dma_start(cx.src_i[:], io["src"].rearrange("(p t) -> p t", p=P)).then_inc(s_in, 16)
        sp.dma_start(cx.dst_i[:], io["dst"].rearrange("(p t) -> p t", p=P)).then_inc(s_in, 16)

    @block.scalar
    def _(act):
        for w, (buf, name) in enumerate(st["weights0"]):
            act.dma_start(buf, rows(io[name])).then_inc(st["s_w0"], 16)

    @block.gpsimd
    def _(pool):
        pool.memset(cx.ident[:], 0.0).then_inc(s_zero, 1)
        pool.iota(iota_i[:], pattern=[[1, N]], base=0, channel_multiplier=0).then_inc(s_const, 1)
        pool.iota(part_i[:], pattern=[[P, NT]], base=0, channel_multiplier=1).then_inc(s_const, 1)
        pool.memset(cx.half_pi[:], HALF_PI)
        pool.wait_ge(s_zero, 1)
        pool.affine_select(out=cx.ident[:], in_=cx.ident[:], compare_op=ALU.not_equal, fill=1.0, base=0,
                           pattern=[[-1, P]], channel_multiplier=1)

    @block.vector
    def _(dve):
        dve.memset(cx.zero_r[:].bitcast(F32), 0.0)
        dve.wait_ge(s_const, 2)
        dve.tensor_copy(cx.iota_h[:], iota_i[:])
        dve.tensor_copy(part_f[:], part_i[:]).then_inc(s_f, 1)
        dve.wait_ge(s_in, 48)
        dve.tensor_copy(cx.src_f[:], cx.src_i[:]).then_inc(s_f, 1)
        dve.tensor_copy(cx.dst_f[:], cx.dst_i[:]).then_inc(s_f, 1)
        dve.wait_ge(s_f, 3)
        dve.scalar_tensor_tensor(out=st["pair_i"][:], in0=cx.src_f[:], scalar=float(N), in1=cx.dst_f[:],
                                 op0=ALU.mult, op1=ALU.add)
        dve.wait_ge(s_row, 16)
        dve.tensor_copy(src_row_h[:].rearrange("q (t p) -> q p t", p=P),
                        src_row[:].rearrange("q (p t) -> q p t", t=ET)).then_inc(s_f, 1)
        dve.wait_ge(s_f, 4)
        for n in range(NT):
            dve.tensor_scalar(st["ohT"][:, n, :], src_row_h[:], part_f[:, n:n + 1], None, ALU.is_equal)

    tmp.close()
    cx.end_phase()


def attention_scores(cx, st):
    nc, io = cx.nc, cx.io
    tmp = ExitStack()
    z = cx.sb("z0", [P, NT, C], F32, tmp)
    qT = cx.sb("qT", [P, CT, N], F32, tmp)
    kT = cx.sb("kT", [P, CT, N], F32, tmp)
    v = cx.sb("v", [P, NT, C], F32, tmp)
    stage = cx.wB[:].rearrange("p (a n h) -> p a n h", a=2, h=H0)
    bv = cx.sb("bv_b", [P, C], F32, tmp)
    cols = cx.sb("cols0", [P, 4, CT], F32, tmp)
    norm = Norm(cx, "n0", tmp)
    s_small = cx.sem("s0_small")
    s_x, s_tr, s_zT, s_v, s_vout = (cx.sem("s0_" + n) for n in ("x", "tr", "zT", "v", "vout"))
    s_vmm, s_qk, s_qk_out, s_smm = (cx.sem("s0_" + n) for n in ("vmm", "qk", "qk_out", "smm"))
    s_ev = [cx.sem("s0_ev_act"), cx.sem("s0_ev_dve")]
    s_st = [cx.sem("s0_st0"), cx.sem("s0_st1")]
    Wq, Wk, Wv = (cx.wA[:, i] for i in range(3))
    v_dram = st["v_dram"].rearrange("(n p) c -> p n c", p=P)
    s_dram = st["s_dram"].rearrange("(n p c) h -> p n c h", n=NT, p=P)
    ps = cx.ps
    block = tmp.enter_context(nc.Block())

    @block.sync
    def _(sp):
        for i, name in enumerate(("L0_gnn_ln1_g", "L0_gnn_ln1_b", "L0_gnn_bq", "L0_gnn_bk")):
            sp.dma_start(cols[:, i, :], col(io[name], CT), allow_slow_non_contiguous=True).then_inc(s_small, 16)
        sp.dma_start(bv[:], row_b(io["L0_gnn_bv"])).then_inc(s_small, 16)
        sp.wait_ge(s_v, NT)
        sp.dma_start(v_dram, v[:]).then_inc(s_vout, 16)
        for n in range(NT):
            sp.wait_ge(s_ev[0], (n + 1) * H0 // 2)
            sp.wait_ge(s_ev[1], (n + 1) * H0 // 2)
            sp.dma_start(s_dram[:, n], stage[:, n % 2]).then_inc(s_st[n % 2], 16)
        for s in s_st:
            sp.wait_ge(s, 16 * NT // 2)
        sp.wait_ge(s_vout, 16)

    @block.vector
    def _(dve):
        dve.sem_inc(s_x, NT)
        norm_vector(dve, norm, cx.x, z, s_x)
        dve.wait_ge(s_small, 80)
        for c in range(1, CT, 2):
            dve.wait_ge(s_tr, c + 1)
            dve.tensor_scalar(cx.xT[:, c, :], ps[:, c, :], cols[:, 0, c:c + 1], cols[:, 1, c:c + 1],
                              ALU.mult, ALU.add).then_inc(s_zT, 1)
        for n in range(NT):
            dve.wait_ge(s_vmm, n + 1)
            dve.tensor_tensor(v[:, n, :], ps[:, 4 + n, :], bv[:], ALU.add).then_inc(s_v, 1)
        for i in range(1, 2 * CT, 2):
            c, out = i % CT, (qT, kT)[i // CT]
            dve.wait_ge(s_qk, i + 1)
            dve.tensor_scalar(out[:, c, :], ps[:, i, :], cols[:, 2 + i // CT, c:c + 1], None,
                              ALU.add).then_inc(s_qk_out, 1)
        for u in range(1, NT * H0, 2):
            n, h = u // H0, u % H0
            dve.wait_ge(s_smm, u + 1)
            if n >= 2 and h == 1:
                dve.wait_ge(s_st[n % 2], 16)
            dve.tensor_scalar(stage[:, n % 2, :, h], ps[:, u % 8, :], 0.125, None, ALU.mult).then_inc(s_ev[1], 1)

    @block.scalar
    def _(act):
        norm_scalar(act, norm)
        act.wait_ge(s_small, 80)
        for c in range(0, CT, 2):
            act.wait_ge(s_tr, c + 1)
            act.activation(cx.xT[:, c, :], ps[:, c, :], ACT.Identity, bias=cols[:, 1, c:c + 1],
                           scale=cols[:, 0, c:c + 1]).then_inc(s_zT, 1)
        for i in range(0, 2 * CT, 2):
            c, out = i % CT, (qT, kT)[i // CT]
            act.wait_ge(s_qk, i + 1)
            act.activation(out[:, c, :], ps[:, i, :], ACT.Identity,
                           bias=cols[:, 2 + i // CT, c:c + 1]).then_inc(s_qk_out, 1)
        for u in range(0, NT * H0, 2):
            n, h = u // H0, u % H0
            act.wait_ge(s_smm, u + 1)
            if n >= 2 and h == 0:
                act.wait_ge(s_st[n % 2], 16)
            act.activation(stage[:, n % 2, :, h], ps[:, u % 8, :], ACT.Copy, scale=0.125).then_inc(s_ev[0], 1)

    @block.tensor
    def _(pe):
        transposes(pe, cx, z, CT, norm.s_out, s_tr)
        pe.wait_ge(s_zT, CT)
        pe.wait_ge(st["s_w0"], 16 * 4)
        for n in range(NT):
            product(pe, ps[:, 4 + n, :], [(cx.xT[:, k, n * P:(n + 1) * P], Wv[:, k, :]) for k in range(CT)]
                    ).then_inc(s_vmm, 1)
        for i in range(2 * CT):
            c, w = i % CT, (Wq, Wk)[i // CT]
            if i >= CT:
                pe.wait_ge(s_v, i - CT + 1)
            product(pe, ps[:, i, :], [(w[:, k, c * P:(c + 1) * P], cx.xT[:, k, :]) for k in range(CT)]
                    ).then_inc(s_qk, 1)
        pe.wait_ge(s_qk_out, 2 * CT)
        for u in range(NT * H0):
            n, h = u // H0, u % H0
            lo = D0 * (h % 2)
            if u >= 8:
                pe.wait_ge(s_ev[u % 2], (u - 8) // 2 + 1)
            pe.matmul(ps[:, u % 8, :], qT[lo:lo + D0, h // 2, n * P:(n + 1) * P], kT[lo:lo + D0, h // 2, :],
                      start=True, stop=True).then_inc(s_smm, 1)

    tmp.close()
    cx.end_phase()


def attention_edges(cx, st):
    nc, io = cx.nc, cx.io
    tmp = ExitStack()
    R, G = 4, 8
    bias = cx.sb("bias", [P, ET, H0], F32, tmp)
    sg = cx.sb("sg", [P, ET, H0], F32, tmp)
    s = cx.sb("s", [P, ET, H0], F32, tmp)
    diff = cx.sb("diff", [P, 2, ET, H0], F32, tmp)
    w = cx.sb("w", [P, ET, H0], BF16, tmp)
    p = cx.sb("p", [P, ET, H0], F32, tmp)
    p_hl = cx.sb("p_hl", [P, ET, 2, H0], F32R, tmp)
    pmax = cx.sb("pmax", [P, H0], F32, tmp)
    gcol = cx.sb("gcol", [H0, 1], F32, tmp)
    base = cx.sb("base", [P, 3, NT, H0], F32, tmp)
    total = cx.sb("total", [P, NT, H0], F32, tmp)
    expo = cx.sb("expo", [P, NT, H0], I32, tmp)
    step = cx.sb("step", [P, NT, H0], F32, tmp)
    bound = cx.sb("bound", [P, NT, H0], F32, tmp)
    bound_hl = cx.sb("bound_hl", [P, NT, 2, H0], BF16, tmp)
    oh = cx.sb("oh", [P, R, N], BF16, tmp)
    oh_r = cx.sb("oh_r", [P, R, N], F32R, tmp)
    vg = cx.wA[:, 0:2].rearrange("p a k c -> p (a k) c")
    pv = cx.sb("pv", [P, R, C], F32, tmp)
    pv_hi = cx.sb("pv_hi", [P, R, C], F32R, tmp)
    pv_lo = cx.sb("pv_lo", [P, R, C], F32R, tmp)
    names = ("bias", "sg", "s", "pmax", "gT", "gcol", "gb", "base", "diff", "w", "oh", "oh_free", "sum",
             "total", "expo", "step", "bound", "hi", "lo", "back", "p", "p_hl",
             "ohr", "pv", "pvhi", "pvlo", "used")
    sem = {n: cx.sem("s1_" + n) for n in names}
    s_vg = [cx.sem(f"s1_vg{i}") for i in range(G)]
    ps = cx.ps
    g_psum = ps[0:H0, 0, 0:P]
    gb_psum = ps[:, 0, P:P + H0]
    sum_psum = ps[:, 1, 0:NT * H0].rearrange("p (n h) -> p n h", n=NT)
    back_psum = ps[:, 2:4, :].rearrange("p b c -> p (b c)")
    back = back_psum.rearrange("p (t k h) -> p t k h", t=ET, k=2)
    block = tmp.enter_context(nc.Block())

    @block.sync
    def _(sp):
        sp.dma_start(bias[:], io["edge_attr_8"].rearrange("(p t) h -> p t h", p=P)).then_inc(sem["bias"], 16)
        sp.dma_start(cx.wB[:, 0:CT * HID].rearrange("p (k n) -> p k n", k=CT), rows(io["L0_gnn_W1"])
                     ).then_inc(st["s_w1"], 16)
        sp.dma_start(cx.wB[:, CT * HID:].rearrange("p (k n) -> p k n", k=HT), rows(io["L0_gnn_W2"])
                     ).then_inc(st["s_w1"], 16)

    @block.gpsimd
    def _(pool):
        for t in range(ET):
            pool.indirect_dma_start(sg[:, t, :], None, st["s_dram"], Offset(ap=st["pair_i"][:, t:t + 1], axis=0)
                                    ).then_inc(sem["sg"], 16)
        for t in range(ET):
            if t >= G:
                pool.wait_ge(sem["pv"], t - G + 1)
            pool.indirect_dma_start(vg[:, t % G, :], None, st["v_dram"], Offset(ap=cx.dst_i[:, t:t + 1], axis=0)
                                    ).then_inc(s_vg[t % G], 16)

    @block.vector
    def _(dve):
        dve.wait_ge(sem["bias"], 16)
        dve.wait_ge(sem["sg"], 16 * ET)
        dve.tensor_tensor(s[:], sg[:], bias[:], ALU.add).then_inc(sem["s"], 1)
        dve.wait_ge(sem["s"], 1)
        dve.tensor_reduce(pmax[:], s[:].rearrange("p t h -> p h t"), AX.X, ALU.max).then_inc(sem["pmax"], 1)
        dve.wait_ge(sem["gT"], 1)
        dve.tensor_reduce(gcol[:], g_psum, AX.X, ALU.max).then_inc(sem["gcol"], 1)
        dve.wait_ge(sem["gb"], 1)
        for n in range(NT):
            dve.tensor_copy(base[:, 0, n, :], gb_psum).then_inc(sem["base"], 1)
        dve.wait_ge(sem["base"], NT)
        dve.sem_inc(sem["oh_free"], R)
        for g, T in enumerate(GUARD_T):
            if g == 0:
                dve.tensor_tensor(diff[:, 0], s[:], base[:, 0, 0:1, :].to_broadcast([P, ET, H0]), ALU.subtract
                                  ).then_inc(sem["diff"], 1)
            else:
                dve.wait_ge(sem["back"], g)
                dve.tensor_tensor(diff[:, 1], s[:], back[:, :, 0, :], ALU.subtract).then_inc(sem["p_hl"], 1)
                dve.wait_ge(sem["p_hl"], g)
                dve.wait_ge(sem["w"], g)
                dve.tensor_tensor(diff[:, 0], diff[:, 1], back[:, :, 1, :], ALU.subtract).then_inc(sem["diff"], 1)
            with dve.Fori(0, ET // R) as i:
                for u in range(R):
                    dve.wait_ge(sem["oh_free"], i * R + (g * ET + u + 1))
                    dve.tensor_scalar(oh[:, u, :], cx.iota_h[:], cx.src_f[:, bass.ds(i * R + u, 1)], None,
                                      ALU.is_equal).then_inc(sem["oh"], 1)
            dve.wait_ge(sem["sum"], g + 1)
            dve.tensor_copy(total[:], sum_psum).then_inc(sem["total"], 1)
            dve.wait_ge(sem["total"], g + 1)
            dve.tensor_scalar(expo[:], total[:].bitcast(I32), 23, None, ALU.logical_shift_right
                              ).then_inc(sem["expo"], 1)
            dve.wait_ge(sem["expo"], g + 1)
            dve.tensor_scalar(step[:], expo[:], -126.0, T * LN2, ALU.add, ALU.mult).then_inc(sem["step"], 1)
            dve.wait_ge(sem["step"], g + 1)
            dve.tensor_tensor(bound[:], step[:], base[:, g], ALU.add).then_inc(sem["bound"], 1)
            dve.wait_ge(sem["bound"], g + 1)
            dve.tensor_copy(bound_hl[:, :, 0, :], bound[:]).then_inc(sem["hi"], 1)
            dve.wait_ge(sem["hi"], g + 1)
            dve.tensor_tensor(bound_hl[:, :, 1, :], bound[:], bound_hl[:, :, 0, :], ALU.subtract
                              ).then_inc(sem["lo"], 1)
            dve.wait_ge(sem["lo"], g + 1)
            dve.tensor_tensor(base[:, g + 1], bound_hl[:, :, 0, :], bound_hl[:, :, 1, :], ALU.add
                              ).then_inc(sem["base"], 1)
            dve.wait_ge(sem["base"], NT + g + 1)
        g = len(GUARD_T)
        dve.wait_ge(sem["back"], g)
        dve.tensor_tensor(diff[:, 1], s[:], back[:, :, 0, :], ALU.subtract).then_inc(sem["p_hl"], 1)
        dve.wait_ge(sem["p_hl"], g)
        dve.wait_ge(sem["w"], g)
        dve.tensor_tensor(diff[:, 0], diff[:, 1], back[:, :, 1, :], ALU.subtract).then_inc(sem["diff"], 1)
        dve.wait_ge(sem["p"], 1)
        dve.tensor_copy(p_hl[:, :, 0, :], p[:]).then_inc(sem["p_hl"], 1)
        dve.wait_ge(sem["p_hl"], g + 1)
        dve.tensor_tensor(p_hl[:, :, 1, :], p[:], p_hl[:, :, 0, :].bitcast(F32), ALU.subtract
                          ).then_inc(sem["p_hl"], 1)

        def rest(i, u):
            dve.wait_ge(sem["pvhi"], i * G + (u + 1))
            dve.tensor_tensor(pv_lo[:, u % R, :], pv[:, u % R, :], pv_hi[:, u % R, :].bitcast(F32),
                              ALU.subtract).then_inc(sem["pvlo"], 1)

        dve.sem_inc(sem["used"], R)
        with dve.Fori(0, ET // G) as i:
            for u in range(G):
                dve.wait_ge(sem["used"], i * G + (u + 1))
                dve.tensor_scalar(oh_r[:, u % R, :], cx.iota_h[:], cx.src_f[:, bass.ds(i * G + u, 1)], None,
                                  ALU.is_equal).then_inc(sem["ohr"], 1)
                dve.wait_ge(s_vg[u], i * 16 + 16)
                dve.tensor_tensor(pv[:, u % R, :].rearrange("p (h d) -> p h d", h=H0),
                                  vg[:, u, :].rearrange("p (h d) -> p h d", h=H0),
                                  p[:, bass.ds(i * G + u, 1), :].rearrange("p o h -> p h o").to_broadcast([P, H0, D0]),
                                  ALU.mult).then_inc(sem["pv"], 1)
                if u:
                    rest(i, u - 1)
            rest(i, G - 1)

    @block.scalar
    def _(act):
        for g, T in enumerate(GUARD_T):
            act.wait_ge(sem["diff"], g + 1)
            if g:
                act.wait_ge(sem["sum"], g)
            act.activation(w[:], diff[:, 0], ACT.Exp, scale=1.0 / T).then_inc(sem["w"], 1)
        act.wait_ge(sem["diff"], len(GUARD_T) + 1)
        act.activation(p[:], diff[:, 0], ACT.Exp).then_inc(sem["p"], 1)
        with act.Fori(0, ET // R) as i:
            for u in range(R):
                act.wait_ge(sem["pv"], i * R + (u + 1))
                act.activation(pv_hi[:, u, :], pv[:, u, :], ACT.Copy).then_inc(sem["pvhi"], 1)

    @block.tensor
    def _(pe):
        pe.wait_ge(sem["pmax"], 1)
        pe.transpose(g_psum, pmax[:], cx.ident[:]).then_inc(sem["gT"], 1)
        pe.wait_ge(sem["gcol"], 1)
        pe.matmul(gb_psum, gcol[:].to_broadcast([H0, P]), cx.ident[0:H0, 0:H0], start=True, stop=True
                  ).then_inc(sem["gb"], 1)
        for g in range(len(GUARD_T)):
            if g:
                pe.wait_ge(sem["total"], g)
            pe.matmul(ps[:, 1, :], cx.zero_r[:, 0:P], cx.zero_r[:], start=True, stop=False)
            pe.wait_ge(sem["w"], g + 1)
            with pe.Fori(0, ET // R) as i:
                for u in range(R):
                    pe.wait_ge(sem["oh"], i * R + (g * ET + u + 1))
                    for n in range(NT):
                        m = pe.matmul(sum_psum[:, n, :], oh[:, u, n * P:(n + 1) * P],
                                      w[:, bass.ds(i * R + u, 1), :].rearrange("p o h -> p (o h)"),
                                      start=False, stop=False)
                    m.then_inc(sem["oh_free"], 1)
            pe.matmul(ps[:, 1, :], cx.zero_r[:, 0:P], cx.zero_r[:], start=False, stop=True
                      ).then_inc(sem["sum"], 1)
            pe.wait_ge(sem["base"], NT + g + 1)
            with pe.Fori(0, ET // R) as i:
                for u in range(R):
                    for n in range(NT):
                        m = pe.matmul(back_psum[:, bass.ds(i * (R * 2 * H0) + u * 2 * H0, 2 * H0)],
                                      st["ohT"][:, n, bass.ds(i * (R * P) + u * P, P)],
                                      bound_hl[:, n].rearrange("p k h -> p (k h)"),
                                      start=(n == 0), stop=(n == NT - 1))
            pe.matmul(ps[:, 4, 0:2], cx.zero_r[:, 0:P], cx.zero_r[:, 0:2], start=True, stop=True
                      ).then_inc(sem["back"], 1)
        pe.wait_ge(sem["p_hl"], len(GUARD_T) + 2)
        banks = [0] + [4 + n for n in range(NT)]
        for b in banks:
            pe.matmul(ps[:, b, :], cx.zero_r[:, 0:P], cx.zero_r[:], start=True, stop=False)
        with pe.Fori(0, ET // R) as i:
            for u in range(R):
                pe.wait_ge(sem["ohr"], i * R + (u + 1))
                pe.wait_ge(sem["pvhi"], i * R + (u + 1))
                pe.wait_ge(sem["pvlo"], i * R + (u + 1))
                for n in range(NT):
                    one = oh_r[:, u, n * P:(n + 1) * P]
                    pe.matmul(ps[:, 0, n * 16:(n + 1) * 16], one,
                              p_hl[:, bass.ds(i * R + u, 1)].rearrange("p o k h -> p (o k h)"),
                              start=False, stop=False)
                    pe.matmul(ps[:, 4 + n, :], one, pv_hi[:, u, :], start=False, stop=False)
                    m = pe.matmul(ps[:, 4 + n, :], one, pv_lo[:, u, :], start=False, stop=False)
                m.then_inc(sem["used"], 1)
        for b in banks:
            pe.matmul(ps[:, b, :], cx.zero_r[:, 0:P], cx.zero_r[:], start=False, stop=True)

    tmp.close()
    cx.end_phase()


def attention_out(cx, st):
    nc, io = cx.nc, cx.io
    tmp = ExitStack()
    den2 = cx.sb("den2", [P, NT, 2, H0], F32, tmp)
    den = cx.sb("den", [P, NT, H0], F32, tmp)
    rden = cx.sb("rden", [P, NT, H0], F32, tmp)
    att = cx.sb("att", [P, NT, C], F32, tmp)
    attT = cx.sb("attT", [P, CT, N], F32, tmp)
    x1 = cx.sb("x1", [P, NT, C], F32, tmp)
    xb = cx.sb("xb", [P, NT, C], F32, tmp)
    z = cx.sb("z1", [P, NT, C], F32, tmp)
    zT = cx.sb("z1T", [P, CT, N], F32, tmp)
    hT = cx.sb("h0T", [P, HT, N], F32, tmp)
    bo = cx.sb("bo_b", [P, C], F32, tmp)
    b2 = cx.sb("b20_b", [P, C], F32, tmp)
    cols = cx.sb("cols1", [P, 2, CT], F32, tmp)
    b1 = cx.sb("b10", [P, HT], F32, tmp)
    n1, n2 = Norm(cx, "n1", tmp), Norm(cx, "n2", tmp)
    names = ("small", "den2", "den", "denm", "rden", "xb", "att", "tr", "attT", "wo", "x1", "tr2", "zT",
             "h", "hT", "ff", "xb2", "y")
    sem = {n: cx.sem("s2_" + n) for n in names}
    W1 = cx.wB[:, 0:CT * HID].rearrange("p (k n) -> p k n", k=CT)
    W2 = cx.wB[:, CT * HID:].rearrange("p (k n) -> p k n", k=HT)
    ps = cx.ps
    block = tmp.enter_context(nc.Block())

    @block.sync
    def _(sp):
        sp.dma_start(bo[:], row_b(io["L0_gnn_bo"])).then_inc(sem["small"], 16)
        sp.dma_start(b2[:], row_b(io["L0_gnn_b2"])).then_inc(sem["small"], 16)
        sp.dma_start(cols[:, 0, :], col(io["L0_gnn_ln2_g"], CT), allow_slow_non_contiguous=True).then_inc(sem["small"], 16)
        sp.dma_start(cols[:, 1, :], col(io["L0_gnn_ln2_b"], CT), allow_slow_non_contiguous=True).then_inc(sem["small"], 16)
        sp.dma_start(b1[:], col(io["L0_gnn_b1"], HT), allow_slow_non_contiguous=True).then_inc(sem["small"], 16)

    @block.vector
    def _(dve):
        dve.tensor_copy(den2[:].rearrange("p n k h -> p (n k h)"), ps[:, 0, 0:NT * 16]).then_inc(sem["den2"], 1)
        dve.wait_ge(sem["den2"], 1)
        dve.tensor_tensor(den[:], den2[:, :, 0, :], den2[:, :, 1, :], ALU.add).then_inc(sem["den"], 1)
        dve.wait_ge(sem["den"], 1)
        dve.tensor_scalar(rden[:], den[:], 1e-37, None, ALU.max).then_inc(sem["denm"], 1)
        dve.wait_ge(sem["denm"], 1)
        dve.reciprocal(den[:], rden[:]).then_inc(sem["rden"], 1)
        dve.wait_ge(sem["rden"], 1)
        for n in range(NT):
            dve.tensor_tensor(att[:, n, :].rearrange("p (h d) -> p h d", h=H0),
                              ps[:, 4 + n, :].rearrange("p (h d) -> p h d", h=H0),
                              den[:, n, :].unsqueeze(2).to_broadcast([P, H0, D0]), ALU.mult).then_inc(sem["att"], 1)
        dve.wait_ge(sem["small"], 80)
        for n in range(NT):
            dve.tensor_tensor(xb[:, n, :], cx.x[:, n, :], bo[:], ALU.add).then_inc(sem["xb"], 1)
        for c in range(1, CT, 2):
            dve.wait_ge(sem["tr"], c + 1)
            dve.tensor_copy(attT[:, c, :], ps[:, c, :]).then_inc(sem["attT"], 1)
        dve.wait_ge(sem["xb"], NT)
        for n in range(NT):
            dve.wait_ge(sem["wo"], n + 1)
            dve.tensor_tensor(x1[:, n, :], ps[:, 4 + n, :], xb[:, n, :], ALU.add).then_inc(sem["x1"], 1)
        norm_vector(dve, n1, x1, z, sem["x1"])
        for c in range(1, CT, 2):
            dve.wait_ge(sem["tr2"], c + 1)
            dve.tensor_scalar(zT[:, c, :], ps[:, c, :], cols[:, 0, c:c + 1], cols[:, 1, c:c + 1],
                              ALU.mult, ALU.add).then_inc(sem["zT"], 1)
        for n in range(NT):
            dve.scalar_tensor_tensor(out=xb[:, n, :], in0=cx.x[:, n, :], scalar=1.0, in1=x1[:, n, :],
                                     op0=ALU.mult, op1=ALU.add).then_inc(sem["xb2"], 1)
        dve.wait_ge(sem["xb2"], NT)
        for n in range(NT):
            dve.tensor_tensor(att[:, n, :], xb[:, n, :], b2[:], ALU.add).then_inc(sem["xb2"], 1)
        dve.wait_ge(sem["xb2"], 2 * NT)
        for n in range(NT):
            dve.wait_ge(sem["ff"], n + 1)
            dve.tensor_tensor(x1[:, n, :], ps[:, 4 + n, :], att[:, n, :], ALU.add).then_inc(sem["y"], 1)
        norm_vector(dve, n2, x1, cx.x, sem["y"])

    @block.scalar
    def _(act):
        for c in range(0, CT, 2):
            act.wait_ge(sem["tr"], c + 1)
            act.activation(attT[:, c, :], ps[:, c, :], ACT.Copy).then_inc(sem["attT"], 1)
        norm_scalar(act, n1)
        act.wait_ge(sem["small"], 80)
        for c in range(0, CT, 2):
            act.wait_ge(sem["tr2"], c + 1)
            act.activation(zT[:, c, :], ps[:, c, :], ACT.Identity, bias=cols[:, 1, c:c + 1],
                           scale=cols[:, 0, c:c + 1]).then_inc(sem["zT"], 1)
        for m in range(HT):
            act.wait_ge(sem["h"], m + 1)
            act.activation(hT[:, m, :], ps[:, (4 + m) % 8, :], ACT.Silu, bias=b1[:, m:m + 1]).then_inc(sem["hT"], 1)
        norm_scalar(act, n2)

    @block.tensor
    def _(pe):
        transposes(pe, cx, att, CT, sem["att"], sem["tr"])
        pe.wait_ge(sem["attT"], CT)
        for n in range(NT):
            product(pe, ps[:, 4 + n, :], [(attT[:, k, n * P:(n + 1) * P], cx.wA[:, 3, k, :]) for k in range(CT)]
                    ).then_inc(sem["wo"], 1)
        transposes(pe, cx, z, CT, n1.s_out, sem["tr2"])
        pe.wait_ge(sem["zT"], CT)
        pe.wait_ge(st["s_w1"], 32)
        for m in range(HT):
            product(pe, ps[:, (4 + m) % 8, :], [(W1[:, k, m * P:(m + 1) * P], zT[:, k, :]) for k in range(CT)]
                    ).then_inc(sem["h"], 1)
        pe.wait_ge(sem["hT"], HT)
        for n in range(NT):
            product(pe, ps[:, 4 + n, :], [(hT[:, k, n * P:(n + 1) * P], W2[:, k, :]) for k in range(HT)]
                    ).then_inc(sem["ff"], 1)

    tmp.close()
    cx.end_phase()


def edge_sums(cx, st):
    nc, io = cx.nc, cx.io
    tmp = ExitStack()
    R = 4
    ea = cx.sb("ea", [P, ET, EA], F32, tmp)
    ea_hl = cx.sb("ea_hl", [P, R, 2, EA], F32R, tmp)
    oh_s = cx.sb("oh_s", [P, R, N], BF16, tmp)
    oh_d = cx.sb("oh_d", [P, R, N], BF16, tmp)
    oh_r = cx.sb("oh_dr", [P, R, N], F32R, tmp)
    ident_b = cx.sb("ident_b", [P, P], BF16, tmp)
    ones = cx.sb("ones_b", [P, P], F32, tmp)
    count = cx.sb("count", [P, N], F32, tmp)
    names = ("ea", "const", "hi", "lo", "ohs", "ohd", "ohr", "used", "tr", "eaT", "mm", "cnt", "trc", "deg",
             "c1")
    sem = {n: cx.sem("s3_" + n) for n in names}
    ps = cx.ps
    block = tmp.enter_context(nc.Block())

    @block.sync
    def _(sp):
        sp.dma_start(ea[:], io["edge_attr_64"].rearrange("(p t) f -> p t f", p=P)).then_inc(sem["ea"], 16)
        sp.dma_start(cx.wA[:, 0:2].rearrange("p a k n -> p (a k n)").rearrange("p (k n) -> p k n", k=CT),
                     rows(io["L1_gnn_W1"])).then_inc(st["s_w2"], 16)
        sp.dma_start(cx.wA[:, 2:4].rearrange("p a k n -> p (a k) n"), rows(io["L1_gnn_Wfc"])
                     ).then_inc(st["s_w2"], 16)
        sp.dma_start(cx.wB[:].rearrange("p (k n) -> p k n", k=HT), rows(io["L1_gnn_W2"])).then_inc(st["s_w2"], 16)

    @block.vector
    def _(dve):
        dve.tensor_copy(ident_b[:], cx.ident[:]).then_inc(sem["const"], 1)
        dve.memset(ones[:], 1.0).then_inc(sem["const"], 1)
        dve.wait_ge(sem["ea"], 16)
        dve.sem_inc(sem["used"], R)
        with dve.Fori(0, ET // R) as i:
            for u in range(R):
                t = i * R + u
                dve.wait_ge(sem["used"], i * R + (u + 1))
                dve.tensor_copy(ea_hl[:, u, 0, :], ea[:, bass.ds(t, 1), :].rearrange("p o f -> p (o f)")
                                ).then_inc(sem["hi"], 1)
                dve.tensor_scalar(oh_s[:, u, :], cx.iota_h[:], cx.src_f[:, bass.ds(t, 1)], None,
                                  ALU.is_equal).then_inc(sem["ohs"], 1)
                dve.tensor_scalar(oh_d[:, u, :], cx.iota_h[:], cx.dst_f[:, bass.ds(t, 1)], None,
                                  ALU.is_equal).then_inc(sem["ohd"], 1)
                dve.tensor_scalar(oh_r[:, u, :], cx.iota_h[:], cx.dst_f[:, bass.ds(t, 1)], None,
                                  ALU.is_equal).then_inc(sem["ohr"], 1)
                dve.wait_ge(sem["hi"], i * R + (u + 1))
                dve.tensor_tensor(ea_hl[:, u, 1, :], ea[:, bass.ds(t, 1), :].rearrange("p o f -> p (o f)"),
                                  ea_hl[:, u, 0, :].bitcast(F32), ALU.subtract).then_inc(sem["lo"], 1)
        dve.wait_ge(sem["mm"], 1)
        for n in range(NT):
            dve.tensor_copy(cx.cnt[:, n, :], ps[:, n, :]).then_inc(sem["cnt"], 1)
        dve.wait_ge(sem["deg"], 1)
        dve.tensor_scalar(count[:], ps[:, 5, :], -1.0, 1.0, ALU.add, ALU.max).then_inc(sem["c1"], 1)
        dve.wait_ge(sem["c1"], 1)
        dve.reciprocal(cx.rcount[:], count[:]).then_inc(sem["c1"], 1)
        dve.wait_ge(sem["c1"], 2)
        dve.tensor_tensor(cx.ea_mean[:], ps[:, 4, :], cx.rcount[:], ALU.mult)
        for n in range(NT):
            dve.wait_ge(sem["trc"], n + 1)
            dve.tensor_scalar(cx.pen[:, n, :], ps[:, n, :], 0.0, -BIG, ALU.is_equal, ALU.mult)

    @block.scalar
    def _(act):
        with act.Fori(0, ET // R) as i:
            for u in range(R):
                act.wait_ge(sem["tr"], i * R + (u + 1))
                act.activation(cx.eaT[:, bass.ds(i * (R * P) + u * P, P)], ps[:, 5 + u % 2, 0:P], ACT.Copy
                               ).then_inc(sem["eaT"], 1)

    @block.tensor
    def _(pe):
        for b in range(NT + 1):
            pe.matmul(ps[:, b, :], cx.zero_r[:, 0:P], cx.zero_r[:], start=True, stop=False)
        pe.sem_inc(sem["eaT"], 2)
        with pe.Fori(0, ET // R) as i:
            for u in range(R):
                pe.wait_ge(sem["ohs"], i * R + (u + 1))
                pe.wait_ge(sem["ohd"], i * R + (u + 1))
                for n in range(NT):
                    pe.matmul(ps[:, n, :], oh_s[:, u, n * P:(n + 1) * P], oh_d[:, u, :], start=False, stop=False)
                pe.wait_ge(sem["ohr"], i * R + (u + 1))
                pe.wait_ge(sem["lo"], i * R + (u + 1))
                pe.matmul(ps[:, 4, :], ea_hl[:, u].rearrange("p k f -> p (k f)"), oh_r[:, u, :],
                          start=False, stop=False)
                pe.wait_ge(sem["eaT"], i * R + (u + 1))
                pe.transpose(ps[:, 5 + u % 2, 0:P], ea_hl[:, u].rearrange("p k f -> p (k f)").bitcast(F32),
                             cx.ident[:]).then_inc(sem["tr"], 1)
                pe.wait_ge(sem["tr"], i * R + (u + 1))
                pe.sem_inc(sem["used"], 1)
        pe.wait_ge(sem["const"], 2)
        for n in range(NT):
            pe.matmul(ps[:, n, n * P:(n + 1) * P], ident_b[:], ident_b[:], start=False, stop=False)
        for b in range(NT + 1):
            m = pe.matmul(ps[:, b, :], cx.zero_r[:, 0:P], cx.zero_r[:], start=False, stop=True)
        m.then_inc(sem["mm"], 1)
        pe.wait_ge(sem["cnt"], NT)
        pe.wait_ge(sem["eaT"], ET + 2)
        product(pe, ps[:, 5, :], [(ones[:], cx.cnt[:, k, :]) for k in range(NT)]).then_inc(sem["deg"], 1)
        transposes(pe, cx, cx.cnt, NT, None, sem["trc"])

    tmp.close()
    cx.end_phase()


W_ = C1 + 4


def gat_output(h_mem):
    return h_mem[:, 0:HT * N].rearrange("p (k n) -> p k n", k=HT)


def gat(cx, st, tag, W, kt, xT, h_mem, a_src, a_dst, b, s_w, w_count, x_in):
    nc, io = cx.nc, cx.io
    tmp = ExitStack()
    h = h_mem[:].rearrange("p (n q c) -> p n q c", n=NT, q=H1)
    outT = gat_output(h_mem)
    o = W.rearrange("p k n -> p (k n)")[:, 0:NT * HID].rearrange("p (n c) -> p n c", n=NT)
    b_b = cx.sb(tag + "b_b", [P, HID], F32, tmp)
    al = cx.sb(tag + "al", [P, NT, 2, H1], F32, tmp)
    als2 = cx.sb(tag + "als2", [P, NT, H1], F32, tmp)
    junk = cx.sb(tag + "junk", [P, N], F32, tmp)
    mx = cx.sb(tag + "mx", [P, NT, H1], F32, tmp)
    zmax = cx.sb(tag + "zmax", [P, NT, H1], F32, tmp)
    emax = cx.sb(tag + "emax", [P, NT, H1], F32, tmp)
    dd = cx.sb(tag + "dd", [P, 2, NT, H1], F32, tmp)
    ex = cx.sb(tag + "ex", [P, 2, 2, N], F32, tmp)
    pm = cx.sb(tag + "pm", [P, 2, N], F32, tmp)
    pr = cx.sb(tag + "pr", [P, 2, NT, N], F32, tmp)
    a_b = pr[:, 1].rearrange("p (a k) c -> p a (k c)", a=2)
    rd = cx.sb(tag + "rd", [P, NT * H1], F32, tmp)
    names = ("small", "ones", "tr", "xT", "mm", "h", "al", "als2", "asb", "mx", "z", "emax", "dd", "db",
             "ex1", "ex2", "pm", "p", "agg", "rd", "o", "tr2", "oT")
    sem = {n: cx.sem(tag + "_" + n) for n in names}
    ps = cx.ps
    block = tmp.enter_context(nc.Block())

    @block.sync
    def _(sp):
        sp.dma_start(a_b[:, 0, :], row_b(a_src.rearrange("h c -> (h c)"))).then_inc(sem["small"], 16)
        sp.dma_start(a_b[:, 1, :], row_b(a_dst.rearrange("h c -> (h c)"))).then_inc(sem["small"], 16)
        sp.dma_start(b_b[:], row_b(b)).then_inc(sem["small"], 16)

    @block.vector
    def _(dve):
        dve.memset(h[:, :, :, C1:W_], 1.0).then_inc(sem["ones"], 1)
        if x_in is not None:
            for c in range(kt):
                dve.wait_ge(sem["tr"], c + 1)
                dve.tensor_copy(xT[:, c, :], ps[:, c, :]).then_inc(sem["xT"], 1)
        dve.wait_ge(sem["small"], 48)
        for n in range(NT):
            for q in range(H1):
                if q % 2 == 0:
                    dve.wait_ge(sem["h"], n * 2 + q // 2 + 1)
                for k in range(2):
                    if n + q + k:
                        dve.wait_ge(sem["al"], (n * H1 + q) * 2 + k)
                    dve.tensor_tensor_reduce(out=junk[:, 0:C1], in0=h[:, n, q, 0:C1],
                                             in1=a_b[:, k, q * C1:(q + 1) * C1], scale=1.0, scalar=0.0,
                                             op0=ALU.mult, op1=ALU.add, accum_out=al[:, n, k, q:q + 1]
                                             ).then_inc(sem["al"], 1)
        dve.wait_ge(sem["al"], 2 * NT * H1)
        dve.tensor_scalar(als2[:], al[:, :, 0, :], 0.2, None, ALU.mult).then_inc(sem["als2"], 1)
        for n in range(NT):
            for q in range(H1):
                i = n * H1 + q
                dve.wait_ge(sem["asb"], q + 1)
                if i:
                    dve.wait_ge(sem["mx"], i)
                dve.tensor_tensor_reduce(out=junk[:], in0=cx.pen[:, n, :], in1=ps[:, q, :], scale=1.0,
                                         scalar=-BIG, op0=ALU.add, op1=ALU.max,
                                         accum_out=mx[:, n, q:q + 1]).then_inc(sem["mx"], 1)
        dve.wait_ge(sem["mx"], NT * H1)
        dve.tensor_tensor(zmax[:], mx[:], al[:, :, 1, :], ALU.add).then_inc(sem["z"], 1)
        dve.wait_ge(sem["z"], 1)
        dve.scalar_tensor_tensor(out=emax[:], in0=zmax[:], scalar=0.2, in1=zmax[:], op0=ALU.mult, op1=ALU.max
                                 ).then_inc(sem["emax"], 1)
        dve.wait_ge(sem["emax"], 1)
        dve.tensor_tensor(dd[:, 0], al[:, :, 1, :], emax[:], ALU.subtract).then_inc(sem["dd"], 1)
        dve.scalar_tensor_tensor(out=dd[:, 1], in0=al[:, :, 1, :], scalar=0.2, in1=emax[:], op0=ALU.mult,
                                 op1=ALU.subtract).then_inc(sem["dd"], 1)

        def numerators(q, s):
            i = q * NT + s
            dve.wait_ge(sem["ex2"], i + 1)
            if i >= 2:
                dve.wait_ge(sem["p"], i - 1)
            dve.scalar_tensor_tensor(out=pm[:, i % 2, :], in0=ex[:, i % 2, 0, :], scalar=1.0,
                                     in1=ex[:, i % 2, 1, :], op0=ALU.min, op1=ALU.max).then_inc(sem["pm"], 1)
            if q >= 2 and s == 0:
                dve.wait_ge(sem["agg"], NT * (q - 1))
            dve.wait_ge(sem["pm"], i + 1)
            dve.scalar_tensor_tensor(out=pr[:, q % 2, s, :], in0=pm[:, i % 2, :], scalar=1.0,
                                     in1=cx.cnt[:, s, :], op0=ALU.min, op1=ALU.mult).then_inc(sem["p"], 1)

        def outputs(q, n):
            i = q * NT + n
            dve.wait_ge(sem["agg"], i + 1)
            dve.reciprocal(rd[:, i:i + 1], ps[:, n, C1:C1 + 1]).then_inc(sem["rd"], 1)
            dve.wait_ge(sem["rd"], i + 1)
            dve.scalar_tensor_tensor(out=o[:, n, q * C1:(q + 1) * C1], in0=ps[:, n, 0:C1],
                                     scalar=rd[:, i:i + 1], in1=b_b[:, q * C1:(q + 1) * C1], op0=ALU.mult,
                                     op1=ALU.add).then_inc(sem["o"], 1)

        for q in range(H1):
            for s in range(NT):
                numerators(q, s)
            if q:
                for n in range(NT):
                    outputs(q - 1, n)
        for n in range(NT):
            outputs(H1 - 1, n)
        for c in range(1, HT, 2):
            dve.wait_ge(sem["tr2"], c + 1)
            dve.tensor_scalar(outT[:, c, :], ps[:, c, :], 0.0, None, ALU.max).then_inc(sem["oT"], 1)

    @block.scalar
    def _(act):
        for i in range(NT * 2):
            n, half = i // 2, i % 2
            act.wait_ge(sem["mm"], i + 1)
            act.activation(h[:, n, 2 * half:2 * half + 2, 0:C1],
                           ps[:, i % 8, :].rearrange("p (q c) -> p q c", q=2), ACT.Copy).then_inc(sem["h"], 1)
        act.wait_ge(sem["als2"], 1)
        for q in range(H1):
            for s in range(NT):
                i = q * NT + s
                bank = 4 + 2 * (q % 2)
                act.wait_ge(sem["db"], 2 * (q + 1))
                if i >= 2:
                    act.wait_ge(sem["pm"], i - 1)
                act.activation(ex[:, i % 2, 0, :], ps[:, bank, :], ACT.Exp, bias=al[:, s, 0, q:q + 1]
                               ).then_inc(sem["ex1"], 1)
                act.wait_ge(sem["ex1"], i + 1)
                act.activation(ex[:, i % 2, 1, :], ps[:, bank + 1, :], ACT.Exp, bias=als2[:, s, q:q + 1]
                               ).then_inc(sem["ex2"], 1)
        for c in range(0, HT, 2):
            act.wait_ge(sem["tr2"], c + 1)
            act.activation(outT[:, c, :], ps[:, c, :], ACT.Relu).then_inc(sem["oT"], 1)

    @block.tensor
    def _(pe):
        if x_in is not None:
            transposes(pe, cx, x_in, kt, None, sem["tr"])
            pe.wait_ge(sem["xT"], kt)
        pe.wait_ge(s_w, w_count)
        for i in range(NT * 2):
            n, half = i // 2, i % 2
            product(pe, ps[:, i % 8, :], [(xT[:, k, n * P:(n + 1) * P], W[:, k, half * C:(half + 1) * C])
                                          for k in range(kt)]).then_inc(sem["mm"], 1)

        def spread(bank, column, done):
            for n in range(NT):
                m = pe.matmul(ps[:, bank, n * P:(n + 1) * P], column(n).to_broadcast([P, P]), cx.ident[:],
                              start=True, stop=True)
            m.then_inc(done, 1)

        pe.wait_ge(sem["als2"], 1)
        for q in range(H1):
            spread(q, lambda n: al[:, n, 0, q:q + 1], sem["asb"])
        pe.wait_ge(sem["dd"], 2)

        def spread_dst(q):
            if q >= 2:
                pe.wait_ge(sem["ex2"], NT * (q - 1))
            for k in range(2):
                spread(4 + 2 * (q % 2) + k, lambda n: dd[:, k, n, q:q + 1], sem["db"])

        pe.wait_ge(sem["ones"], 1)
        spread_dst(0)
        for q in range(H1):
            if q + 1 < H1:
                spread_dst(q + 1)
            pe.wait_ge(sem["p"], NT * (q + 1))
            for n in range(NT):
                if q:
                    pe.wait_ge(sem["o"], NT * (q - 1) + n + 1)
                product(pe, ps[:, n, 0:C1 + 2],
                        [(pr[:, q % 2, s, n * P:(n + 1) * P], h[:, s, q, 0:C1 + 2]) for s in range(NT)]
                        ).then_inc(sem["agg"], 1)
        pe.wait_ge(sem["o"], NT * H1)
        transposes(pe, cx, o, HT, None, sem["tr2"])

    tmp.close()
    cx.end_phase()


def gat_out(cx, st, hT):
    nc, io = cx.nc, cx.io
    tmp = ExitStack()
    bfc = cx.sb("bfc_b", [P, C], F32, tmp)
    xb = cx.sb("xb1", [P, NT, C], F32, tmp)
    y = cx.sb("y1", [P, NT, C], F32, tmp)
    norm = Norm(cx, "n3", tmp)
    s_small, s_xb, s_mm, s_y = (cx.sem("s5_" + n) for n in ("small", "xb", "mm", "y"))
    Wfc = cx.wA[:, 2:4].rearrange("p a k n -> p (a k) n")
    ps = cx.ps
    block = tmp.enter_context(nc.Block())

    @block.sync
    def _(sp):
        sp.dma_start(bfc[:], row_b(io["L1_gnn_bfc"])).then_inc(s_small, 16)

    @block.vector
    def _(dve):
        dve.wait_ge(s_small, 16)
        for n in range(NT):
            dve.tensor_tensor(xb[:, n, :], cx.x[:, n, :], bfc[:], ALU.add).then_inc(s_xb, 1)
        dve.wait_ge(s_xb, NT)
        for n in range(NT):
            dve.wait_ge(s_mm, n + 1)
            dve.tensor_tensor(y[:, n, :], ps[:, n, :], xb[:, n, :], ALU.add).then_inc(s_y, 1)
        norm_vector(dve, norm, y, cx.x, s_y)

    @block.scalar
    def _(act):
        norm_scalar(act, norm)

    @block.tensor
    def _(pe):
        for n in range(NT):
            product(pe, ps[:, n, :], [(hT[:, k, n * P:(n + 1) * P], Wfc[:, k, :]) for k in range(HT)]
                    ).then_inc(s_mm, 1)

    tmp.close()
    cx.end_phase()


def residual_layer(cx, st):
    nc, io = cx.nc, cx.io
    tmp = ExitStack()
    W1e = cx.sb("W1e", [P, HID], F32, tmp)
    b1 = cx.sb("b12", [P, HT], F32, tmp)
    b2 = cx.sb("b22_b", [P, C], F32, tmp)
    hT = cx.sb("h2T", [P, HT, N], F32, tmp)
    xb = cx.sb("xb2", [P, NT, C], F32, tmp)
    y = cx.sb("y2", [P, NT, C], F32, tmp)
    norm = Norm(cx, "n4", tmp)
    names = ("small", "w", "tr", "xT", "h", "hT", "xb", "mm", "y")
    sem = {n: cx.sem("s6_" + n) for n in names}
    W1 = cx.wA[:].rearrange("p a k n -> p (a k n)")[:, 0:CT * HID].rearrange("p (k n) -> p k n", k=CT)
    W2 = cx.wA[:].rearrange("p a k n -> p (a k n)")[:, CT * HID:].rearrange("p (k n) -> p k n", k=HT)
    ps = cx.ps
    block = tmp.enter_context(nc.Block())

    @block.sync
    def _(sp):
        sp.dma_start(W1, rows(io["L2_gnn_W1"][0:C, :])).then_inc(sem["w"], 16)
        for k in range(2):
            sp.dma_start(W1e[k * EA:(k + 1) * EA, :], io["L2_gnn_W1"][C:C + EA, :]).then_inc(sem["w"], 16)
        sp.dma_start(b1[:], col(io["L2_gnn_b1"], HT), allow_slow_non_contiguous=True).then_inc(sem["small"], 16)
        sp.dma_start(b2[:], row_b(io["L2_gnn_b2"])).then_inc(sem["small"], 16)
        sp.dma_start(W2, rows(io["L2_gnn_W2"])).then_inc(sem["w"], 16)

    @block.vector
    def _(dve):
        for c in range(CT):
            dve.wait_ge(sem["tr"], c + 1)
            dve.tensor_copy(cx.xT[:, c, :], ps[:, c, :]).then_inc(sem["xT"], 1)
        dve.wait_ge(sem["small"], 32)
        for n in range(NT):
            dve.scalar_tensor_tensor(out=xb[:, n, :], in0=cx.x[:, n, :], scalar=2.0, in1=b2[:], op0=ALU.mult,
                                     op1=ALU.add).then_inc(sem["xb"], 1)
        dve.wait_ge(sem["xb"], NT)
        for n in range(NT):
            dve.wait_ge(sem["mm"], n + 1)
            dve.tensor_tensor(y[:, n, :], ps[:, 4 + n, :], xb[:, n, :], ALU.add).then_inc(sem["y"], 1)
        norm_vector(dve, norm, y, cx.x, sem["y"])

    @block.scalar
    def _(act):
        act.wait_ge(sem["small"], 32)
        for m in range(HT):
            act.wait_ge(sem["h"], m + 1)
            act.activation(hT[:, m, :], ps[:, (4 + m) % 8, :], ACT.Relu, bias=b1[:, m:m + 1]).then_inc(sem["hT"], 1)
        norm_scalar(act, norm)

    @block.tensor
    def _(pe):
        transposes(pe, cx, cx.x, CT, None, sem["tr"])
        pe.wait_ge(sem["xT"], CT)
        pe.wait_ge(sem["w"], 64)
        for m in range(HT):
            product(pe, ps[:, (4 + m) % 8, :],
                    [(W1[:, k, m * P:(m + 1) * P], cx.xT[:, k, :]) for k in range(CT)]
                    + [(W1e[:, m * P:(m + 1) * P], cx.ea_mean[:])]).then_inc(sem["h"], 1)
        pe.wait_ge(sem["hT"], HT)
        for n in range(NT):
            product(pe, ps[:, 4 + n, :], [(hT[:, k, n * P:(n + 1) * P], W2[:, k, :]) for k in range(HT)]
                    ).then_inc(sem["mm"], 1)

    tmp.close()
    cx.end_phase()


def edge_mlp_nodes(cx, st):
    nc, io = cx.nc, cx.io
    tmp = ExitStack()
    W = cx.wB[:].rearrange("p (k n) -> p k n", n=C)
    b1 = cx.sb("b13_b", [P, C], F32, tmp)
    out = cx.sb("xab", [P, 2, NT, C], F32, tmp)
    names = ("w", "small", "tr", "xT", "mm", "out", "dram")
    sem = {n: cx.sem("s7_" + n) for n in names}
    ps = cx.ps
    block = tmp.enter_context(nc.Block())

    @block.sync
    def _(sp):
        sp.dma_start(W[:, 0:2 * CT, :], rows(io["L3_gnn_W1"][0:2 * C, :])).then_inc(sem["w"], 16)
        sp.dma_start(b1[:], row_b(io["L3_gnn_b1"])).then_inc(sem["small"], 16)
        for k, dram in enumerate((st["xa_dram"], st["xb_dram"])):
            sp.wait_ge(sem["out"], NT * (k + 1))
            sp.dma_start(dram.rearrange("(n p) c -> p n c", p=P), out[:, k]).then_inc(sem["dram"], 16)
        sp.wait_ge(sem["dram"], 32)

    @block.vector
    def _(dve):
        for c in range(CT):
            dve.wait_ge(sem["tr"], c + 1)
            dve.tensor_copy(cx.xT[:, c, :], ps[:, c, :]).then_inc(sem["xT"], 1)
        dve.wait_ge(sem["small"], 16)
        for i in range(2 * NT):
            k, n = i // NT, i % NT
            dve.wait_ge(sem["mm"], i + 1)
            if k == 0:
                dve.tensor_tensor(out[:, k, n, :], ps[:, (4 + i) % 8, :], b1[:], ALU.add).then_inc(sem["out"], 1)
            else:
                dve.tensor_copy(out[:, k, n, :], ps[:, (4 + i) % 8, :]).then_inc(sem["out"], 1)

    @block.tensor
    def _(pe):
        transposes(pe, cx, cx.x, CT, None, sem["tr"])
        pe.wait_ge(sem["xT"], CT)
        pe.wait_ge(sem["w"], 16)
        for i in range(2 * NT):
            k, n = i // NT, i % NT
            product(pe, ps[:, (4 + i) % 8, :],
                    [(cx.xT[:, c, n * P:(n + 1) * P], W[:, k * CT + c, :]) for c in range(CT)]
                    ).then_inc(sem["mm"], 1)

    tmp.close()
    cx.end_phase()


def edge_mlp(cx, st):
    nc, io = cx.nc, cx.io
    tmp = ExitStack()
    B = 2
    NB = ET // B
    W2h = cx.sb("W2h", [P, CT, C], F32R, tmp)
    W2l = cx.sb("W2l", [P, CT, C], F32R, tmp)
    Wch = cx.sb("Wch", [P, C], F32R, tmp)
    Wcl = cx.sb("Wcl", [P, C], F32R, tmp)
    b2 = cx.sb("b23_b", [P, C], F32, tmp)
    g = cx.sb("g", [P, 2, B, 2, C], F32, tmp)
    x1 = cx.wB[:, 0:2048].rearrange("p (r c e) -> p r c e", r=2, c=CT)
    x2 = cx.wB[:, 2048:4096].rearrange("p (r u c) -> p r u c", r=2, u=B)
    q = cx.sb("q", [P, 2, CT * B * P], F32, tmp)
    t = cx.wB[:, 4096:8192].rearrange("p (r k e) -> p r k e", r=2, k=2)
    f = cx.wA[:, 3].rearrange("p k c -> p (k c)").rearrange("p (a e) -> p a e", a=2)
    W2f = f.rearrange("p a (k c) -> p (a k) c", k=2)
    Wcf = q[:, 0, 0:C]
    hh = cx.sb("hh", [P, 2, CT, B * P], F32R, tmp)
    hl = cx.sb("hl", [P, 2, CT, B * P], F32R, tmp)
    mh = cx.sb("mh", [P, 2, B, C], F32R, tmp)
    ml = cx.sb("ml", [P, 2, B, C], F32R, tmp)
    oh = cx.sb("oh3", [P, 2, B, N], F32R, tmp)
    names = ("w", "wh", "wl", "pre", "x1", "w2", "x2", "q1", "q2", "a1", "a2", "t1", "t2", "h", "m", "hh", "mh",
             "hl", "ml", "oh", "sum")
    sem = {n: cx.sem("s8_" + n) for n in names}
    s_g = [cx.sem(f"s8_g{i}") for i in range(2 * B * 2)]
    ps = cx.ps
    block = tmp.enter_context(nc.Block())
    FLAT = CT * B * P

    def rounds(engine, body):
        for k in range(-3, 1):
            body(k, k % 2, lambda a, c: a * k + c, {s for s, (lo, hi) in SPAN.items() if lo <= k <= hi})
        first, last = 1, NB - 4
        assert (last - first + 1) % 2 == 0
        with engine.Fori(0, (last - first + 1) // 2) as j:
            for v in range(2):
                k0 = first + v
                body(k0, k0 % 2, lambda a, c, k0=k0: j * (2 * a) + (a * k0 + c), set(SPAN))
        for k in range(last + 1, NB + 1):
            body(k, k % 2, lambda a, c: a * k + c, {s for s, (lo, hi) in SPAN.items() if lo <= k <= hi})

    SPAN = {"pre": (-3, NB - 4), "mish1": (-2, NB - 3), "second": (-1, NB - 2), "mish2": (0, NB - 1),
            "sum": (1, NB)}

    @block.sync
    def _(sp):
        sp.dma_start(W2f[:], rows(io["L3_gnn_W2"])).then_inc(sem["w"], 16)
        for k in range(2):
            sp.dma_start(Wcf[k * EA:(k + 1) * EA, :], io["L3_gnn_W1"][2 * C:2 * C + EA, :]).then_inc(sem["w"], 16)
        sp.dma_start(b2[:], row_b(io["L3_gnn_b2"])).then_inc(sem["w"], 16)
        sp.dma_start(cx.wA[:].rearrange("p a k n -> p (a k) n")[:, 0:2 * CT, :], rows(io["L3_gnn_W3"])
                     ).then_inc(st["s_w3"], 16)
        sp.dma_start(cx.wA[:].rearrange("p a k n -> p (a k) n")[:, 2 * CT:3 * CT, :], rows(io["L3_gnn_W4"])
                     ).then_inc(st["s_w3"], 16)

    @block.gpsimd
    def _(pool):
        for b in range(NB):
            for u in range(B):
                for k, (dram, idx) in enumerate(((st["xa_dram"], cx.src_i), (st["xb_dram"], cx.dst_i))):
                    if b >= 2 and u == 0 and k == 0:
                        pool.wait_ge(sem["pre"], 2 * (b - 1))
                    tile = b * B + u
                    pool.indirect_dma_start(g[:, b % 2, u, k, :], None, dram,
                                            Offset(ap=idx[:, tile:tile + 1], axis=0)
                                            ).then_inc(s_g[((b % 2) * B + u) * 2 + k], 16)

    @block.vector
    def _(dve):
        dve.wait_ge(sem["w"], 64)
        dve.tensor_copy(W2h[:], W2f[:]).then_inc(sem["wh"], 1)
        dve.tensor_copy(Wch[:], Wcf[:]).then_inc(sem["wh"], 1)
        dve.wait_ge(sem["wh"], 2)
        dve.tensor_tensor(W2l[:], W2f[:], W2h[:].bitcast(F32), ALU.subtract).then_inc(sem["wl"], 1)
        dve.tensor_tensor(Wcl[:], Wcf[:], Wch[:].bitcast(F32), ALU.subtract).then_inc(sem["wl"], 1)
        dve.sem_inc(sem["sum"], 2)

        def body(k, r, at, on):
            if "second" in on:
                for u in range(B):
                    dve.wait_ge(sem["w2"], at(B, B + u + 1))
                    if k >= 1 and u == 0:
                        dve.wait_ge(sem["m"], at(1, 0))
                    dve.tensor_tensor(x2[:, 1 - r, u, :], ps[:, 2 + u, :], b2[:], ALU.add).then_inc(sem["x2"], 1)
            if "sum" in on:
                dve.wait_ge(sem["sum"], at(1, 0))
                for u in range(B):
                    dve.tensor_scalar(oh[:, 1 - r, u, :], cx.iota_h[:], cx.dst_f[:, bass.ds(at(B, u - B), 1)],
                                      None, ALU.is_equal).then_inc(sem["oh"], 1)
            if "pre" in on:
                for h in range(2):
                    dve.wait_ge(sem["pre"], at(2, 7 + h))
                    if k >= -1 and h == 0:
                        dve.wait_ge(sem["h"], at(1, 2))
                    dve.tensor_copy(x1[:, 1 - r, 2 * h:2 * h + 2, :].rearrange("p c e -> p (c e)"),
                                    ps[:, h, :]).then_inc(sem["x1"], 1)
            if "mish1" in on:
                dve.wait_ge(sem["t1"], at(1, 3))
                if k >= -1:
                    dve.wait_ge(sem["hl"], at(1, 2))
                dve.tensor_tensor(f[:, 0], x1[:, r].rearrange("p c e -> p (c e)"), t[:, r, 0], ALU.mult
                                  ).then_inc(sem["h"], 1)
            if "mish2" in on:
                dve.wait_ge(sem["t2"], at(1, 1))
                if k >= 1:
                    dve.wait_ge(sem["ml"], at(1, 0))
                dve.tensor_tensor(f[:, 1], x2[:, r].rearrange("p u c -> p (u c)"), t[:, r, 1], ALU.mult
                                  ).then_inc(sem["m"], 1)
            if "mish1" in on:
                dve.wait_ge(sem["h"], at(1, 3))
                if k >= 0:
                    dve.wait_ge(sem["w2"], at(B, B))
                dve.tensor_copy(hh[:, r].rearrange("p c e -> p (c e)"), f[:, 0]).then_inc(sem["hh"], 1)
            if "mish2" in on:
                dve.wait_ge(sem["m"], at(1, 1))
                if k >= 2:
                    dve.wait_ge(sem["sum"], at(1, 1))
                dve.tensor_copy(mh[:, r].rearrange("p u c -> p (u c)"), f[:, 1]).then_inc(sem["mh"], 1)
            if "mish1" in on:
                dve.wait_ge(sem["hh"], at(1, 3))
                dve.tensor_tensor(hl[:, r].rearrange("p c e -> p (c e)"), f[:, 0],
                                  hh[:, r].rearrange("p c e -> p (c e)").bitcast(F32), ALU.subtract
                                  ).then_inc(sem["hl"], 1)
            if "mish2" in on:
                dve.wait_ge(sem["mh"], at(1, 1))
                dve.tensor_tensor(ml[:, r].rearrange("p u c -> p (u c)"), f[:, 1],
                                  mh[:, r].rearrange("p u c -> p (u c)").bitcast(F32), ALU.subtract
                                  ).then_inc(sem["ml"], 1)

        rounds(dve, body)

    @block.scalar
    def _(act):
        def body(k, r, at, on):
            if "mish1" in on:
                act.wait_ge(sem["x1"], at(2, 6))
                if k >= -1:
                    act.wait_ge(sem["t1"], at(1, 2))
                act.activation(q[:, 0], x1[:, r].rearrange("p c e -> p (c e)"), ACT.Sigmoid, scale=-1.0
                               ).then_inc(sem["q1"], 1)
            if "mish2" in on:
                act.wait_ge(sem["x2"], at(B, B))
                if k >= 1:
                    act.wait_ge(sem["t2"], at(1, 0))
                act.activation(q[:, 1], x2[:, r].rearrange("p u c -> p (u c)"), ACT.Sigmoid, scale=-1.0
                               ).then_inc(sem["q2"], 1)
            if "mish1" in on:
                act.wait_ge(sem["q1"], at(1, 3))
                act.activation(q[:, 0], q[:, 0], ACT.Arctan).then_inc(sem["a1"], 1)
            if "mish2" in on:
                act.wait_ge(sem["q2"], at(1, 1))
                act.activation(q[:, 1], q[:, 1], ACT.Arctan).then_inc(sem["a2"], 1)
            if "mish1" in on:
                act.wait_ge(sem["a1"], at(1, 3))
                if k >= 0:
                    act.wait_ge(sem["h"], at(1, 1))
                act.activation(t[:, r, 0], q[:, 0], ACT.Sin, bias=cx.half_pi[:], scale=-2.0).then_inc(sem["t1"], 1)
            if "mish2" in on:
                act.wait_ge(sem["a2"], at(1, 1))
                if k >= 2:
                    act.wait_ge(sem["m"], at(1, -1))
                act.activation(t[:, r, 1], q[:, 1], ACT.Sin, bias=cx.half_pi[:], scale=-2.0).then_inc(sem["t2"], 1)

        rounds(act, body)

    @block.tensor
    def _(pe):
        for c in range(CT):
            pe.matmul(ps[:, 4 + c, :], cx.zero_r[:, 0:P], cx.zero_r[:], start=True, stop=False)
        pe.wait_ge(sem["wl"], 2)

        def body(k, r, at, on):
            if "second" in on:
                pe.wait_ge(sem["hl"], at(1, 2))
                for u in range(B):
                    if k >= 0:
                        pe.wait_ge(sem["x2"], at(B, u + 1))
                    cols = slice(u * P, (u + 1) * P)
                    product(pe, ps[:, 2 + u, :],
                            [(a[:, 1 - r, c, cols], w[:, c, :]) for c in range(CT)
                             for a, w in ((hh, W2h), (hh, W2l), (hl, W2h))]).then_inc(sem["w2"], 1)
            if "sum" in on:
                pe.wait_ge(sem["ml"], at(1, 0))
                pe.wait_ge(sem["oh"], at(B, 0))
                for u in range(B):
                    for c in range(CT):
                        for a in (mh, ml):
                            m = pe.matmul(ps[:, 4 + c, :], a[:, 1 - r, u, c * P:(c + 1) * P], oh[:, 1 - r, u, :],
                                          start=False, stop=False)
                m.then_inc(sem["sum"], 1)
            if "pre" in on:
                for h in range(2):
                    if k >= -2:
                        pe.wait_ge(sem["x1"], at(2, 5 + h))
                    if h == 0:
                        for i in range(2 * B):
                            slot = (1 - r) * B * 2 + i
                            if k % 2 == 0:
                                pe.wait_ge(s_g[slot], at(8, 32))
                            else:
                                pe.wait_ge(s_g[slot], at(8, 40))
                    for c in (2 * h, 2 * h + 1):
                        out = ps[:, h, (c % 2) * B * P:(c % 2 + 1) * B * P]
                        edges = cx.eaT[:, bass.ds(at(B * P, 3 * B * P), B * P)]
                        pe.matmul(out, Wch[:, c * P:(c + 1) * P], edges, start=True, stop=False)
                        for u in range(B):
                            for i in range(2):
                                pe.matmul(out[:, u * P:(u + 1) * P], g[:, 1 - r, u, i, c * P:(c + 1) * P],
                                          cx.ident[:], is_transpose=True, start=False, stop=False)
                        m = pe.matmul(out, Wcl[:, c * P:(c + 1) * P], edges, start=False, stop=True)
                    m.then_inc(sem["pre"], 1)

        rounds(pe, body)
        for c in range(CT):
            pe.matmul(ps[:, 4 + c, :], cx.zero_r[:, 0:P], cx.zero_r[:], start=False, stop=True)

    tmp.close()
    cx.end_phase()


def edge_mlp_out(cx, st):
    nc, io = cx.nc, cx.io
    tmp = ExitStack()
    aggT = cx.sb("aggT", [P, CT, N], F32, tmp)
    b3 = cx.sb("b33", [P, CT], F32, tmp)
    xu = cx.sb("xu", [P, CT, N], F32, tmp)
    qu = cx.sb("qu", [P, CT, N], F32, tmp)
    uT = cx.sb("uT", [P, CT, N], F32, tmp)
    rowsb = cx.sb("rows3", [P, 3, C], F32, tmp)
    xb = cx.sb("xb3", [P, NT, C], F32, tmp)
    y = cx.sb("y3", [P, NT, C], F32, tmp)
    z = cx.sb("z3", [P, NT, C], F32, tmp)
    n5, n6 = Norm(cx, "n5", tmp), Norm(cx, "n6", tmp)
    names = ("small", "aggT", "mm", "xu", "q", "a", "t", "u", "xb", "mm2", "y", "g", "b", "r", "store")
    sem = {n: cx.sem("s9_" + n) for n in names}
    W = cx.wA[:].rearrange("p a k n -> p (a k) n")
    W3, W4 = W[:, 0:2 * CT, :], W[:, 2 * CT:3 * CT, :]
    ps = cx.ps
    block = tmp.enter_context(nc.Block())

    @block.sync
    def _(sp):
        sp.dma_start(b3[:], col(io["L3_gnn_b3"], CT), allow_slow_non_contiguous=True).then_inc(sem["small"], 16)
        for i, name in enumerate(("L3_gnn_b4", "L3_gnn_gamma", "L3_gnn_beta")):
            sp.dma_start(rowsb[:, i, :], row_b(io[name])).then_inc(sem["small"], 16)
        sp.wait_ge(n6.s_out, NT)
        sp.dma_start(rows(io["out"]), z[:]).then_inc(sem["store"], 16)
        sp.wait_ge(sem["store"], 16)

    @block.vector
    def _(dve):
        for c in range(1, CT, 2):
            dve.tensor_copy(aggT[:, c, :], ps[:, 4 + c, :]).then_inc(sem["aggT"], 1)
        dve.wait_ge(sem["small"], 64)
        for n in range(NT):
            dve.tensor_tensor(xb[:, n, :], cx.x[:, n, :], rowsb[:, 0, :], ALU.add).then_inc(sem["xb"], 1)
        for c in range(CT):
            dve.wait_ge(sem["mm"], c + 1)
            dve.tensor_scalar(xu[:, c, :], ps[:, c, :], b3[:, c:c + 1], None, ALU.add).then_inc(sem["xu"], 1)
        dve.wait_ge(sem["xu"], CT)
        for c in range(CT):
            dve.wait_ge(sem["t"], 1)
            dve.tensor_tensor(uT[:, c, :], xu[:, c, :], qu[:, c, :], ALU.mult).then_inc(sem["u"], 1)
        dve.wait_ge(sem["xb"], NT)
        for n in range(NT):
            dve.wait_ge(sem["mm2"], n + 1)
            dve.tensor_tensor(y[:, n, :], ps[:, 4 + n, :], xb[:, n, :], ALU.add).then_inc(sem["y"], 1)
        norm_vector(dve, n5, y, z, sem["y"])
        dve.wait_ge(n5.s_out, NT)
        for n in range(NT):
            dve.tensor_tensor(xb[:, n, :], z[:, n, :], rowsb[:, 1, :], ALU.mult).then_inc(sem["g"], 1)
        for n in range(NT):
            dve.wait_ge(sem["g"], n + 1)
            dve.tensor_tensor(z[:, n, :], xb[:, n, :], rowsb[:, 2, :], ALU.add).then_inc(sem["b"], 1)
        for n in range(NT):
            dve.wait_ge(sem["b"], n + 1)
            dve.tensor_tensor(y[:, n, :], z[:, n, :], cx.x[:, n, :], ALU.add).then_inc(sem["r"], 1)
        norm_vector(dve, n6, y, z, sem["r"])

    @block.scalar
    def _(act):
        for c in range(0, CT, 2):
            act.activation(aggT[:, c, :], ps[:, 4 + c, :], ACT.Copy).then_inc(sem["aggT"], 1)
        act.wait_ge(sem["xu"], CT)
        act.activation(qu[:], xu[:], ACT.Sigmoid, scale=-1.0).then_inc(sem["q"], 1)
        act.wait_ge(sem["q"], 1)
        act.activation(qu[:], qu[:], ACT.Arctan).then_inc(sem["a"], 1)
        act.wait_ge(sem["a"], 1)
        act.activation(qu[:], qu[:], ACT.Sin, bias=cx.half_pi[:], scale=-2.0).then_inc(sem["t"], 1)
        norm_scalar(act, n5)
        norm_scalar(act, n6)

    @block.tensor
    def _(pe):
        pe.wait_ge(sem["aggT"], CT)
        pe.wait_ge(st["s_w3"], 32)
        for c in range(CT):
            product(pe, ps[:, c, :],
                    [(W3[:, k, c * P:(c + 1) * P], cx.xT[:, k, :]) for k in range(CT)]
                    + [(W3[:, CT + k, c * P:(c + 1) * P], aggT[:, k, :]) for k in range(CT)]
                    ).then_inc(sem["mm"], 1)
        pe.wait_ge(sem["u"], CT)
        for n in range(NT):
            product(pe, ps[:, 4 + n, :], [(uT[:, k, n * P:(n + 1) * P], W4[:, k, :]) for k in range(CT)]
                    ).then_inc(sem["mm2"], 1)

    tmp.close()
    cx.end_phase()


def build_program(nc, io):
    with ExitStack() as stack:
        cx = Ctx(nc, io, stack)
        cx.ps = stack.enter_context(nc.psum_tensor("ps", [P, 8, 512], F32))
        cx.ident = cx.sb("ident", [P, P])
        cx.zero_r = cx.sb("zero_r", [P, C], F32R)
        cx.iota_h = cx.sb("iota_h", [P, N], FP16)
        cx.half_pi = cx.sb("half_pi", [P, 1])
        cx.x = cx.sb("x", [P, NT, C])
        cx.xT = cx.sb("xT", [P, CT, N])
        cx.src_i = cx.sb("src_i", [P, ET], I32)
        cx.dst_i = cx.sb("dst_i", [P, ET], I32)
        cx.src_f = cx.sb("src_f", [P, ET])
        cx.dst_f = cx.sb("dst_f", [P, ET])
        cx.wA = cx.sb("wA", [P, 4, CT, C])
        cx.wB = cx.sb("wB", [P, HT * HID])
        st = {"pair_i": cx.sb("pair_i", [P, ET], I32)}
        for name in ("s_w0", "s_w1", "s_w2", "s_w3"):
            st[name] = stack.enter_context(nc.semaphore(name))
        for name, shape in (("v_dram", [N, C]), ("s_dram", [N * N, H0]), ("xa_dram", [N, C]), ("xb_dram", [N, C])):
            st[name] = nc.dram_tensor(name, shape, F32).ap()
        st["weights0"] = [(cx.wA[:, i], f"L0_gnn_{n}") for i, n in enumerate(("Wq", "Wk", "Wv", "Wo"))]
        with ExitStack() as layer0:
            st["ohT"] = cx.sb("ohT", [P, NT, E], BF16, layer0)
            setup(cx, st)
            attention_scores(cx, st)
            attention_edges(cx, st)
        attention_out(cx, st)
        cx.eaT = cx.sb("eaT", [P, E], F32R)
        with ExitStack() as graph:
            cx.cnt = cx.sb("cnt", [P, NT, N], F32, graph)
            cx.pen = cx.sb("pen", [P, NT, N], F32, graph)
            cx.rcount = cx.sb("rcount", [P, N], F32, graph)
            cx.ea_mean = cx.sb("ea_mean", [P, N], F32, graph)
            edge_sums(cx, st)
            with ExitStack() as layer1:
                h1 = cx.sb("h1", [P, NT * H1 * W_], F32, layer1)
                h2 = cx.sb("h2", [P, NT * H1 * W_], F32, layer1)
                gat(cx, st, "g1", cx.wA[:, 0:2].rearrange("p a k n -> p (a k n)").rearrange("p (k n) -> p k n", k=CT),
                    CT, cx.xT, h1, io["L1_gnn_a_src1"], io["L1_gnn_a_dst1"], io["L1_gnn_b1"], st["s_w2"], 48, cx.x)
                gat(cx, st, "g2", cx.wB[:].rearrange("p (k n) -> p k n", k=HT), HT, gat_output(h1), h2,
                    io["L1_gnn_a_src2"], io["L1_gnn_a_dst2"], io["L1_gnn_b2"], st["s_w2"], 48, None)
                gat_out(cx, st, gat_output(h2))
            residual_layer(cx, st)
            edge_mlp_nodes(cx, st)
        edge_mlp(cx, st)
        edge_mlp_out(cx, st)


USED = ("x", "src", "dst", "edge_attr_64", "edge_attr_8",
        *(f"L0_gnn_{n}" for n in ("Wq", "bq", "Wk", "bk", "Wv", "bv", "Wo", "bo", "ln1_g", "ln1_b", "ln2_g",
                                  "ln2_b", "W1", "b1", "W2", "b2")),
        *(f"L1_gnn_{n}" for n in ("W1", "a_src1", "a_dst1", "b1", "W2", "a_src2", "a_dst2", "b2", "Wfc", "bfc")),
        *(f"L2_gnn_{n}" for n in ("W1", "b1", "W2", "b2")),
        *(f"L3_gnn_{n}" for n in ("W1", "b1", "W2", "b2", "W3", "b3", "W4", "b4", "gamma", "beta")))


def kernel(**inputs):
    import numpy as np
    import concourse.bacc as bacc
    from concourse.bass_utils import run_bass_kernel_spmd

    nc = bacc.Bacc("TRN2", target_bir_lowering=False, num_devices=1)
    arrays, io = {}, {}
    for name in USED:
        a = np.ascontiguousarray(inputs[name])
        arrays[f"in_{name}_dram"] = a
        io[name] = nc.dram_tensor(f"in_{name}_dram", a.shape, mybir.dt.from_np(a.dtype), kind="ExternalInput").ap()
    io["out"] = nc.dram_tensor("out_0_dram", [N, C], F32, kind="ExternalOutput").ap()
    build_program(nc, io)
    r = run_bass_kernel_spmd(nc, [arrays], core_ids=[0])
    return r.results[0]["out_0_dram"]
```

```python
from contextlib import ExitStack

import concourse.bass as bass
from concourse import mybir

F32 = mybir.dt.float32
F32R = mybir.dt.float32r
BF16 = mybir.dt.bfloat16
FP16 = mybir.dt.float16
I32 = mybir.dt.int32
ALU = mybir.AluOpType
ACT = mybir.ActivationFunctionType
AX = mybir.AxisListType
Offset = bass.IndirectOffsetOnAxis

P = 128
N = 512
C = 512
E = 8192
NT = N // P
CT = C // P
ET = E // P
H0, D0 = 8, 64
HID = 1024
HT = HID // P
H1, C1 = 4, 256
EA = 64
EPS = 1e-5
LN2 = 0.6931471805599453
BIG = 3.0e38
HALF_PI = 1.5707963267948966
GUARD_T, GUARD_M = 8.0, 8
GUARD_STEP = 108 * LN2 * GUARD_T
GUARD_MARGIN = 30.0


class Ctx:

    def __init__(self, nc, io, stack):
        self.nc, self.io, self.stack = nc, io, stack
        self.phase_sems = []

    def sb(self, name, shape, dt=F32, stack=None):
        return (stack or self.stack).enter_context(self.nc.sbuf_tensor(name, shape, dt))

    def sem(self, name):
        s = self.nc.alloc_semaphore(name=name)
        self.phase_sems.append(s)
        return s

    def end_phase(self):
        self.nc.clear_and_free_semaphores(self.phase_sems)
        self.nc.all_engine_barrier()
        self.phase_sems = []


def row_b(vec):
    return vec.partition_broadcast(P)


def col(vec, tiles):
    return vec.rearrange("(k p) -> p k", p=P)


def rows(mat):
    return mat.rearrange("(k p) n -> p k n", p=P)


class Norm:

    def __init__(self, cx, tag, stack):
        self.stats = cx.sb(f"{tag}_stats", [P, NT, 6], F32, stack)
        self.mv = cx.sb(f"{tag}_mv", [P, NT, 2], F32, stack)
        self.var = cx.sb(f"{tag}_var", [P, NT], F32, stack)
        self.std = cx.sb(f"{tag}_std", [P, NT], F32, stack)
        self.rstd = cx.sb(f"{tag}_rstd", [P, NT], F32, stack)
        self.s_stats = cx.sem(f"{tag}_s_stats")
        self.s_aggr = cx.sem(f"{tag}_s_aggr")
        self.s_var = cx.sem(f"{tag}_s_var")
        self.s_std = cx.sem(f"{tag}_s_std")
        self.s_rstd = cx.sem(f"{tag}_s_rstd")
        self.s_out = cx.sem(f"{tag}_s_out")


def norm_vector(e, n, x, out, s_x):
    for i in range(NT):
        e.wait_ge(s_x, i + 1)
        e.bn_stats(n.stats[:, i, :], x[:, i, :]).then_inc(n.s_stats, 1)
    for i in range(NT):
        e.wait_ge(n.s_stats, i + 1)
        e.bn_aggr(n.mv[:, i, :], n.stats[:, i, :]).then_inc(n.s_aggr, 1)
    e.wait_ge(n.s_aggr, NT)
    e.tensor_scalar(n.var[:], n.mv[:, :, 1], EPS, None, ALU.add).then_inc(n.s_var, 1)
    e.wait_ge(n.s_std, 1)
    e.reciprocal(n.rstd[:], n.std[:]).then_inc(n.s_rstd, 1)
    e.wait_ge(n.s_rstd, 1)
    for i in range(NT):
        e.tensor_scalar(out[:, i, :], x[:, i, :], n.mv[:, i, 0:1], n.rstd[:, i:i + 1],
                        ALU.subtract, ALU.mult).then_inc(n.s_out, 1)


def norm_scalar(e, n):
    e.wait_ge(n.s_var, 1)
    e.activation(n.std[:], n.var[:], ACT.Sqrt).then_inc(n.s_std, 1)


def transposes(pe, cx, x, tiles, s_x, s_done, bank0=0, s_free=None):
    for c in range(tiles):
        for n in range(NT):
            if c == 0 and s_x is not None:
                pe.wait_ge(s_x, n + 1)
            t = pe.transpose(cx.ps[:, bank0 + c, n * P:(n + 1) * P], x[:, n, c * P:(c + 1) * P], cx.ident[:])
        t.then_inc(s_done, 1)


def product(pe, out, pairs):
    for k, (lhsT, rhs) in enumerate(pairs):
        m = pe.matmul(out, lhsT, rhs, start=(k == 0), stop=(k == len(pairs) - 1))
    return m


def setup(cx, st):
    nc, io = cx.nc, cx.io
    tmp = ExitStack()
    iota_i = cx.sb("iota_i", [P, N], I32, tmp)
    part_i = cx.sb("part_i", [P, NT], I32, tmp)
    s_in, s_const, s_f = cx.sem("s_in"), cx.sem("s_const"), cx.sem("s_f")
    s_zero = cx.sem("s_zero")
    block = tmp.enter_context(nc.Block())

    @block.sync
    def _(sp):
        sp.dma_start(cx.src_i[:], io["src"].rearrange("(p t) -> p t", p=P)).then_inc(s_in, 16)
        sp.dma_start(cx.dst_i[:], io["dst"].rearrange("(p t) -> p t", p=P)).then_inc(s_in, 16)
        sp.dma_start(cx.x[:], rows(io["x"])).then_inc(st["s_x0"], 16)

    @block.scalar
    def _(act):
        for w, (buf, name) in enumerate(st["weights0"]):
            act.dma_start(buf, rows(io[name])).then_inc(st["s_w0"], 16)

    @block.gpsimd
    def _(pool):
        pool.memset(cx.ident[:], 0.0).then_inc(s_zero, 1)
        pool.iota(iota_i[:], pattern=[[1, N]], base=0, channel_multiplier=0).then_inc(s_const, 1)
        pool.iota(part_i[:], pattern=[[P, NT]], base=0, channel_multiplier=1).then_inc(s_const, 1)
        pool.memset(cx.half_pi[:], HALF_PI)
        pool.wait_ge(s_zero, 1)
        pool.affine_select(out=cx.ident[:], in_=cx.ident[:], compare_op=ALU.not_equal, fill=1.0, base=0,
                           pattern=[[-1, P]], channel_multiplier=1)

    @block.vector
    def _(dve):
        dve.memset(cx.zero_r[:].bitcast(F32), 0.0)
        dve.wait_ge(s_const, 2)
        dve.tensor_copy(cx.iota_h[:], iota_i[:])
        dve.tensor_copy(cx.part_f[:], part_i[:]).then_inc(s_f, 1)
        dve.wait_ge(s_in, 32)
        dve.tensor_copy(cx.src_f[:], cx.src_i[:]).then_inc(s_f, 1)
        dve.tensor_copy(cx.dst_f[:], cx.dst_i[:]).then_inc(s_f, 1)
        dve.wait_ge(s_f, 3)
        dve.scalar_tensor_tensor(out=st["pair_i"][:], in0=cx.src_f[:], scalar=float(N), in1=cx.dst_f[:],
                                 op0=ALU.mult, op1=ALU.add)

    tmp.close()
    cx.end_phase()


def attention_scores(cx, st):
    nc, io = cx.nc, cx.io
    tmp = ExitStack()
    z = cx.sb("z0", [P, NT, C], F32, tmp)
    qT = cx.sb("qT", [P, CT, N], F32, tmp)
    kT = cx.sb("kT", [P, CT, N], F32, tmp)
    v = cx.sb("v", [P, NT, C], F32, tmp)
    stage = cx.wB[:].rearrange("p (a n h) -> p a n h", a=2, h=H0)
    bv = cx.sb("bv_b", [P, C], F32, tmp)
    cols = cx.sb("cols0", [P, 4, CT], F32, tmp)
    norm = Norm(cx, "n0", tmp)
    s_small = cx.sem("s0_small")
    s_x, s_tr, s_zT, s_v, s_vout = (cx.sem("s0_" + n) for n in ("x", "tr", "zT", "v", "vout"))
    s_vmm, s_qk, s_qk_out, s_smm = (cx.sem("s0_" + n) for n in ("vmm", "qk", "qk_out", "smm"))
    s_spread, s_row = cx.sem("s0_spread"), cx.sem("s0_row")
    s_ev = [cx.sem("s0_ev_act"), cx.sem("s0_ev_dve")]
    s_st = [cx.sem("s0_st0"), cx.sem("s0_st1")]
    Wq, Wk, Wv = (cx.wA[:, i] for i in range(3))
    v_dram = st["v_dram"].rearrange("(n p) c -> p n c", p=P)
    s_dram = st["s_dram"].rearrange("(n p c) h -> p n c h", n=NT, p=P)
    ps = cx.ps
    block = tmp.enter_context(nc.Block())

    @block.sync
    def _(sp):
        for i, name in enumerate(("L0_gnn_ln1_g", "L0_gnn_ln1_b", "L0_gnn_bq", "L0_gnn_bk")):
            sp.dma_start(cols[:, i, :], col(io[name], CT), allow_slow_non_contiguous=True).then_inc(s_small, 16)
        sp.dma_start(bv[:], row_b(io["L0_gnn_bv"])).then_inc(s_small, 16)
        sp.wait_ge(s_v, NT)
        sp.dma_start(v_dram, v[:]).then_inc(s_vout, 16)
        for n in range(NT):
            sp.wait_ge(s_ev[0], (n + 1) * H0 // 2)
            sp.wait_ge(s_ev[1], (n + 1) * H0 // 2)
            sp.dma_start(s_dram[:, n], stage[:, n % 2]).then_inc(s_st[n % 2], 16)
        for s in s_st:
            sp.wait_ge(s, 16 * NT // 2)
        sp.wait_ge(s_vout, 16)

    @block.vector
    def _(dve):
        dve.wait_ge(st["s_x0"], 16)
        dve.sem_inc(s_x, NT)
        norm_vector(dve, norm, cx.x, z, s_x)
        dve.wait_ge(s_small, 80)
        for c in range(1, CT, 2):
            dve.wait_ge(s_tr, c + 1)
            dve.tensor_scalar(cx.xT[:, c, :], ps[:, c, :], cols[:, 0, c:c + 1], cols[:, 1, c:c + 1],
                              ALU.mult, ALU.add).then_inc(s_zT, 1)
        for n in range(NT):
            dve.wait_ge(s_vmm, n + 1)
            dve.tensor_tensor(v[:, n, :], ps[:, 4 + n, :], bv[:], ALU.add).then_inc(s_v, 1)
        for i in range(1, 2 * CT, 2):
            c, out = i % CT, (qT, kT)[i // CT]
            dve.wait_ge(s_qk, i + 1)
            dve.tensor_scalar(out[:, c, :], ps[:, i, :], cols[:, 2 + i // CT, c:c + 1], None,
                              ALU.add).then_inc(s_qk_out, 1)
        for u in range(1, NT * H0, 2):
            n, h = u // H0, u % H0
            dve.wait_ge(s_smm, u + 1)
            if n >= 2 and h == 1:
                dve.wait_ge(s_st[n % 2], 16)
            dve.tensor_scalar(stage[:, n % 2, :, h], ps[:, u % 8, :], 0.125, None, ALU.mult).then_inc(s_ev[1], 1)

    @block.scalar
    def _(act):
        def row_of_src(groups):
            for g in groups:
                act.wait_ge(s_spread, g + 1)
                act.activation(st["src_row"][:, g * N:(g + 1) * N], ps[:, 4 + g % 4, :], ACT.Copy
                               ).then_inc(s_row, 1)

        row_of_src(range(4))
        norm_scalar(act, norm)
        row_of_src(range(4, ET // 4))
        act.wait_ge(s_small, 80)
        for c in range(0, CT, 2):
            act.wait_ge(s_tr, c + 1)
            act.activation(cx.xT[:, c, :], ps[:, c, :], ACT.Identity, bias=cols[:, 1, c:c + 1],
                           scale=cols[:, 0, c:c + 1]).then_inc(s_zT, 1)
        for i in range(0, 2 * CT, 2):
            c, out = i % CT, (qT, kT)[i // CT]
            act.wait_ge(s_qk, i + 1)
            act.activation(out[:, c, :], ps[:, i, :], ACT.Identity,
                           bias=cols[:, 2 + i // CT, c:c + 1]).then_inc(s_qk_out, 1)
        for u in range(0, NT * H0, 2):
            n, h = u // H0, u % H0
            act.wait_ge(s_smm, u + 1)
            if n >= 2 and h == 0:
                act.wait_ge(s_st[n % 2], 16)
            act.activation(stage[:, n % 2, :, h], ps[:, u % 8, :], ACT.Copy, scale=0.125).then_inc(s_ev[0], 1)

    @block.tensor
    def _(pe):
        for g in range(ET // 4):
            if g >= 4:
                pe.wait_ge(s_row, g - 3)
            for u in range(4):
                m = pe.matmul(ps[:, 4 + g % 4, u * P:(u + 1) * P],
                              cx.src_f[:, 4 * g + u:4 * g + u + 1].to_broadcast([P, P]), cx.ident[:],
                              start=True, stop=True)
            m.then_inc(s_spread, 1)
        transposes(pe, cx, z, CT, norm.s_out, s_tr)
        pe.wait_ge(s_row, ET // 4)
        pe.wait_ge(s_zT, CT)
        pe.wait_ge(st["s_w0"], 16 * 4)
        for n in range(NT):
            product(pe, ps[:, 4 + n, :], [(cx.xT[:, k, n * P:(n + 1) * P], Wv[:, k, :]) for k in range(CT)]
                    ).then_inc(s_vmm, 1)
        for i in range(2 * CT):
            c, w = i % CT, (Wq, Wk)[i // CT]
            if i >= CT:
                pe.wait_ge(s_v, i - CT + 1)
            product(pe, ps[:, i, :], [(w[:, k, c * P:(c + 1) * P], cx.xT[:, k, :]) for k in range(CT)]
                    ).then_inc(s_qk, 1)
        pe.wait_ge(s_qk_out, 2 * CT)
        for u in range(NT * H0):
            n, h = u // H0, u % H0
            lo = D0 * (h % 2)
            if u >= 8:
                pe.wait_ge(s_ev[u % 2], (u - 8) // 2 + 1)
            pe.matmul(ps[:, u % 8, :], qT[lo:lo + D0, h // 2, n * P:(n + 1) * P], kT[lo:lo + D0, h // 2, :],
                      start=True, stop=True).then_inc(s_smm, 1)

    tmp.close()
    cx.end_phase()


def attention_edges(cx, st):
    nc, io = cx.nc, cx.io
    tmp = ExitStack()
    R, G, M = 4, 8, GUARD_M
    sg = st["sg"]
    bias = cx.sb("bias", [P, ET, H0], F32, tmp)
    s = cx.sb("s", [P, ET, H0], F32, tmp)
    diff = cx.sb("diff", [P, ET, H0], F32, tmp)
    diff2 = cx.sb("diff2", [P, ET, H0], F32, tmp)
    p = cx.sb("p", [P, ET, H0], F32, tmp)
    p_hl = cx.sb("p_hl", [P, ET, 2, H0], F32R, tmp)
    p_ring = cx.sb("p_ring", [P, R, 2 * H0], F32R, tmp)
    pmax = cx.sb("pmax", [P, H0], F32, tmp)
    gcol = cx.sb("gcol", [H0, 1], F32, tmp)
    top = cx.sb("top", [P, H0], F32, tmp)
    small = [P, NT, M, H0]
    total = cx.sb("total", small, F32, tmp)
    expo = cx.sb("expo", small, I32, tmp)
    cand = cx.sb("cand", small, F32, tmp)
    cand2 = cx.sb("cand2", small, F32, tmp)
    cand3 = cx.sb("cand3", small, F32, tmp)
    empty = cx.sb("empty", [P, NT, M, H0], F32, tmp)
    best = cx.sb("best", [P, NT, H0], F32, tmp)
    bound = cx.sb("bound", [P, NT, H0], F32, tmp)
    bound_hl = cx.sb("bound_hl", [P, NT, 2, H0], BF16, tmp)
    edge_bound = cx.sb("edge_bound", [P, ET, 2, H0], F32, tmp)
    guard = ExitStack()
    w = cx.sb("w", [P, ET, M, H0], BF16, guard)
    oh = cx.sb("oh", [P, R, N], BF16, guard)
    ohT = cx.sb("ohT", [P, 2, NT, R * P], BF16, guard)
    guard.close()
    oh_r = cx.sb("oh_r", [P, R, N], F32R, tmp)
    pv = cx.xT
    pv_hi = cx.sb("pv_hi", [P, R, C], F32R, tmp)
    pv_lo = cx.sb("pv_lo", [P, R, C], F32R, tmp)
    vg = cx.wA[:, 0:2].rearrange("p a k c -> p (a k) c")
    args = [mem.rearrange("p k c -> p (k c)").rearrange("p (m t h) -> p m t h", m=M // 2, h=H0)
            for mem in (cx.xT[:], cx.wA[:, 2])]
    names = ("bias", "s", "pmax", "gT", "gcol", "gb", "top", "diff", "arg", "w", "oh", "oh_free", "sum",
             "total", "expo", "cand", "best", "bound", "hi", "lo", "ohT", "back", "eb", "d2", "d3", "p", "p_hl",
             "ohr", "pv", "pvhi", "pvlo", "used")
    sem = {n: cx.sem("s1_" + n) for n in names}
    s_vg = [cx.sem(f"s1_vg{i}") for i in range(G)]
    ps = cx.ps
    g_psum = ps[0:H0, 0, 0:P]
    gb_psum = ps[:, 0, P:P + H0]
    sum_psum = ps[:, 1, 0:NT * M * H0].rearrange("p (n c) -> p n c", n=NT)
    block = tmp.enter_context(nc.Block())

    @block.sync
    def _(sp):
        sp.dma_start(bias[:], io["edge_attr_8"].rearrange("(p t) h -> p t h", p=P)).then_inc(sem["bias"], 16)

    @block.gpsimd
    def _(pool):
        for t in range(ET):
            if t >= G:
                pool.wait_ge(sem["pv"], t - G + 1)
            pool.indirect_dma_start(vg[:, t % G, :], None, st["v_dram"], Offset(ap=cx.dst_i[:, t:t + 1], axis=0)
                                    ).then_inc(s_vg[t % G], 16)

    @block.vector
    def _(dve):
        dve.wait_ge(sem["bias"], 16)
        dve.wait_ge(st["s_sg"], 16 * ET)
        dve.tensor_tensor(s[:], sg[:], bias[:], ALU.add).then_inc(sem["s"], 1)
        dve.wait_ge(sem["s"], 1)
        dve.tensor_reduce(pmax[:], s[:].rearrange("p t h -> p h t"), AX.X, ALU.max).then_inc(sem["pmax"], 1)
        dve.wait_ge(sem["gT"], 1)
        dve.tensor_reduce(gcol[:], g_psum, AX.X, ALU.max).then_inc(sem["gcol"], 1)
        dve.wait_ge(sem["gb"], 1)
        dve.tensor_copy(top[:], gb_psum).then_inc(sem["top"], 1)
        dve.wait_ge(sem["top"], 1)
        dve.tensor_tensor(diff[:], s[:], top[:].unsqueeze(1).to_broadcast([P, ET, H0]), ALU.subtract
                          ).then_inc(sem["diff"], 1)
        dve.wait_ge(sem["diff"], 1)
        for m in range(M):
            dve.tensor_scalar(args[m // (M // 2)][:, m % (M // 2)], diff[:], m * GUARD_STEP, GUARD_STEP, ALU.add, ALU.min
                              ).then_inc(sem["arg"], 1)
        with dve.Fori(0, ET // R) as i:
            for u in range(R):
                dve.wait_ge(sem["oh_free"], i * R + (u + 1))
                dve.tensor_scalar(oh[:, u, :], cx.iota_h[:], cx.src_f[:, bass.ds(i * R + u, 1)], None,
                                  ALU.is_equal).then_inc(sem["oh"], 1)
        dve.wait_ge(sem["sum"], 1)
        dve.tensor_copy(total[:].rearrange("p n m h -> p n (m h)"), sum_psum).then_inc(sem["total"], 1)
        dve.wait_ge(sem["total"], 1)
        dve.tensor_scalar(expo[:], total[:].bitcast(I32), 23, None, ALU.logical_shift_right
                          ).then_inc(sem["expo"], 1)
        dve.wait_ge(sem["expo"], 1)
        dve.tensor_scalar(cand[:], expo[:], -126.0, GUARD_T * LN2, ALU.add, ALU.mult).then_inc(sem["cand"], 1)
        dve.tensor_scalar(empty[:], expo[:], 0.5, -1e30, ALU.is_lt, ALU.mult).then_inc(sem["cand"], 1)
        dve.wait_ge(sem["cand"], 2)
        for m in range(M):
            dve.tensor_scalar(cand2[:, :, m, :], cand[:, :, m, :], -m * GUARD_STEP - GUARD_MARGIN, None, ALU.add
                              ).then_inc(sem["cand"], 1)
        dve.wait_ge(sem["cand"], M + 2)
        dve.tensor_tensor(cand3[:, :, 0:M - 1, :], cand2[:, :, 0:M - 1, :], empty[:, :, 0:M - 1, :], ALU.add
                          ).then_inc(sem["cand"], 1)
        dve.tensor_copy(cand3[:, :, M - 1, :], cand2[:, :, M - 1, :]).then_inc(sem["cand"], 1)
        dve.wait_ge(sem["cand"], M + 4)
        dve.tensor_reduce(best[:], cand3[:].rearrange("p n m h -> p n h m"), AX.X, ALU.max).then_inc(sem["best"], 1)
        dve.wait_ge(sem["best"], 1)
        dve.tensor_tensor(bound[:], best[:], top[:].unsqueeze(1).to_broadcast([P, NT, H0]), ALU.add
                          ).then_inc(sem["bound"], 1)
        dve.wait_ge(sem["bound"], 1)
        dve.tensor_copy(bound_hl[:, :, 0, :], bound[:]).then_inc(sem["hi"], 1)
        dve.wait_ge(sem["hi"], 1)
        dve.tensor_tensor(bound_hl[:, :, 1, :], bound[:], bound_hl[:, :, 0, :], ALU.subtract
                          ).then_inc(sem["lo"], 1)
        with dve.Fori(0, ET // R // 2) as i:
            for u in range(2):
                dve.wait_ge(sem["back"], i * 2 + (u + 1))
                for n in range(NT):
                    dve.tensor_scalar(ohT[:, u, n, :],
                                      st["src_row"][:, bass.ds(i * (2 * R * P) + u * R * P, R * P)],
                                      cx.part_f[:, n:n + 1], None, ALU.is_equal).then_inc(sem["ohT"], 1)
        dve.wait_ge(sem["eb"], ET // R + 2)
        dve.tensor_tensor(diff2[:], s[:], edge_bound[:, :, 0, :], ALU.subtract).then_inc(sem["d2"], 1)
        dve.wait_ge(sem["d2"], 1)
        dve.tensor_tensor(diff[:], diff2[:], edge_bound[:, :, 1, :], ALU.subtract).then_inc(sem["d3"], 1)
        dve.wait_ge(sem["p"], 1)
        dve.tensor_copy(p_hl[:, :, 0, :], p[:]).then_inc(sem["p_hl"], 1)
        dve.wait_ge(sem["p_hl"], 1)
        dve.tensor_tensor(p_hl[:, :, 1, :], p[:], p_hl[:, :, 0, :].bitcast(F32), ALU.subtract
                          ).then_inc(sem["p_hl"], 1)

        def low_part(i, u):
            dve.wait_ge(sem["pvhi"], i * G + (u + 1))
            dve.tensor_tensor(pv_lo[:, u % R, :], pv[:, u % R, :], pv_hi[:, u % R, :].bitcast(F32),
                              ALU.subtract).then_inc(sem["pvlo"], 1)

        with dve.Fori(0, ET // G) as i:
            for u in range(G):
                dve.wait_ge(sem["used"], i * G + (u + 1))
                dve.tensor_scalar(oh_r[:, u % R, :], cx.iota_h[:], cx.src_f[:, bass.ds(i * G + u, 1)], None,
                                  ALU.is_equal).then_inc(sem["ohr"], 1)
                dve.wait_ge(s_vg[u], i * 16 + 16)
                dve.tensor_tensor(pv[:, u % R, :].rearrange("p (h d) -> p h d", h=H0),
                                  vg[:, u, :].rearrange("p (h d) -> p h d", h=H0),
                                  p[:, bass.ds(i * G + u, 1), :].rearrange("p o h -> p h o").to_broadcast([P, H0, D0]),
                                  ALU.mult).then_inc(sem["pv"], 1)
                if u:
                    low_part(i, u - 1)
            low_part(i, G - 1)

    @block.scalar
    def _(act):
        for half in range(2):
            act.wait_ge(sem["arg"], M // 2 * (half + 1))
            ms = slice(half * M // 2, (half + 1) * M // 2)
            act.activation(w[:, :, ms, :].rearrange("p t m h -> p m t h"), args[half], ACT.Exp,
                           scale=1.0 / GUARD_T).then_inc(sem["w"], 1)
        with act.Fori(0, ET // R // 2) as i:
            for u in range(2):
                act.wait_ge(sem["back"], i * 2 + (u + 3))
                act.activation(edge_bound[:, bass.ds(i * (2 * R) + u * R, R)].rearrange("p t k h -> p (t k h)"),
                               ps[:, 2 + u, 0:R * 2 * H0], ACT.Copy).then_inc(sem["eb"], 1)
        act.wait_ge(sem["d3"], 1)
        act.activation(p[:], diff[:], ACT.Exp).then_inc(sem["p"], 1)
        act.wait_ge(sem["p_hl"], 2)
        with act.Fori(0, ET // R) as i:
            for u in range(R):
                act.wait_ge(sem["used"], i * R + (u + 1))
                act.activation(p_ring[:, u, :],
                               p_hl[:, bass.ds(i * R + u, 1)].rearrange("p o k h -> p (o k h)"), ACT.Copy)
                act.wait_ge(sem["pv"], i * R + (u + 1))
                act.activation(pv_hi[:, u, :], pv[:, u, :], ACT.Copy).then_inc(sem["pvhi"], 1)

    @block.tensor
    def _(pe):
        pe.wait_ge(sem["pmax"], 1)
        pe.transpose(g_psum, pmax[:], cx.ident[:]).then_inc(sem["gT"], 1)
        pe.wait_ge(sem["gcol"], 1)
        pe.matmul(gb_psum, gcol[:].to_broadcast([H0, P]), cx.ident[0:H0, 0:H0], start=True, stop=True
                  ).then_inc(sem["gb"], 1)
        pe.matmul(ps[:, 1, :], cx.zero_r[:, 0:P], cx.zero_r[:], start=True, stop=False)
        pe.sem_inc(sem["oh_free"], R)
        pe.wait_ge(sem["w"], 2)
        with pe.Fori(0, ET // R) as i:
            for u in range(R):
                pe.wait_ge(sem["oh"], i * R + (u + 1))
                for n in range(NT):
                    m = pe.matmul(sum_psum[:, n, :], oh[:, u, n * P:(n + 1) * P],
                                  w[:, bass.ds(i * R + u, 1)].rearrange("p o m h -> p (o m h)"),
                                  start=False, stop=False)
                m.then_inc(sem["oh_free"], 1)
        pe.matmul(ps[:, 1, :], cx.zero_r[:, 0:P], cx.zero_r[:], start=False, stop=True
                  ).then_inc(sem["sum"], 1)
        pe.sem_inc(sem["back"], 2)
        pe.sem_inc(sem["eb"], 2)
        pe.wait_ge(sem["lo"], 1)
        with pe.Fori(0, ET // R // 2) as i:
            for u in range(2):
                pe.wait_ge(sem["eb"], i * 2 + (u + 1))
                pe.wait_ge(sem["ohT"], i * (2 * NT) + (u + 1) * NT)
                for t in range(R):
                    for n in range(NT):
                        m = pe.matmul(ps[:, 2 + u, t * 2 * H0:(t + 1) * 2 * H0], ohT[:, u, n, t * P:(t + 1) * P],
                                      bound_hl[:, n].rearrange("p k h -> p (k h)"),
                                      start=(n == 0), stop=(n == NT - 1))
                m.then_inc(sem["back"], 1)
        banks = [0] + [4 + n for n in range(NT)]
        for b in banks:
            pe.matmul(ps[:, b, :], cx.zero_r[:, 0:P], cx.zero_r[:], start=True, stop=False)
        pe.sem_inc(sem["used"], R)
        with pe.Fori(0, ET // R) as i:
            for u in range(R):
                pe.wait_ge(sem["ohr"], i * R + (u + 1))
                pe.wait_ge(sem["pvhi"], i * R + (u + 1))
                for n in range(NT):
                    one = oh_r[:, u, n * P:(n + 1) * P]
                    pe.matmul(ps[:, 0, n * 16:(n + 1) * 16], one, p_ring[:, u, :], start=False, stop=False)
                    pe.matmul(ps[:, 4 + n, :], one, pv_hi[:, u, :], start=False, stop=False)
                pe.wait_ge(sem["pvlo"], i * R + (u + 1))
                for n in range(NT):
                    m = pe.matmul(ps[:, 4 + n, :], oh_r[:, u, n * P:(n + 1) * P], pv_lo[:, u, :],
                                  start=False, stop=False)
                m.then_inc(sem["used"], 1)
        for b in banks:
            pe.matmul(ps[:, b, :], cx.zero_r[:, 0:P], cx.zero_r[:], start=False, stop=True)

    tmp.close()
    cx.end_phase()


def gat1_weights(cx):
    return cx.wA[:, 0:2].rearrange("p a k n -> p (a k n)").rearrange("p (k n) -> p k n", k=CT)


def attention_out(cx, st):
    nc, io = cx.nc, cx.io
    tmp = ExitStack()
    den2 = cx.sb("den2", [P, NT, 2, H0], F32, tmp)
    den = cx.sb("den", [P, NT, H0], F32, tmp)
    rden = cx.sb("rden", [P, NT, H0], F32, tmp)
    att = cx.sb("att", [P, NT, C], F32, tmp)
    attT = cx.sb("attT", [P, CT, N], F32, tmp)
    x1 = cx.sb("x1", [P, NT, C], F32, tmp)
    xb = cx.sb("xb", [P, NT, C], F32, tmp)
    z = cx.sb("z1", [P, NT, C], F32, tmp)
    zT = cx.sb("z1T", [P, CT, N], F32, tmp)
    hT = cx.sb("h0T", [P, HT, N], F32, tmp)
    bo = cx.sb("bo_b", [P, C], F32, tmp)
    b2 = cx.sb("b20_b", [P, C], F32, tmp)
    cols = cx.sb("cols1", [P, 2, CT], F32, tmp)
    b1 = cx.sb("b10", [P, HT], F32, tmp)
    n1, n2 = Norm(cx, "n1", tmp), Norm(cx, "n2", tmp)
    names = ("small", "den2", "den", "denm", "rden", "xb", "att", "tr", "attT", "wo", "x1", "tr2", "zT",
             "h", "hT", "ff", "xb2", "y")
    sem = {n: cx.sem("s2_" + n) for n in names}
    W1 = cx.wB[:, 0:CT * HID].rearrange("p (k n) -> p k n", k=CT)
    W2 = cx.wB[:, CT * HID:].rearrange("p (k n) -> p k n", k=HT)
    ps = cx.ps
    block = tmp.enter_context(nc.Block())

    @block.sync
    def _(sp):
        sp.dma_start(gat1_weights(cx), rows(io["L1_gnn_W1"])).then_inc(st["s_w2"], 16)
        sp.dma_start(bo[:], row_b(io["L0_gnn_bo"])).then_inc(sem["small"], 16)
        sp.dma_start(b2[:], row_b(io["L0_gnn_b2"])).then_inc(sem["small"], 16)
        sp.dma_start(cols[:, 0, :], col(io["L0_gnn_ln2_g"], CT), allow_slow_non_contiguous=True).then_inc(sem["small"], 16)
        sp.dma_start(cols[:, 1, :], col(io["L0_gnn_ln2_b"], CT), allow_slow_non_contiguous=True).then_inc(sem["small"], 16)
        sp.dma_start(b1[:], col(io["L0_gnn_b1"], HT), allow_slow_non_contiguous=True).then_inc(sem["small"], 16)

    @block.vector
    def _(dve):
        dve.tensor_copy(den2[:].rearrange("p n k h -> p (n k h)"), ps[:, 0, 0:NT * 16]).then_inc(sem["den2"], 1)
        dve.wait_ge(sem["den2"], 1)
        dve.tensor_tensor(den[:], den2[:, :, 0, :], den2[:, :, 1, :], ALU.add).then_inc(sem["den"], 1)
        dve.wait_ge(sem["den"], 1)
        dve.tensor_scalar(rden[:], den[:], 1e-37, None, ALU.max).then_inc(sem["denm"], 1)
        dve.wait_ge(sem["denm"], 1)
        dve.reciprocal(den[:], rden[:]).then_inc(sem["rden"], 1)
        dve.wait_ge(sem["rden"], 1)
        for n in range(NT):
            dve.tensor_tensor(att[:, n, :].rearrange("p (h d) -> p h d", h=H0),
                              ps[:, 4 + n, :].rearrange("p (h d) -> p h d", h=H0),
                              den[:, n, :].unsqueeze(2).to_broadcast([P, H0, D0]), ALU.mult).then_inc(sem["att"], 1)
        dve.wait_ge(sem["small"], 80)
        for n in range(NT):
            dve.tensor_tensor(xb[:, n, :], cx.x[:, n, :], bo[:], ALU.add).then_inc(sem["xb"], 1)
        for c in range(1, CT, 2):
            dve.wait_ge(sem["tr"], c + 1)
            dve.tensor_copy(attT[:, c, :], ps[:, c, :]).then_inc(sem["attT"], 1)
        dve.wait_ge(sem["xb"], NT)
        for n in range(NT):
            dve.wait_ge(sem["wo"], n + 1)
            dve.tensor_tensor(x1[:, n, :], ps[:, 4 + n, :], xb[:, n, :], ALU.add).then_inc(sem["x1"], 1)
        norm_vector(dve, n1, x1, z, sem["x1"])
        for c in range(1, CT, 2):
            dve.wait_ge(sem["tr2"], c + 1)
            dve.tensor_scalar(zT[:, c, :], ps[:, c, :], cols[:, 0, c:c + 1], cols[:, 1, c:c + 1],
                              ALU.mult, ALU.add).then_inc(sem["zT"], 1)
        for n in range(NT):
            dve.scalar_tensor_tensor(out=xb[:, n, :], in0=cx.x[:, n, :], scalar=1.0, in1=x1[:, n, :],
                                     op0=ALU.mult, op1=ALU.add).then_inc(sem["xb2"], 1)
        dve.wait_ge(sem["xb2"], NT)
        for n in range(NT):
            dve.tensor_tensor(att[:, n, :], xb[:, n, :], b2[:], ALU.add).then_inc(sem["xb2"], 1)
        dve.wait_ge(sem["xb2"], 2 * NT)
        for n in range(NT):
            dve.wait_ge(sem["ff"], n + 1)
            dve.tensor_tensor(x1[:, n, :], ps[:, 4 + n, :], att[:, n, :], ALU.add).then_inc(sem["y"], 1)
        norm_vector(dve, n2, x1, cx.x, sem["y"])

    @block.scalar
    def _(act):
        for c in range(0, CT, 2):
            act.wait_ge(sem["tr"], c + 1)
            act.activation(attT[:, c, :], ps[:, c, :], ACT.Copy).then_inc(sem["attT"], 1)
        norm_scalar(act, n1)
        act.wait_ge(sem["small"], 80)
        for c in range(0, CT, 2):
            act.wait_ge(sem["tr2"], c + 1)
            act.activation(zT[:, c, :], ps[:, c, :], ACT.Identity, bias=cols[:, 1, c:c + 1],
                           scale=cols[:, 0, c:c + 1]).then_inc(sem["zT"], 1)
        for m in range(HT):
            act.wait_ge(sem["h"], m + 1)
            act.activation(hT[:, m, :], ps[:, (4 + m) % 8, :], ACT.Silu, bias=b1[:, m:m + 1]).then_inc(sem["hT"], 1)
        norm_scalar(act, n2)

    @block.tensor
    def _(pe):
        transposes(pe, cx, att, CT, sem["att"], sem["tr"])
        pe.wait_ge(sem["attT"], CT)
        for n in range(NT):
            product(pe, ps[:, 4 + n, :], [(attT[:, k, n * P:(n + 1) * P], cx.wA[:, 3, k, :]) for k in range(CT)]
                    ).then_inc(sem["wo"], 1)
        transposes(pe, cx, z, CT, n1.s_out, sem["tr2"])
        pe.wait_ge(sem["zT"], CT)
        pe.wait_ge(st["s_w1"], 32)
        for m in range(HT):
            product(pe, ps[:, (4 + m) % 8, :], [(W1[:, k, m * P:(m + 1) * P], zT[:, k, :]) for k in range(CT)]
                    ).then_inc(sem["h"], 1)
        pe.wait_ge(sem["hT"], HT)
        for n in range(NT):
            product(pe, ps[:, 4 + n, :], [(hT[:, k, n * P:(n + 1) * P], W2[:, k, :]) for k in range(HT)]
                    ).then_inc(sem["ff"], 1)

    tmp.close()
    cx.end_phase()


def edge_sums(cx, st):
    nc, io = cx.nc, cx.io
    tmp = ExitStack()
    R = 4
    ea = cx.sb("ea", [P, ET, EA], F32, tmp)
    ea_hl = cx.sb("ea_hl", [P, R, 2, EA], F32R, tmp)
    oh_s = cx.sb("oh_s", [P, R, N], F32R, tmp)
    oh_d = cx.sb("oh_d", [P, R, N], F32R, tmp)
    ident_b = cx.sb("ident_b", [P, P], BF16, tmp)
    ones = cx.sb("ones_b", [P, P], F32, tmp)
    count = cx.sb("count", [P, N], F32, tmp)
    names = ("ea", "const", "hi", "lo", "ohs", "ohd", "used", "tr", "eaT", "mm", "cnt", "trc", "deg",
             "c1")
    sem = {n: cx.sem("s3_" + n) for n in names}
    ps = cx.ps
    block = tmp.enter_context(nc.Block())

    @block.sync
    def _(sp):
        sp.dma_start(ea[:], io["edge_attr_64"].rearrange("(p t) f -> p t f", p=P)).then_inc(sem["ea"], 16)
        sp.dma_start(cx.wB[:, 0:CT * HID].rearrange("p (k n) -> p k n", k=CT), rows(io["L0_gnn_W1"])
                     ).then_inc(st["s_w1"], 16)
        sp.dma_start(cx.wB[:, CT * HID:].rearrange("p (k n) -> p k n", k=HT), rows(io["L0_gnn_W2"])
                     ).then_inc(st["s_w1"], 16)

    @block.gpsimd
    def _(pool):
        for t in range(ET):
            pool.indirect_dma_start(st["sg"][:, t, :], None, st["s_dram"],
                                    Offset(ap=st["pair_i"][:, t:t + 1], axis=0)).then_inc(st["s_sg"], 16)

    @block.vector
    def _(dve):
        dve.tensor_copy(ident_b[:], cx.ident[:]).then_inc(sem["const"], 1)
        dve.memset(ones[:], 1.0).then_inc(sem["const"], 1)
        dve.wait_ge(sem["ea"], 16)
        with dve.Fori(0, ET // R) as i:
            for u in range(R):
                t = i * R + u
                dve.wait_ge(sem["used"], i * R + (u + 1))
                for oh, nodes, done in ((oh_d, cx.dst_f, "ohd"), (oh_s, cx.src_f, "ohs")):
                    dve.tensor_scalar(oh[:, u, :], cx.iota_h[:], nodes[:, bass.ds(t, 1)], None,
                                      ALU.is_equal).then_inc(sem[done], 1)
                dve.wait_ge(sem["hi"], i * R + (u + 1))
                dve.tensor_tensor(ea_hl[:, u, 1, :], ea[:, bass.ds(t, 1), :].rearrange("p o f -> p (o f)"),
                                  ea_hl[:, u, 0, :].bitcast(F32), ALU.subtract).then_inc(sem["lo"], 1)
        dve.wait_ge(sem["mm"], 1)
        for n in range(NT):
            dve.tensor_copy(cx.cnt[:, n, :], ps[:, n, :]).then_inc(sem["cnt"], 1)
        dve.wait_ge(sem["deg"], 1)
        dve.tensor_scalar(count[:], ps[:, 5, :], -1.0, 1.0, ALU.add, ALU.max).then_inc(sem["c1"], 1)
        dve.wait_ge(sem["c1"], 1)
        dve.reciprocal(cx.rcount[:], count[:]).then_inc(sem["c1"], 1)
        dve.wait_ge(sem["c1"], 2)
        dve.tensor_tensor(cx.ea_mean[:], ps[:, 4, :], cx.rcount[:], ALU.mult)
        for n in range(NT):
            dve.wait_ge(sem["trc"], n + 1)
            dve.tensor_scalar(cx.pen[:, n, :], ps[:, n, :], 0.0, -BIG, ALU.is_equal, ALU.mult)

    @block.scalar
    def _(act):
        def transposed(i, u):
            act.wait_ge(sem["tr"], i * R + (u + 1))
            act.activation(cx.eaT[:, bass.ds(i * (R * P) + u * P, P)], ps[:, 5 + u % 2, 0:P], ACT.Copy
                           ).then_inc(sem["eaT"], 1)

        act.wait_ge(sem["ea"], 16)
        with act.Fori(0, ET // R) as i:
            for u in range(R):
                act.wait_ge(sem["used"], i * R + (u + 1))
                act.activation(ea_hl[:, u, 0, :], ea[:, bass.ds(i * R + u, 1), :].rearrange("p o f -> p (o f)"),
                               ACT.Copy).then_inc(sem["hi"], 1)
                if u >= 1:
                    transposed(i, u - 1)
            transposed(i, R - 1)

    @block.tensor
    def _(pe):
        for b in range(NT + 1):
            pe.matmul(ps[:, b, :], cx.zero_r[:, 0:P], cx.zero_r[:], start=True, stop=False)
        pe.sem_inc(sem["eaT"], 2)
        pe.sem_inc(sem["used"], R)
        with pe.Fori(0, ET // R) as i:
            for u in range(R):
                pe.wait_ge(sem["lo"], i * R + (u + 1))
                pe.wait_ge(sem["eaT"], i * R + (u + 1))
                pe.transpose(ps[:, 5 + u % 2, 0:P], ea_hl[:, u].rearrange("p k f -> p (k f)").bitcast(F32),
                             cx.ident[:]).then_inc(sem["tr"], 1)
                pe.matmul(ps[:, 4, :], ea_hl[:, u].rearrange("p k f -> p (k f)"), oh_d[:, u, :],
                          start=False, stop=False)
                for n in range(NT):
                    m = pe.matmul(ps[:, n, :], oh_s[:, u, n * P:(n + 1) * P], oh_d[:, u, :],
                                  start=False, stop=False)
                m.then_inc(sem["used"], 1)
        pe.wait_ge(sem["const"], 2)
        for n in range(NT):
            pe.matmul(ps[:, n, n * P:(n + 1) * P], ident_b[:], ident_b[:], start=False, stop=False)
        for b in range(NT + 1):
            m = pe.matmul(ps[:, b, :], cx.zero_r[:, 0:P], cx.zero_r[:], start=False, stop=True)
        m.then_inc(sem["mm"], 1)
        pe.wait_ge(sem["cnt"], NT)
        pe.wait_ge(sem["eaT"], ET + 2)
        product(pe, ps[:, 5, :], [(ones[:], cx.cnt[:, k, :]) for k in range(NT)]).then_inc(sem["deg"], 1)
        transposes(pe, cx, cx.cnt, NT, None, sem["trc"])

    tmp.close()
    cx.end_phase()


W_ = C1 + 4


def gat_output(h_mem):
    return h_mem[:, 0:HT * N].rearrange("p (k n) -> p k n", k=HT)


def gat(cx, st, tag, W, kt, xT, h_mem, a_src, a_dst, b, s_w, w_count, x_in):
    nc, io = cx.nc, cx.io
    tmp = ExitStack()
    h = h_mem[:].rearrange("p (n q c) -> p n q c", n=NT, q=H1)
    outT = gat_output(h_mem)
    o = W.rearrange("p k n -> p (k n)")[:, 0:NT * HID].rearrange("p (n c) -> p n c", n=NT)
    b_b = cx.sb(tag + "b_b", [P, HID], F32, tmp)
    al = cx.sb(tag + "al", [P, NT, 2, H1], F32, tmp)
    als2 = cx.sb(tag + "als2", [P, NT, H1], F32, tmp)
    junk = cx.sb(tag + "junk", [P, N], F32, tmp)
    mx = cx.sb(tag + "mx", [P, NT, H1], F32, tmp)
    zmax = cx.sb(tag + "zmax", [P, NT, H1], F32, tmp)
    emax = cx.sb(tag + "emax", [P, NT, H1], F32, tmp)
    dd = cx.sb(tag + "dd", [P, 2, NT, H1], F32, tmp)
    ex = cx.sb(tag + "ex", [P, 2, 2, N], F32, tmp)
    pm = cx.sb(tag + "pm", [P, 2, N], F32, tmp)
    pr = cx.sb(tag + "pr", [P, 2, NT, N], F32, tmp)
    a_b = pr[:, 1].rearrange("p (a k) c -> p a (k c)", a=2)
    rd = cx.sb(tag + "rd", [P, NT * H1], F32, tmp)
    names = ("small", "ones", "tr", "xT", "mm", "h", "al", "als2", "asb", "mx", "z", "emax", "dd", "db",
             "ex1", "ex2", "pm", "p", "agg", "rd", "o", "tr2", "oT")
    sem = {n: cx.sem(tag + "_" + n) for n in names}
    ps = cx.ps
    block = tmp.enter_context(nc.Block())

    @block.sync
    def _(sp):
        sp.dma_start(a_b[:, 0, :], row_b(a_src.rearrange("h c -> (h c)"))).then_inc(sem["small"], 16)
        sp.dma_start(a_b[:, 1, :], row_b(a_dst.rearrange("h c -> (h c)"))).then_inc(sem["small"], 16)
        sp.dma_start(b_b[:], row_b(b)).then_inc(sem["small"], 16)
        if x_in is not None:
            sp.dma_start(cx.wB[:].rearrange("p (k n) -> p k n", k=HT), rows(io["L1_gnn_W2"])
                         ).then_inc(st["s_w3"], 16)
            sp.dma_start(cx.wA[:, 2:4].rearrange("p a k n -> p (a k) n"), rows(io["L1_gnn_Wfc"])
                         ).then_inc(st["s_w4"], 16)

    @block.vector
    def _(dve):
        dve.memset(h[:, :, :, C1:W_], 1.0).then_inc(sem["ones"], 1)
        if x_in is not None:
            for c in range(kt):
                dve.wait_ge(sem["tr"], c + 1)
                dve.tensor_copy(xT[:, c, :], ps[:, c, :]).then_inc(sem["xT"], 1)
        dve.wait_ge(sem["small"], 48)
        for n in range(NT):
            for q in range(H1):
                if q % 2 == 0:
                    dve.wait_ge(sem["h"], n * 2 + q // 2 + 1)
                for k in range(2):
                    if n + q + k:
                        dve.wait_ge(sem["al"], (n * H1 + q) * 2 + k)
                    dve.tensor_tensor_reduce(out=junk[:, 0:C1], in0=h[:, n, q, 0:C1],
                                             in1=a_b[:, k, q * C1:(q + 1) * C1], scale=1.0, scalar=0.0,
                                             op0=ALU.mult, op1=ALU.add, accum_out=al[:, n, k, q:q + 1]
                                             ).then_inc(sem["al"], 1)
        dve.wait_ge(sem["al"], 2 * NT * H1)
        dve.tensor_scalar(als2[:], al[:, :, 0, :], 0.2, None, ALU.mult).then_inc(sem["als2"], 1)
        for n in range(NT):
            for q in range(H1):
                i = n * H1 + q
                dve.wait_ge(sem["asb"], q + 1)
                if i:
                    dve.wait_ge(sem["mx"], i)
                dve.tensor_tensor_reduce(out=junk[:], in0=cx.pen[:, n, :], in1=ps[:, q, :], scale=1.0,
                                         scalar=-BIG, op0=ALU.add, op1=ALU.max,
                                         accum_out=mx[:, n, q:q + 1]).then_inc(sem["mx"], 1)
        dve.wait_ge(sem["mx"], NT * H1)
        dve.tensor_tensor(zmax[:], mx[:], al[:, :, 1, :], ALU.add).then_inc(sem["z"], 1)
        dve.wait_ge(sem["z"], 1)
        dve.scalar_tensor_tensor(out=emax[:], in0=zmax[:], scalar=0.2, in1=zmax[:], op0=ALU.mult, op1=ALU.max
                                 ).then_inc(sem["emax"], 1)
        dve.wait_ge(sem["emax"], 1)
        dve.tensor_tensor(dd[:, 0], al[:, :, 1, :], emax[:], ALU.subtract).then_inc(sem["dd"], 1)
        dve.scalar_tensor_tensor(out=dd[:, 1], in0=al[:, :, 1, :], scalar=0.2, in1=emax[:], op0=ALU.mult,
                                 op1=ALU.subtract).then_inc(sem["dd"], 1)

        def numerators(q, s):
            i = q * NT + s
            dve.wait_ge(sem["ex2"], i + 1)
            if i >= 2:
                dve.wait_ge(sem["p"], i - 1)
            dve.scalar_tensor_tensor(out=pm[:, i % 2, :], in0=ex[:, i % 2, 0, :], scalar=1.0,
                                     in1=ex[:, i % 2, 1, :], op0=ALU.min, op1=ALU.max).then_inc(sem["pm"], 1)
            if q >= 2 and s == 0:
                dve.wait_ge(sem["agg"], NT * (q - 1))
            dve.wait_ge(sem["pm"], i + 1)
            dve.scalar_tensor_tensor(out=pr[:, q % 2, s, :], in0=pm[:, i % 2, :], scalar=1.0,
                                     in1=cx.cnt[:, s, :], op0=ALU.min, op1=ALU.mult).then_inc(sem["p"], 1)

        def outputs(q, n):
            i = q * NT + n
            dve.wait_ge(sem["agg"], i + 1)
            dve.reciprocal(rd[:, i:i + 1], ps[:, n, C1:C1 + 1]).then_inc(sem["rd"], 1)
            dve.wait_ge(sem["rd"], i + 1)
            dve.scalar_tensor_tensor(out=o[:, n, q * C1:(q + 1) * C1], in0=ps[:, n, 0:C1],
                                     scalar=rd[:, i:i + 1], in1=b_b[:, q * C1:(q + 1) * C1], op0=ALU.mult,
                                     op1=ALU.add).then_inc(sem["o"], 1)

        for q in range(H1):
            for s in range(NT):
                numerators(q, s)
            if q:
                for n in range(NT):
                    outputs(q - 1, n)
        for n in range(NT):
            outputs(H1 - 1, n)
        for c in range(1, HT, 2):
            dve.wait_ge(sem["tr2"], c + 1)
            dve.tensor_scalar(outT[:, c, :], ps[:, c, :], 0.0, None, ALU.max).then_inc(sem["oT"], 1)

    @block.scalar
    def _(act):
        for i in range(NT * 2):
            n, half = i // 2, i % 2
            act.wait_ge(sem["mm"], i + 1)
            act.activation(h[:, n, 2 * half:2 * half + 2, 0:C1],
                           ps[:, i % 8, :].rearrange("p (q c) -> p q c", q=2), ACT.Copy).then_inc(sem["h"], 1)
        act.wait_ge(sem["als2"], 1)
        for q in range(H1):
            for s in range(NT):
                i = q * NT + s
                bank = 4 + 2 * (q % 2)
                act.wait_ge(sem["db"], 2 * (q + 1))
                if i >= 2:
                    act.wait_ge(sem["pm"], i - 1)
                act.activation(ex[:, i % 2, 0, :], ps[:, bank, :], ACT.Exp, bias=al[:, s, 0, q:q + 1]
                               ).then_inc(sem["ex1"], 1)
                act.wait_ge(sem["ex1"], i + 1)
                act.activation(ex[:, i % 2, 1, :], ps[:, bank + 1, :], ACT.Exp, bias=als2[:, s, q:q + 1]
                               ).then_inc(sem["ex2"], 1)
        for c in range(0, HT, 2):
            act.wait_ge(sem["tr2"], c + 1)
            act.activation(outT[:, c, :], ps[:, c, :], ACT.Relu).then_inc(sem["oT"], 1)

    @block.tensor
    def _(pe):
        if x_in is not None:
            transposes(pe, cx, x_in, kt, None, sem["tr"])
            pe.wait_ge(sem["xT"], kt)
        pe.wait_ge(s_w, w_count)
        for i in range(NT * 2):
            n, half = i // 2, i % 2
            product(pe, ps[:, i % 8, :], [(xT[:, k, n * P:(n + 1) * P], W[:, k, half * C:(half + 1) * C])
                                          for k in range(kt)]).then_inc(sem["mm"], 1)

        def spread(bank, column, done):
            for n in range(NT):
                m = pe.matmul(ps[:, bank, n * P:(n + 1) * P], column(n).to_broadcast([P, P]), cx.ident[:],
                              start=True, stop=True)
            m.then_inc(done, 1)

        pe.wait_ge(sem["als2"], 1)
        for q in range(H1):
            spread(q, lambda n: al[:, n, 0, q:q + 1], sem["asb"])
        pe.wait_ge(sem["dd"], 2)

        def spread_dst(q):
            if q >= 2:
                pe.wait_ge(sem["ex2"], NT * (q - 1))
            for k in range(2):
                spread(4 + 2 * (q % 2) + k, lambda n: dd[:, k, n, q:q + 1], sem["db"])

        pe.wait_ge(sem["ones"], 1)
        spread_dst(0)
        for q in range(H1):
            if q + 1 < H1:
                spread_dst(q + 1)
            pe.wait_ge(sem["p"], NT * (q + 1))
            for n in range(NT):
                if q:
                    pe.wait_ge(sem["o"], NT * (q - 1) + n + 1)
                product(pe, ps[:, n, 0:C1 + 2],
                        [(pr[:, q % 2, s, n * P:(n + 1) * P], h[:, s, q, 0:C1 + 2]) for s in range(NT)]
                        ).then_inc(sem["agg"], 1)
        pe.wait_ge(sem["o"], NT * H1)
        transposes(pe, cx, o, HT, None, sem["tr2"])

    tmp.close()
    cx.end_phase()


def gat_out(cx, st, hT):
    nc, io = cx.nc, cx.io
    tmp = ExitStack()
    bfc = cx.sb("bfc_b", [P, C], F32, tmp)
    xb = cx.sb("xb1", [P, NT, C], F32, tmp)
    y = cx.sb("y1", [P, NT, C], F32, tmp)
    norm = Norm(cx, "n3", tmp)
    s_small, s_xb, s_mm, s_y = (cx.sem("s5_" + n) for n in ("small", "xb", "mm", "y"))
    Wfc = cx.wA[:, 2:4].rearrange("p a k n -> p (a k) n")
    ps = cx.ps
    block = tmp.enter_context(nc.Block())

    @block.sync
    def _(sp):
        sp.dma_start(bfc[:], row_b(io["L1_gnn_bfc"])).then_inc(s_small, 16)
        sp.dma_start(cx.wB[:, 0:CT * HID].rearrange("p (k n) -> p k n", k=CT), rows(io["L2_gnn_W1"][0:C, :])
                     ).then_inc(st["s_w5"], 16)
        sp.dma_start(cx.wB[:, CT * HID:].rearrange("p (k n) -> p k n", k=HT), rows(io["L2_gnn_W2"])
                     ).then_inc(st["s_w5"], 16)

    @block.vector
    def _(dve):
        dve.wait_ge(s_small, 16)
        for n in range(NT):
            dve.tensor_tensor(xb[:, n, :], cx.x[:, n, :], bfc[:], ALU.add).then_inc(s_xb, 1)
        dve.wait_ge(s_xb, NT)
        for n in range(NT):
            dve.wait_ge(s_mm, n + 1)
            dve.tensor_tensor(y[:, n, :], ps[:, n, :], xb[:, n, :], ALU.add).then_inc(s_y, 1)
        norm_vector(dve, norm, y, cx.x, s_y)

    @block.scalar
    def _(act):
        norm_scalar(act, norm)

    @block.tensor
    def _(pe):
        pe.wait_ge(st["s_w4"], 16)
        for n in range(NT):
            product(pe, ps[:, n, :], [(hT[:, k, n * P:(n + 1) * P], Wfc[:, k, :]) for k in range(HT)]
                    ).then_inc(s_mm, 1)

    tmp.close()
    cx.end_phase()


def residual_layer(cx, st):
    nc, io = cx.nc, cx.io
    tmp = ExitStack()
    W1e = cx.sb("W1e", [P, HID], F32, tmp)
    b1 = cx.sb("b12", [P, HT], F32, tmp)
    b2 = cx.sb("b22_b", [P, C], F32, tmp)
    hT = cx.sb("h2T", [P, HT, N], F32, tmp)
    xb = cx.sb("xb2", [P, NT, C], F32, tmp)
    y = cx.sb("y2", [P, NT, C], F32, tmp)
    norm = Norm(cx, "n4", tmp)
    names = ("small", "w", "tr", "xT", "h", "hT", "xb", "mm", "y")
    sem = {n: cx.sem("s6_" + n) for n in names}
    W1 = cx.wB[:, 0:CT * HID].rearrange("p (k n) -> p k n", k=CT)
    W2 = cx.wB[:, CT * HID:].rearrange("p (k n) -> p k n", k=HT)
    ps = cx.ps
    block = tmp.enter_context(nc.Block())

    @block.sync
    def _(sp):
        for k in range(2):
            sp.dma_start(W1e[k * EA:(k + 1) * EA, :], io["L2_gnn_W1"][C:C + EA, :]).then_inc(sem["w"], 16)
        sp.dma_start(b1[:], col(io["L2_gnn_b1"], HT), allow_slow_non_contiguous=True).then_inc(sem["small"], 16)
        sp.dma_start(b2[:], row_b(io["L2_gnn_b2"])).then_inc(sem["small"], 16)
        sp.dma_start(cx.wA[:].rearrange("p a k n -> p (a k) n")[:, 0:2 * CT, :],
                     rows(io["L3_gnn_W1"][0:C * 2, :])).then_inc(st["s_w6"], 16)

    @block.vector
    def _(dve):
        for c in range(CT):
            dve.wait_ge(sem["tr"], c + 1)
            dve.tensor_copy(cx.xT[:, c, :], ps[:, c, :]).then_inc(sem["xT"], 1)
        dve.wait_ge(sem["small"], 32)
        for n in range(NT):
            dve.scalar_tensor_tensor(out=xb[:, n, :], in0=cx.x[:, n, :], scalar=2.0, in1=b2[:], op0=ALU.mult,
                                     op1=ALU.add).then_inc(sem["xb"], 1)
        dve.wait_ge(sem["xb"], NT)
        for n in range(NT):
            dve.wait_ge(sem["mm"], n + 1)
            dve.tensor_tensor(y[:, n, :], ps[:, 4 + n, :], xb[:, n, :], ALU.add).then_inc(sem["y"], 1)
        norm_vector(dve, norm, y, cx.x, sem["y"])

    @block.scalar
    def _(act):
        act.wait_ge(sem["small"], 32)
        for m in range(HT):
            act.wait_ge(sem["h"], m + 1)
            act.activation(hT[:, m, :], ps[:, (4 + m) % 8, :], ACT.Relu, bias=b1[:, m:m + 1]).then_inc(sem["hT"], 1)
        norm_scalar(act, norm)

    @block.tensor
    def _(pe):
        transposes(pe, cx, cx.x, CT, None, sem["tr"])
        pe.wait_ge(sem["xT"], CT)
        pe.wait_ge(sem["w"], 32)
        pe.wait_ge(st["s_w5"], 32)
        for m in range(HT):
            product(pe, ps[:, (4 + m) % 8, :],
                    [(W1[:, k, m * P:(m + 1) * P], cx.xT[:, k, :]) for k in range(CT)]
                    + [(W1e[:, m * P:(m + 1) * P], cx.ea_mean[:])]).then_inc(sem["h"], 1)
        pe.wait_ge(sem["hT"], HT)
        for n in range(NT):
            product(pe, ps[:, 4 + n, :], [(hT[:, k, n * P:(n + 1) * P], W2[:, k, :]) for k in range(HT)]
                    ).then_inc(sem["mm"], 1)

    tmp.close()
    cx.end_phase()


def edge_weights(cx):
    return (cx.wB[:, 0:CT * C].rearrange("p (k n) -> p k n", k=CT), cx.wB[:, CT * C:(CT + 1) * C])


def edge_mlp_nodes(cx, st):
    nc, io = cx.nc, cx.io
    tmp = ExitStack()
    W = cx.wA[:].rearrange("p a k n -> p (a k) n")
    b1 = cx.sb("b13_b", [P, C], F32, tmp)
    out = cx.sb("xab", [P, 2, NT, C], F32, tmp)
    names = ("w", "small", "tr", "xT", "mm", "out", "dram")
    sem = {n: cx.sem("s7_" + n) for n in names}
    ps = cx.ps
    block = tmp.enter_context(nc.Block())

    @block.sync
    def _(sp):
        sp.dma_start(edge_weights(cx)[0], rows(io["L3_gnn_W2"])).then_inc(st["s_w7"], 16)
        for k in range(2):
            sp.dma_start(edge_weights(cx)[1][k * EA:(k + 1) * EA, :], io["L3_gnn_W1"][2 * C:2 * C + EA, :]
                         ).then_inc(st["s_w7"], 16)
        sp.dma_start(b1[:], row_b(io["L3_gnn_b1"])).then_inc(sem["small"], 16)
        for k, dram in enumerate((st["xa_dram"], st["xb_dram"])):
            sp.wait_ge(sem["out"], NT * (k + 1))
            sp.dma_start(dram.rearrange("(n p) c -> p n c", p=P), out[:, k]).then_inc(sem["dram"], 16)
        sp.wait_ge(sem["dram"], 32)

    @block.vector
    def _(dve):
        for c in range(CT):
            dve.wait_ge(sem["tr"], c + 1)
            dve.tensor_copy(cx.xT[:, c, :], ps[:, c, :]).then_inc(sem["xT"], 1)
        dve.wait_ge(sem["small"], 16)
        for i in range(2 * NT):
            k, n = i // NT, i % NT
            dve.wait_ge(sem["mm"], i + 1)
            if k == 0:
                dve.tensor_tensor(out[:, k, n, :], ps[:, (4 + i) % 8, :], b1[:], ALU.add).then_inc(sem["out"], 1)
            else:
                dve.tensor_copy(out[:, k, n, :], ps[:, (4 + i) % 8, :]).then_inc(sem["out"], 1)

    @block.tensor
    def _(pe):
        transposes(pe, cx, cx.x, CT, None, sem["tr"])
        pe.wait_ge(sem["xT"], CT)
        pe.wait_ge(st["s_w6"], 16)
        for i in range(2 * NT):
            k, n = i // NT, i % NT
            product(pe, ps[:, (4 + i) % 8, :],
                    [(cx.xT[:, c, n * P:(n + 1) * P], W[:, k * CT + c, :]) for c in range(CT)]
                    ).then_inc(sem["mm"], 1)

    tmp.close()
    cx.end_phase()


def edge_mlp(cx, st):
    nc, io = cx.nc, cx.io
    tmp = ExitStack()
    B = 2
    NB = ET // B
    W2h = cx.sb("W2h", [P, CT, C], F32R, tmp)
    W2l = cx.sb("W2l", [P, CT, C], F32R, tmp)
    Wch = cx.sb("Wch", [P, C], F32R, tmp)
    Wcl = cx.sb("Wcl", [P, C], F32R, tmp)
    b2 = cx.sb("b23_b", [P, C], F32, tmp)
    g = cx.sb("g", [P, 2, B, 2, C], F32, tmp)
    x1 = cx.wB[:, 0:2048].rearrange("p (r c e) -> p r c e", r=2, c=CT)
    x2 = cx.wB[:, 2048:4096].rearrange("p (r u c) -> p r u c", r=2, u=B)
    q = cx.sb("q", [P, 2, CT * B * P], F32, tmp)
    t = cx.wB[:, 4096:8192].rearrange("p (r k e) -> p r k e", r=2, k=2)
    f = cx.wA[:, 3].rearrange("p k c -> p (k c)").rearrange("p (a e) -> p a e", a=2)
    W2f, Wcf = edge_weights(cx)
    hh = cx.sb("hh", [P, 2, CT, B * P], F32R, tmp)
    hl = cx.sb("hl", [P, 2, CT, B * P], F32R, tmp)
    mh = cx.sb("mh", [P, 2, B, C], F32R, tmp)
    ml = cx.sb("ml", [P, 2, B, C], F32R, tmp)
    oh = cx.sb("oh3", [P, 2, B, N], F32R, tmp)
    names = ("w", "wh", "wl", "pre", "x1", "w2", "x2", "q1", "q2", "a1", "a2", "t1", "t2", "h", "m", "hh", "mh",
             "hl", "ml", "oh", "sum")
    sem = {n: cx.sem("s8_" + n) for n in names}
    s_g = [cx.sem(f"s8_g{i}") for i in range(2 * B * 2)]
    ps = cx.ps
    block = tmp.enter_context(nc.Block())
    FLAT = CT * B * P

    def rounds(engine, body):
        for k in range(-3, 1):
            body(k, k % 2, lambda a, c: a * k + c, {s for s, (lo, hi) in SPAN.items() if lo <= k <= hi})
        first, last = 1, NB - 4
        assert (last - first + 1) % 2 == 0
        with engine.Fori(0, (last - first + 1) // 2) as j:
            for v in range(2):
                k0 = first + v
                body(k0, k0 % 2, lambda a, c, k0=k0: j * (2 * a) + (a * k0 + c), set(SPAN))
        for k in range(last + 1, NB + 1):
            body(k, k % 2, lambda a, c: a * k + c, {s for s, (lo, hi) in SPAN.items() if lo <= k <= hi})

    SPAN = {"pre": (-3, NB - 4), "mish1": (-2, NB - 3), "second": (-1, NB - 2), "mish2": (0, NB - 1),
            "sum": (1, NB)}

    @block.sync
    def _(sp):
        sp.dma_start(b2[:], row_b(io["L3_gnn_b2"])).then_inc(sem["w"], 16)
        sp.dma_start(cx.wA[:].rearrange("p a k n -> p (a k) n")[:, 0:2 * CT, :], rows(io["L3_gnn_W3"])
                     ).then_inc(st["s_w8"], 16)
        sp.dma_start(cx.wA[:].rearrange("p a k n -> p (a k) n")[:, 2 * CT:3 * CT, :], rows(io["L3_gnn_W4"])
                     ).then_inc(st["s_w8"], 16)

    @block.gpsimd
    def _(pool):
        for b in range(NB):
            for u in range(B):
                for k, (dram, idx) in enumerate(((st["xa_dram"], cx.src_i), (st["xb_dram"], cx.dst_i))):
                    if b >= 2 and u == 0 and k == 0:
                        pool.wait_ge(sem["pre"], 2 * (b - 1))
                    tile = b * B + u
                    pool.indirect_dma_start(g[:, b % 2, u, k, :], None, dram,
                                            Offset(ap=idx[:, tile:tile + 1], axis=0)
                                            ).then_inc(s_g[((b % 2) * B + u) * 2 + k], 16)

    @block.vector
    def _(dve):
        dve.wait_ge(sem["w"], 16)
        dve.wait_ge(st["s_w7"], 48)
        dve.tensor_copy(W2h[:], W2f[:]).then_inc(sem["wh"], 1)
        dve.tensor_copy(Wch[:], Wcf[:]).then_inc(sem["wh"], 1)
        dve.wait_ge(sem["wh"], 2)
        dve.tensor_tensor(W2l[:], W2f[:], W2h[:].bitcast(F32), ALU.subtract).then_inc(sem["wl"], 1)
        dve.tensor_tensor(Wcl[:], Wcf[:], Wch[:].bitcast(F32), ALU.subtract).then_inc(sem["wl"], 1)
        dve.sem_inc(sem["sum"], 2)

        def body(k, r, at, on):
            if "second" in on:
                for u in range(B):
                    dve.wait_ge(sem["w2"], at(B, B + u + 1))
                    if k >= 1 and u == 0:
                        dve.wait_ge(sem["m"], at(1, 0))
                    dve.tensor_tensor(x2[:, 1 - r, u, :], ps[:, 2 + u, :], b2[:], ALU.add).then_inc(sem["x2"], 1)
            if "mish2" in on:
                dve.wait_ge(sem["sum"], at(1, 1))
                for u in range(B):
                    dve.tensor_scalar(oh[:, r, u, :], cx.iota_h[:], cx.dst_f[:, bass.ds(at(B, u), 1)],
                                      None, ALU.is_equal).then_inc(sem["oh"], 1)
            if "mish1" in on:
                dve.wait_ge(sem["t1"], at(1, 3))
                if k >= -1:
                    dve.wait_ge(sem["hl"], at(1, 2))
                dve.tensor_tensor(f[:, 0], x1[:, r].rearrange("p c e -> p (c e)"), t[:, r, 0], ALU.mult
                                  ).then_inc(sem["h"], 1)
                dve.wait_ge(sem["h"], at(1, 3))
                if k >= 0:
                    dve.wait_ge(sem["w2"], at(B, B))
                dve.tensor_copy(hh[:, r].rearrange("p c e -> p (c e)"), f[:, 0]).then_inc(sem["hh"], 1)
                dve.wait_ge(sem["hh"], at(1, 3))
                dve.tensor_tensor(hl[:, r].rearrange("p c e -> p (c e)"), f[:, 0],
                                  hh[:, r].rearrange("p c e -> p (c e)").bitcast(F32), ALU.subtract
                                  ).then_inc(sem["hl"], 1)
            if "pre" in on:
                for h in range(2):
                    dve.wait_ge(sem["pre"], at(2, 7 + h))
                    if k >= -1 and h == 0:
                        dve.wait_ge(sem["h"], at(1, 2))
                    dve.tensor_copy(x1[:, 1 - r, 2 * h:2 * h + 2, :].rearrange("p c e -> p (c e)"),
                                    ps[:, h, :]).then_inc(sem["x1"], 1)
            if "mish2" in on:
                dve.wait_ge(sem["t2"], at(1, 1))
                if k >= 1:
                    dve.wait_ge(sem["ml"], at(1, 0))
                dve.tensor_tensor(f[:, 1], x2[:, r].rearrange("p u c -> p (u c)"), t[:, r, 1], ALU.mult
                                  ).then_inc(sem["m"], 1)
                dve.wait_ge(sem["m"], at(1, 1))
                dve.tensor_copy(mh[:, r].rearrange("p u c -> p (u c)"), f[:, 1]).then_inc(sem["mh"], 1)
                dve.wait_ge(sem["mh"], at(1, 1))
                dve.tensor_tensor(ml[:, r].rearrange("p u c -> p (u c)"), f[:, 1],
                                  mh[:, r].rearrange("p u c -> p (u c)").bitcast(F32), ALU.subtract
                                  ).then_inc(sem["ml"], 1)

        rounds(dve, body)

    @block.scalar
    def _(act):
        def body(k, r, at, on):
            if "mish2" in on:
                act.wait_ge(sem["x2"], at(B, B))
                if k >= 1:
                    act.wait_ge(sem["t2"], at(1, 0))
                act.activation(q[:, 1], x2[:, r].rearrange("p u c -> p (u c)"), ACT.Sigmoid, scale=-1.0
                               ).then_inc(sem["q2"], 1)
            if "mish1" in on:
                act.wait_ge(sem["x1"], at(2, 6))
                if k >= -1:
                    act.wait_ge(sem["t1"], at(1, 2))
                act.activation(q[:, 0], x1[:, r].rearrange("p c e -> p (c e)"), ACT.Sigmoid, scale=-1.0
                               ).then_inc(sem["q1"], 1)
            if "mish1" in on:
                act.wait_ge(sem["q1"], at(1, 3))
                act.activation(q[:, 0], q[:, 0], ACT.Arctan).then_inc(sem["a1"], 1)
            if "mish2" in on:
                act.wait_ge(sem["q2"], at(1, 1))
                act.activation(q[:, 1], q[:, 1], ACT.Arctan).then_inc(sem["a2"], 1)
            if "mish1" in on:
                act.wait_ge(sem["a1"], at(1, 3))
                if k >= 0:
                    act.wait_ge(sem["h"], at(1, 1))
                act.activation(t[:, r, 0], q[:, 0], ACT.Sin, bias=cx.half_pi[:], scale=-2.0).then_inc(sem["t1"], 1)
            if "mish2" in on:
                act.wait_ge(sem["a2"], at(1, 1))
                if k >= 2:
                    act.wait_ge(sem["m"], at(1, -1))
                act.activation(t[:, r, 1], q[:, 1], ACT.Sin, bias=cx.half_pi[:], scale=-2.0).then_inc(sem["t2"], 1)

        rounds(act, body)

    @block.tensor
    def _(pe):
        for c in range(CT):
            pe.matmul(ps[:, 4 + c, :], cx.zero_r[:, 0:P], cx.zero_r[:], start=True, stop=False)
        pe.wait_ge(sem["wl"], 2)

        def body(k, r, at, on):
            if "second" in on:
                pe.wait_ge(sem["hl"], at(1, 2))
                for u in range(B):
                    if k >= 0:
                        pe.wait_ge(sem["x2"], at(B, u + 1))
                    cols = slice(u * P, (u + 1) * P)
                    product(pe, ps[:, 2 + u, :],
                            [(a[:, 1 - r, c, cols], w[:, c, :]) for c in range(CT)
                             for a, w in ((hh, W2h), (hh, W2l), (hl, W2h))]).then_inc(sem["w2"], 1)
            if "sum" in on:
                pe.wait_ge(sem["ml"], at(1, 0))
                pe.wait_ge(sem["oh"], at(B, 0))
                for u in range(B):
                    for c in range(CT):
                        for a in (mh, ml):
                            m = pe.matmul(ps[:, 4 + c, :], a[:, 1 - r, u, c * P:(c + 1) * P], oh[:, 1 - r, u, :],
                                          start=False, stop=False)
                m.then_inc(sem["sum"], 1)
            if "pre" in on:
                for h in range(2):
                    if k >= -2:
                        pe.wait_ge(sem["x1"], at(2, 5 + h))
                    if h == 0:
                        for i in range(2 * B):
                            slot = (1 - r) * B * 2 + i
                            if k % 2 == 0:
                                pe.wait_ge(s_g[slot], at(8, 32))
                            else:
                                pe.wait_ge(s_g[slot], at(8, 40))
                    for c in (2 * h, 2 * h + 1):
                        out = ps[:, h, (c % 2) * B * P:(c % 2 + 1) * B * P]
                        edges = cx.eaT[:, bass.ds(at(B * P, 3 * B * P), B * P)]
                        pe.matmul(out, Wch[:, c * P:(c + 1) * P], edges, start=True, stop=False)
                        for u in range(B):
                            for i in range(2):
                                pe.matmul(out[:, u * P:(u + 1) * P], g[:, 1 - r, u, i, c * P:(c + 1) * P],
                                          cx.ident[:], is_transpose=True, start=False, stop=False)
                        m = pe.matmul(out, Wcl[:, c * P:(c + 1) * P], edges, start=False, stop=True)
                    m.then_inc(sem["pre"], 1)

        rounds(pe, body)
        for c in range(CT):
            pe.matmul(ps[:, 4 + c, :], cx.zero_r[:, 0:P], cx.zero_r[:], start=False, stop=True)

    tmp.close()
    cx.end_phase()


def edge_mlp_out(cx, st):
    nc, io = cx.nc, cx.io
    tmp = ExitStack()
    aggT = cx.sb("aggT", [P, CT, N], F32, tmp)
    b3 = cx.sb("b33", [P, CT], F32, tmp)
    xu = cx.sb("xu", [P, CT, N], F32, tmp)
    qu = cx.sb("qu", [P, CT, N], F32, tmp)
    uT = cx.sb("uT", [P, CT, N], F32, tmp)
    rowsb = cx.sb("rows3", [P, 3, C], F32, tmp)
    xb = cx.sb("xb3", [P, NT, C], F32, tmp)
    y = cx.sb("y3", [P, NT, C], F32, tmp)
    z = cx.sb("z3", [P, NT, C], F32, tmp)
    n5, n6 = Norm(cx, "n5", tmp), Norm(cx, "n6", tmp)
    names = ("small", "aggT", "mm", "xu", "q", "a", "t", "u", "xb", "mm2", "y", "g", "b", "r", "store")
    sem = {n: cx.sem("s9_" + n) for n in names}
    W = cx.wA[:].rearrange("p a k n -> p (a k) n")
    W3, W4 = W[:, 0:2 * CT, :], W[:, 2 * CT:3 * CT, :]
    ps = cx.ps
    block = tmp.enter_context(nc.Block())

    @block.sync
    def _(sp):
        sp.dma_start(b3[:], col(io["L3_gnn_b3"], CT), allow_slow_non_contiguous=True).then_inc(sem["small"], 16)
        for i, name in enumerate(("L3_gnn_b4", "L3_gnn_gamma", "L3_gnn_beta")):
            sp.dma_start(rowsb[:, i, :], row_b(io[name])).then_inc(sem["small"], 16)
        sp.wait_ge(n6.s_out, NT)
        sp.dma_start(rows(io["out"]), z[:]).then_inc(sem["store"], 16)
        sp.wait_ge(sem["store"], 16)

    @block.vector
    def _(dve):
        for c in range(1, CT, 2):
            dve.tensor_copy(aggT[:, c, :], ps[:, 4 + c, :]).then_inc(sem["aggT"], 1)
        dve.wait_ge(sem["small"], 64)
        for n in range(NT):
            dve.tensor_tensor(xb[:, n, :], cx.x[:, n, :], rowsb[:, 0, :], ALU.add).then_inc(sem["xb"], 1)
        for c in range(CT):
            dve.wait_ge(sem["mm"], c + 1)
            dve.tensor_scalar(xu[:, c, :], ps[:, c, :], b3[:, c:c + 1], None, ALU.add).then_inc(sem["xu"], 1)
        dve.wait_ge(sem["xu"], CT)
        for c in range(CT):
            dve.wait_ge(sem["t"], 1)
            dve.tensor_tensor(uT[:, c, :], xu[:, c, :], qu[:, c, :], ALU.mult).then_inc(sem["u"], 1)
        dve.wait_ge(sem["xb"], NT)
        for n in range(NT):
            dve.wait_ge(sem["mm2"], n + 1)
            dve.tensor_tensor(y[:, n, :], ps[:, 4 + n, :], xb[:, n, :], ALU.add).then_inc(sem["y"], 1)
        norm_vector(dve, n5, y, z, sem["y"])
        dve.wait_ge(n5.s_out, NT)
        for n in range(NT):
            dve.tensor_tensor(xb[:, n, :], z[:, n, :], rowsb[:, 1, :], ALU.mult).then_inc(sem["g"], 1)
        for n in range(NT):
            dve.wait_ge(sem["g"], n + 1)
            dve.tensor_tensor(z[:, n, :], xb[:, n, :], rowsb[:, 2, :], ALU.add).then_inc(sem["b"], 1)
        for n in range(NT):
            dve.wait_ge(sem["b"], n + 1)
            dve.tensor_tensor(y[:, n, :], z[:, n, :], cx.x[:, n, :], ALU.add).then_inc(sem["r"], 1)
        norm_vector(dve, n6, y, z, sem["r"])

    @block.scalar
    def _(act):
        for c in range(0, CT, 2):
            act.activation(aggT[:, c, :], ps[:, 4 + c, :], ACT.Copy).then_inc(sem["aggT"], 1)
        act.wait_ge(sem["xu"], CT)
        act.activation(qu[:], xu[:], ACT.Sigmoid, scale=-1.0).then_inc(sem["q"], 1)
        act.wait_ge(sem["q"], 1)
        act.activation(qu[:], qu[:], ACT.Arctan).then_inc(sem["a"], 1)
        act.wait_ge(sem["a"], 1)
        act.activation(qu[:], qu[:], ACT.Sin, bias=cx.half_pi[:], scale=-2.0).then_inc(sem["t"], 1)
        norm_scalar(act, n5)
        norm_scalar(act, n6)

    @block.tensor
    def _(pe):
        pe.wait_ge(sem["aggT"], CT)
        pe.wait_ge(st["s_w8"], 32)
        for c in range(CT):
            product(pe, ps[:, c, :],
                    [(W3[:, k, c * P:(c + 1) * P], cx.xT[:, k, :]) for k in range(CT)]
                    + [(W3[:, CT + k, c * P:(c + 1) * P], aggT[:, k, :]) for k in range(CT)]
                    ).then_inc(sem["mm"], 1)
        pe.wait_ge(sem["u"], CT)
        for n in range(NT):
            product(pe, ps[:, 4 + n, :], [(uT[:, k, n * P:(n + 1) * P], W4[:, k, :]) for k in range(CT)]
                    ).then_inc(sem["mm2"], 1)

    tmp.close()
    cx.end_phase()


def build_program(nc, io):
    with ExitStack() as stack:
        cx = Ctx(nc, io, stack)
        cx.ps = stack.enter_context(nc.psum_tensor("ps", [P, 8, 512], F32))
        cx.ident = cx.sb("ident", [P, P])
        cx.zero_r = cx.sb("zero_r", [P, C], F32R)
        cx.iota_h = cx.sb("iota_h", [P, N], FP16)
        cx.half_pi = cx.sb("half_pi", [P, 1])
        cx.part_f = cx.sb("part_f", [P, NT])
        cx.x = cx.sb("x", [P, NT, C])
        cx.xT = cx.sb("xT", [P, CT, N])
        cx.src_i = cx.sb("src_i", [P, ET], I32)
        cx.dst_i = cx.sb("dst_i", [P, ET], I32)
        cx.src_f = cx.sb("src_f", [P, ET])
        cx.dst_f = cx.sb("dst_f", [P, ET])
        cx.wA = cx.sb("wA", [P, 4, CT, C])
        cx.wB = cx.sb("wB", [P, HT * HID])
        st = {"pair_i": cx.sb("pair_i", [P, ET], I32)}
        for name in ("s_x0", "s_sg", *(f"s_w{i}" for i in range(9))):
            st[name] = stack.enter_context(nc.semaphore(name))
        for name, shape in (("v_dram", [N, C]), ("s_dram", [N * N, H0]), ("xa_dram", [N, C]), ("xb_dram", [N, C])):
            st[name] = nc.dram_tensor(name, shape, F32).ap()
        st["weights0"] = [(cx.wA[:, i], f"L0_gnn_{n}") for i, n in enumerate(("Wq", "Wk", "Wv", "Wo"))]
        cx.eaT = cx.sb("eaT", [P, E], F32R)
        with ExitStack() as graph:
            cx.cnt = cx.sb("cnt", [P, NT, N], F32, graph)
            cx.pen = cx.sb("pen", [P, NT, N], F32, graph)
            cx.rcount = cx.sb("rcount", [P, N], F32, graph)
            cx.ea_mean = cx.sb("ea_mean", [P, N], F32, graph)
            with ExitStack() as layer0:
                st["src_row"] = cx.sb("src_row", [P, E], FP16, layer0)
                st["sg"] = cx.sb("sg", [P, ET, H0], F32, layer0)
                setup(cx, st)
                attention_scores(cx, st)
                edge_sums(cx, st)
                attention_edges(cx, st)
            attention_out(cx, st)
            with ExitStack() as layer1:
                h1 = cx.sb("h1", [P, NT * H1 * W_], F32, layer1)
                h2 = cx.sb("h2", [P, NT * H1 * W_], F32, layer1)
                gat(cx, st, "g1", gat1_weights(cx), CT, cx.xT, h1, io["L1_gnn_a_src1"], io["L1_gnn_a_dst1"],
                    io["L1_gnn_b1"], st["s_w2"], 16, cx.x)
                gat(cx, st, "g2", cx.wB[:].rearrange("p (k n) -> p k n", k=HT), HT, gat_output(h1), h2,
                    io["L1_gnn_a_src2"], io["L1_gnn_a_dst2"], io["L1_gnn_b2"], st["s_w3"], 16, None)
                gat_out(cx, st, gat_output(h2))
            residual_layer(cx, st)
        edge_mlp_nodes(cx, st)
        edge_mlp(cx, st)
        edge_mlp_out(cx, st)


USED = ("x", "src", "dst", "edge_attr_64", "edge_attr_8",
        *(f"L0_gnn_{n}" for n in ("Wq", "bq", "Wk", "bk", "Wv", "bv", "Wo", "bo", "ln1_g", "ln1_b", "ln2_g",
                                  "ln2_b", "W1", "b1", "W2", "b2")),
        *(f"L1_gnn_{n}" for n in ("W1", "a_src1", "a_dst1", "b1", "W2", "a_src2", "a_dst2", "b2", "Wfc", "bfc")),
        *(f"L2_gnn_{n}" for n in ("W1", "b1", "W2", "b2")),
        *(f"L3_gnn_{n}" for n in ("W1", "b1", "W2", "b2", "W3", "b3", "W4", "b4", "gamma", "beta")))


def kernel(**inputs):
    import numpy as np
    import concourse.bacc as bacc
    from concourse.bass_utils import run_bass_kernel_spmd

    nc = bacc.Bacc("TRN2", target_bir_lowering=False, num_devices=1)
    arrays, io = {}, {}
    for name in USED:
        a = np.ascontiguousarray(inputs[name])
        arrays[f"in_{name}_dram"] = a
        io[name] = nc.dram_tensor(f"in_{name}_dram", a.shape, mybir.dt.from_np(a.dtype), kind="ExternalInput").ap()
    io["out"] = nc.dram_tensor("out_0_dram", [N, C], F32, kind="ExternalOutput").ap()
    build_program(nc, io)
    r = run_bass_kernel_spmd(nc, [arrays], core_ids=[0])
    return r.results[0]["out_0_dram"]
```

```python
from contextlib import ExitStack

import concourse.bass as bass
from concourse import mybir

F32 = mybir.dt.float32
F32R = mybir.dt.float32r
BF16 = mybir.dt.bfloat16
FP16 = mybir.dt.float16
I32 = mybir.dt.int32
ALU = mybir.AluOpType
ACT = mybir.ActivationFunctionType
AX = mybir.AxisListType
Offset = bass.IndirectOffsetOnAxis

P = 128
N = 512
C = 512
E = 8192
NT = N // P
CT = C // P
ET = E // P
H0, D0 = 8, 64
HID = 1024
HT = HID // P
H1, C1 = 4, 256
EA = 64
EPS = 1e-5
LN2 = 0.6931471805599453
BIG = 3.0e38
HALF_PI = 1.5707963267948966
GUARD_T, GUARD_M = 8.0, 8
GUARD_STEP = 108 * LN2 * GUARD_T
GUARD_MARGIN = 30.0


class Ctx:

    def __init__(self, nc, io, stack):
        self.nc, self.io, self.stack = nc, io, stack
        self.phase_sems = []

    def sb(self, name, shape, dt=F32, stack=None):
        return (stack or self.stack).enter_context(self.nc.sbuf_tensor(name, shape, dt))

    def sem(self, name):
        s = self.nc.alloc_semaphore(name=name)
        self.phase_sems.append(s)
        return s

    def end_phase(self):
        self.nc.clear_and_free_semaphores(self.phase_sems)
        self.nc.all_engine_barrier()
        self.phase_sems = []


def row_b(vec):
    return vec.partition_broadcast(P)


def col(vec, tiles):
    return vec.rearrange("(k p) -> p k", p=P)


def rows(mat):
    return mat.rearrange("(k p) n -> p k n", p=P)


class Norm:

    def __init__(self, cx, tag, stack):
        self.stats = cx.sb(f"{tag}_stats", [P, NT, 6], F32, stack)
        self.mv = cx.sb(f"{tag}_mv", [P, NT, 2], F32, stack)
        self.var = cx.sb(f"{tag}_var", [P, NT], F32, stack)
        self.std = cx.sb(f"{tag}_std", [P, NT], F32, stack)
        self.rstd = cx.sb(f"{tag}_rstd", [P, NT], F32, stack)
        self.s_stats = cx.sem(f"{tag}_s_stats")
        self.s_aggr = cx.sem(f"{tag}_s_aggr")
        self.s_var = cx.sem(f"{tag}_s_var")
        self.s_std = cx.sem(f"{tag}_s_std")
        self.s_rstd = cx.sem(f"{tag}_s_rstd")
        self.s_out = cx.sem(f"{tag}_s_out")


def norm_vector(e, n, x, out, s_x):
    for i in range(NT):
        e.wait_ge(s_x, i + 1)
        e.bn_stats(n.stats[:, i, :], x[:, i, :]).then_inc(n.s_stats, 1)
    for i in range(NT):
        e.wait_ge(n.s_stats, i + 1)
        e.bn_aggr(n.mv[:, i, :], n.stats[:, i, :]).then_inc(n.s_aggr, 1)
    e.wait_ge(n.s_aggr, NT)
    e.tensor_scalar(n.var[:], n.mv[:, :, 1], EPS, None, ALU.add).then_inc(n.s_var, 1)
    e.wait_ge(n.s_std, 1)
    e.reciprocal(n.rstd[:], n.std[:]).then_inc(n.s_rstd, 1)
    e.wait_ge(n.s_rstd, 1)
    for i in range(NT if out is not None else 0):
        e.tensor_scalar(out[:, i, :], x[:, i, :], n.mv[:, i, 0:1], n.rstd[:, i:i + 1],
                        ALU.subtract, ALU.mult).then_inc(n.s_out, 1)


def norm_scalar(e, n):
    e.wait_ge(n.s_var, 1)
    e.activation(n.std[:], n.var[:], ACT.Sqrt).then_inc(n.s_std, 1)


def transposes(pe, cx, x, tiles, s_x, s_done, bank0=0):
    for n in range(NT):
        if s_x is not None:
            pe.wait_ge(s_x, n + 1)
        for c in range(tiles):
            t = pe.transpose(cx.ps[:, bank0 + c, n * P:(n + 1) * P], x[:, n, c * P:(c + 1) * P], cx.ident[:])
            if n == NT - 1:
                t.then_inc(s_done, 1)


def product(pe, out, pairs):
    for k, (lhsT, rhs) in enumerate(pairs):
        m = pe.matmul(out, lhsT, rhs, start=(k == 0), stop=(k == len(pairs) - 1))
    return m


class Split:

    def __init__(self, cx, tag, mem, steps):
        parts = mem.rearrange("p (r k c) -> p r k c", r=2, k=4)
        self.high, self.low = parts[:, :, 0:2], parts[:, :, 2:4]
        self.steps, self.ps = steps, cx.ps
        self.s_high = cx.sem(tag + "_high")
        self.s_low = cx.sem(tag + "_low")
        self.s_done = cx.sem(tag + "_done")

    def scalar(self, act, lo, hi):
        for i in range(lo, hi):
            if i >= 2:
                act.wait_ge(self.s_done, i - 1)
            for k in range(2):
                act.activation(self.high[:, i % 2, k], self.steps[i][k], ACT.Copy).then_inc(self.s_high, 1)

    def vector(self, dve, lo, hi):
        for i in range(lo, hi):
            for k in range(2):
                dve.wait_ge(self.s_high, 2 * i + k + 1)
                dve.tensor_tensor(self.low[:, i % 2, k], self.steps[i][k],
                                  self.high[:, i % 2, k].bitcast(F32), ALU.subtract).then_inc(self.s_low, 1)

    def tensor(self, pe, lo, hi, banks_free=None, s_mm=None):
        for i in range(lo, hi):
            _, _, bank, first, last = self.steps[i]
            pe.wait_ge(self.s_low, 2 * i + 2)
            for n in range(4):
                if first and banks_free:
                    banks_free(n)
                cols = slice(n * P, (n + 1) * P)
                for j, (a, b) in enumerate(((self.high, self.high), (self.high, self.low), (self.low, self.high))):
                    m = pe.matmul(self.ps[:, bank + n, :], a[:, i % 2, 0, cols], b[:, i % 2, 1, :],
                                  start=first and j == 0, stop=last and j == 2)
                if last and n < 3:
                    m.then_inc(s_mm, 1)
            m.then_inc(self.s_done, 1)
            if last:
                pe.wait_ge(self.s_done, i + 1)
                pe.sem_inc(s_mm, 1)


def chunks(pairs, bank):
    return [(a, b, bank, i == 0, i == len(pairs) - 1) for i, (a, b) in enumerate(pairs)]


def setup(cx, st):
    nc, io = cx.nc, cx.io
    tmp = ExitStack()
    iota_i = cx.sb("iota_i", [P, N], I32, tmp)
    part_i = cx.sb("part_i", [P, NT], I32, tmp)
    s_in, s_const, s_f = cx.sem("s_in"), cx.sem("s_const"), cx.sem("s_f")
    s_zero = cx.sem("s_zero")
    block = tmp.enter_context(nc.Block())

    @block.sync
    def _(sp):
        sp.dma_start(cx.src_i[:], io["src"].rearrange("(p t) -> p t", p=P)).then_inc(s_in, 16)
        sp.dma_start(cx.dst_i[:], io["dst"].rearrange("(p t) -> p t", p=P)).then_inc(s_in, 16)
        sp.dma_start(cx.x[:], rows(io["x"])).then_inc(st["s_x0"], 16)

    @block.scalar
    def _(act):
        for w, (buf, name) in enumerate(st["weights0"]):
            act.dma_start(buf, rows(io[name])).then_inc(st["s_w0"], 16)

    @block.gpsimd
    def _(pool):
        pool.memset(cx.ident[:], 0.0).then_inc(s_zero, 1)
        pool.iota(iota_i[:], pattern=[[1, N]], base=0, channel_multiplier=0).then_inc(s_const, 1)
        pool.iota(part_i[:], pattern=[[P, NT]], base=0, channel_multiplier=1).then_inc(s_const, 1)
        pool.memset(cx.half_pi[:], HALF_PI)
        pool.wait_ge(s_zero, 1)
        pool.affine_select(out=cx.ident[:], in_=cx.ident[:], compare_op=ALU.not_equal, fill=1.0, base=0,
                           pattern=[[-1, P]], channel_multiplier=1).then_inc(s_zero, 1)

    @block.vector
    def _(dve):
        dve.memset(cx.zero_r[:].bitcast(F32), 0.0)
        dve.wait_ge(s_const, 2)
        dve.tensor_copy(cx.iota_h[:], iota_i[:])
        dve.tensor_copy(cx.part_f[:], part_i[:]).then_inc(s_f, 1)
        dve.wait_ge(s_in, 32)
        dve.tensor_copy(cx.src_f[:], cx.src_i[:]).then_inc(s_f, 1)
        dve.tensor_copy(cx.dst_f[:], cx.dst_i[:]).then_inc(s_f, 1)
        dve.tensor_copy(cx.src_h[:], cx.src_i[:])
        dve.wait_ge(s_zero, 2)
        dve.tensor_copy(cx.ident_h[:], cx.ident[:])
        dve.wait_ge(s_f, 3)
        dve.scalar_tensor_tensor(out=st["pair_i"][:], in0=cx.src_f[:], scalar=float(N), in1=cx.dst_f[:],
                                 op0=ALU.mult, op1=ALU.add)

    tmp.close()
    cx.end_phase()


def attention_scores(cx, st):
    nc, io = cx.nc, cx.io
    tmp = ExitStack()
    z = cx.sb("z0", [P, NT, C], F32, tmp)
    qT = cx.sb("qT", [P, CT, N], F32, tmp)
    kT = cx.sb("kT", [P, CT, N], F32, tmp)
    v = cx.sb("v", [P, NT, C], F32, tmp)
    stage = cx.wB[:].rearrange("p (a n h) -> p a n h", a=2, h=H0)
    bv = cx.sb("bv_b", [P, C], F32, tmp)
    cols = cx.sb("cols0", [P, 4, CT], F32, tmp)
    norm = Norm(cx, "n0", tmp)
    s_small = cx.sem("s0_small")
    s_x, s_tr, s_zT, s_v = (cx.sem("s0_" + n) for n in ("x", "tr", "zT", "v"))
    s_vmm, s_qk, s_smm = (cx.sem("s0_" + n) for n in ("vmm", "qk", "smm"))
    s_spread, s_row = cx.sem("s0_spread"), cx.sem("s0_row")
    s_qk_out = [cx.sem("s0_qk_out_act"), cx.sem("s0_qk_out_dve")]
    s_ev = [cx.sem("s0_ev_act"), cx.sem("s0_ev_dve")]
    s_st = st["s_st"]
    Wq, Wk, Wv = (cx.wA[:, i] for i in range(3))
    split = Split(cx, "s0x", cx.eaT[:, 0:E // 2],
                  chunks([(cx.xT[:, k, :], Wv[:, k, :]) for k in range(CT)], 4)
                  + chunks([(Wq[:, k, :], cx.xT[:, k, :]) for k in range(CT)], 0)
                  + chunks([(Wk[:, k, :], cx.xT[:, k, :]) for k in range(CT)], 4))
    v_dram = st["v_dram"].rearrange("(n p) c -> p n c", p=P)
    s_dram = st["s_dram"].rearrange("(n p c) h -> p n c h", n=NT, p=P)
    ps = cx.ps
    block = tmp.enter_context(nc.Block())

    @block.sync
    def _(sp):
        for i, name in enumerate(("L0_gnn_ln1_g", "L0_gnn_ln1_b", "L0_gnn_bq", "L0_gnn_bk")):
            sp.dma_start(cols[:, i, :], col(io[name], CT), allow_slow_non_contiguous=True).then_inc(s_small, 16)
        sp.dma_start(bv[:], row_b(io["L0_gnn_bv"])).then_inc(s_small, 16)
        sp.wait_ge(s_v, NT)
        sp.dma_start(v_dram, v[:]).then_inc(st["s_vout"], 16)
        for n in range(NT):
            sp.wait_ge(s_ev[0], (n + 1) * H0 // 2)
            sp.wait_ge(s_ev[1], (n + 1) * H0 // 2)
            sp.dma_start(s_dram[:, n], stage[:, n % 2]).then_inc(s_st[n % 2], 16)
        sp.wait_ge(st["s_vout"], 16)

    @block.vector
    def _(dve):
        dve.wait_ge(st["s_x0"], 16)
        dve.sem_inc(s_x, NT)
        norm_vector(dve, norm, cx.x, z, s_x)
        dve.wait_ge(s_small, 80)
        for c in range(1, CT, 2):
            dve.wait_ge(s_tr, c + 1)
            dve.tensor_scalar(cx.xT[:, c, :], ps[:, c, :], cols[:, 0, c:c + 1], cols[:, 1, c:c + 1],
                              ALU.mult, ALU.add).then_inc(s_zT, 1)
        split.vector(dve, 0, CT + 2)
        for n in range(NT):
            dve.wait_ge(s_vmm, n + 1)
            dve.tensor_tensor(v[:, n, :], ps[:, 4 + n, :], bv[:], ALU.add).then_inc(s_v, 1)
        for i in range(1, 2 * CT, 2):
            c, out = i % CT, (qT, kT)[i // CT]
            if i == 1:
                split.vector(dve, CT + 2, 2 * CT + 2)
            if i == CT + 1:
                split.vector(dve, 2 * CT + 2, 3 * CT)
            dve.wait_ge(s_qk, i + 1)
            dve.tensor_scalar(out[:, c, :], ps[:, i, :], cols[:, 2 + i // CT, c:c + 1], None,
                              ALU.add).then_inc(s_qk_out[1], 1)
        for u in range(1, NT * H0, 2):
            n, h = u // H0, u % H0
            dve.wait_ge(s_smm, u + 1)
            if n >= 2 and h == 1:
                dve.wait_ge(s_st[n % 2], 16)
            dve.tensor_scalar(stage[:, n % 2, :, h], ps[:, u % 8, :], 0.125, None, ALU.mult).then_inc(s_ev[1], 1)

    @block.scalar
    def _(act):
        def row_of_src(groups):
            for g in groups:
                act.wait_ge(s_spread, g + 1)
                act.activation(st["src_row"][:, g * N:(g + 1) * N], ps[:, 4 + g % 4, :], ACT.Copy
                               ).then_inc(s_row, 1)

        row_of_src(range(4))
        norm_scalar(act, norm)
        row_of_src(range(4, ET // 4))
        act.wait_ge(s_small, 80)
        for c in range(0, CT, 2):
            act.wait_ge(s_tr, c + 1)
            act.activation(cx.xT[:, c, :], ps[:, c, :], ACT.Identity, bias=cols[:, 1, c:c + 1],
                           scale=cols[:, 0, c:c + 1]).then_inc(s_zT, 1)
        act.wait_ge(s_zT, CT)
        act.wait_ge(st["s_w0"], 16 * 4)
        split.scalar(act, 0, 2 * CT + 2)
        for i in range(0, 2 * CT, 2):
            c, out = i % CT, (qT, kT)[i // CT]
            if i == CT:
                split.scalar(act, 2 * CT + 2, 3 * CT)
            act.wait_ge(s_qk, i + 1)
            act.activation(out[:, c, :], ps[:, i, :], ACT.Identity,
                           bias=cols[:, 2 + i // CT, c:c + 1]).then_inc(s_qk_out[0], 1)
        for u in range(0, NT * H0, 2):
            n, h = u // H0, u % H0
            act.wait_ge(s_smm, u + 1)
            if n >= 2 and h == 0:
                act.wait_ge(s_st[n % 2], 16)
            act.activation(stage[:, n % 2, :, h], ps[:, u % 8, :], ACT.Copy, scale=0.125).then_inc(s_ev[0], 1)

    @block.tensor
    def _(pe):
        for g in range(ET // 4):
            if g >= 4:
                pe.wait_ge(s_row, g - 3)
            for u in range(4):
                m = pe.matmul(ps[:, 4 + g % 4, u * P:(u + 1) * P],
                              cx.src_h[:, 4 * g + u:4 * g + u + 1].to_broadcast([P, P]), cx.ident_h[:],
                              start=True, stop=True)
            m.then_inc(s_spread, 1)
        transposes(pe, cx, z, CT, norm.s_out, s_tr)
        pe.wait_ge(s_row, ET // 4)
        split.tensor(pe, 0, CT, s_mm=s_vmm)
        split.tensor(pe, CT, 2 * CT, s_mm=s_qk)
        split.tensor(pe, 2 * CT, 3 * CT, lambda n: pe.wait_ge(s_v, n + 1), s_qk)
        for u in range(NT * H0):
            n, h = u // H0, u % H0
            lo = D0 * (h % 2)
            if u < H0:
                c = h // 2
                pe.wait_ge(s_qk_out[c % 2], (CT + c) // 2 + 1)
                pe.wait_ge(s_qk_out[u % 2], u // 2 + 1)
            if u >= 8:
                pe.wait_ge(s_ev[u % 2], (u - 8) // 2 + 1)
            pe.matmul(ps[:, u % 8, :], qT[lo:lo + D0, h // 2, n * P:(n + 1) * P], kT[lo:lo + D0, h // 2, :],
                      start=True, stop=True).then_inc(s_smm, 1)

    tmp.close()
    cx.end_phase()


def attention_edges(cx, st):
    nc, io = cx.nc, cx.io
    tmp = ExitStack()
    R, G, M = 4, 8, GUARD_M
    sg = st["sg"]
    bias = st["bias"]
    s = cx.sb("s", [P, ET, H0], F32, tmp)
    diff = cx.sb("diff", [P, ET, H0], F32, tmp)
    diff2 = cx.sb("diff2", [P, ET, H0], F32, tmp)
    p = cx.sb("p", [P, ET, H0], F32, tmp)
    p_hl = cx.sb("p_hl", [P, ET, 2, H0], F32R, tmp)
    p_ring = cx.sb("p_ring", [P, R, P], F32R, tmp)
    pmax = cx.sb("pmax", [P, H0], F32, tmp)
    gcol = cx.sb("gcol", [H0, 1], F32, tmp)
    top = cx.sb("top", [P, H0], F32, tmp)
    small = [P, NT, M, H0]
    total = cx.sb("total", small, F32, tmp)
    expo = cx.sb("expo", small, I32, tmp)
    cand = cx.sb("cand", small, F32, tmp)
    cand2 = cx.sb("cand2", small, F32, tmp)
    cand3 = cx.sb("cand3", small, F32, tmp)
    empty = cx.sb("empty", [P, NT, M, H0], F32, tmp)
    best = cx.sb("best", [P, NT, H0], F32, tmp)
    bound = cx.sb("bound", [P, NT, H0], F32, tmp)
    bound_hl = cx.sb("bound_hl", [P, NT, 2, H0], BF16, tmp)
    edge_bound = cx.sb("edge_bound", [P, ET, 2, H0], F32, tmp)
    guard = ExitStack()
    w = cx.sb("w", [P, ET, M, H0], BF16, guard)
    oh = cx.sb("oh", [P, R, N], BF16, guard)
    ohT = cx.sb("ohT", [P, 2, NT, R * P], BF16, guard)
    guard.close()
    oh_r = cx.sb("oh_r", [P, R, N], F32R, tmp)
    pv = cx.xT
    pv_hi = cx.sb("pv_hi", [P, R, C], F32R, tmp)
    pv_lo = cx.sb("pv_lo", [P, R, C], F32R, tmp)
    vg = cx.wA[:, 0:2].rearrange("p a k c -> p (a k) c")
    args = [mem.rearrange("p k c -> p (k c)").rearrange("p (m t h) -> p m t h", m=M // 2, h=H0)
            for mem in (cx.xT[:], cx.wA[:, 2])]
    names = ("s", "pmax", "gT", "gcol", "gb", "top", "diff", "arg", "w", "oh", "oh_free", "sum",
             "total", "expo", "cand", "best", "bound", "hi", "lo", "ohT", "back", "eb", "d2", "d3", "p", "p_hl",
             "ohr", "pv", "pvhi", "pvlo", "used")
    sem = {n: cx.sem("s1_" + n) for n in names}
    s_vg = [cx.sem(f"s1_vg{i}") for i in range(G)]
    ps = cx.ps
    g_psum = ps[0:H0, 0, 0:P]
    gb_psum = ps[:, 0, P:P + H0]
    sum_psum = ps[:, 1, 0:NT * M * H0].rearrange("p (n c) -> p n c", n=NT)
    block = tmp.enter_context(nc.Block())

    @block.gpsimd
    def _(pool):
        for t in range(ET):
            if t >= G:
                pool.wait_ge(sem["pv"], t - G + 1)
            pool.indirect_dma_start(vg[:, t % G, :], None, st["v_dram"], Offset(ap=cx.dst_i[:, t:t + 1], axis=0)
                                    ).then_inc(s_vg[t % G], 16)

    @block.vector
    def _(dve):
        dve.memset(p_ring[:].bitcast(F32), 0.0)
        dve.wait_ge(st["s_bias"], 16)
        dve.wait_ge(st["s_sg"], 16 * ET)
        dve.tensor_tensor(s[:], sg[:], bias[:], ALU.add).then_inc(sem["s"], 1)
        dve.wait_ge(sem["s"], 1)
        dve.tensor_reduce(pmax[:], s[:].rearrange("p t h -> p h t"), AX.X, ALU.max).then_inc(sem["pmax"], 1)
        dve.wait_ge(sem["gT"], 1)
        dve.tensor_reduce(gcol[:], g_psum, AX.X, ALU.max).then_inc(sem["gcol"], 1)
        dve.wait_ge(sem["gb"], 1)
        dve.tensor_copy(top[:], gb_psum).then_inc(sem["top"], 1)
        dve.wait_ge(sem["top"], 1)
        dve.tensor_tensor(diff[:], s[:], top[:].unsqueeze(1).to_broadcast([P, ET, H0]), ALU.subtract
                          ).then_inc(sem["diff"], 1)
        dve.wait_ge(sem["diff"], 1)
        for m in range(M):
            dve.tensor_scalar(args[m // (M // 2)][:, m % (M // 2)], diff[:], m * GUARD_STEP, GUARD_STEP, ALU.add, ALU.min
                              ).then_inc(sem["arg"], 1)
        with dve.Fori(0, ET // G) as i:
            for u in range(G):
                dve.wait_ge(sem["oh_free"], i * G + (u + 1))
                dve.tensor_scalar(oh[:, u % R, :], cx.iota_h[:], cx.src_f[:, bass.ds(i * G + u, 1)], None,
                                  ALU.is_equal).then_inc(sem["oh"], 1)
        dve.wait_ge(sem["sum"], 1)
        dve.tensor_copy(total[:].rearrange("p n m h -> p n (m h)"), sum_psum).then_inc(sem["total"], 1)
        dve.wait_ge(sem["total"], 1)
        dve.tensor_scalar(expo[:], total[:].bitcast(I32), 23, None, ALU.logical_shift_right
                          ).then_inc(sem["expo"], 1)
        dve.wait_ge(sem["expo"], 1)
        dve.tensor_scalar(cand[:], expo[:], -126.0, GUARD_T * LN2, ALU.add, ALU.mult).then_inc(sem["cand"], 1)
        dve.tensor_scalar(empty[:], expo[:], 0.5, -1e30, ALU.is_lt, ALU.mult).then_inc(sem["cand"], 1)
        dve.wait_ge(sem["cand"], 2)
        for m in range(M):
            dve.tensor_scalar(cand2[:, :, m, :], cand[:, :, m, :], -m * GUARD_STEP - GUARD_MARGIN, None, ALU.add
                              ).then_inc(sem["cand"], 1)
        dve.wait_ge(sem["cand"], M + 2)
        dve.tensor_tensor(cand3[:, :, 0:M - 1, :], cand2[:, :, 0:M - 1, :], empty[:, :, 0:M - 1, :], ALU.add
                          ).then_inc(sem["cand"], 1)
        dve.tensor_copy(cand3[:, :, M - 1, :], cand2[:, :, M - 1, :]).then_inc(sem["cand"], 1)
        dve.wait_ge(sem["cand"], M + 4)
        dve.tensor_reduce(best[:], cand3[:].rearrange("p n m h -> p n h m"), AX.X, ALU.max).then_inc(sem["best"], 1)
        dve.wait_ge(sem["best"], 1)
        dve.tensor_tensor(bound[:], best[:], top[:].unsqueeze(1).to_broadcast([P, NT, H0]), ALU.add
                          ).then_inc(sem["bound"], 1)
        dve.wait_ge(sem["bound"], 1)
        dve.tensor_copy(bound_hl[:, :, 0, :], bound[:]).then_inc(sem["hi"], 1)
        dve.wait_ge(sem["hi"], 1)
        dve.tensor_tensor(bound_hl[:, :, 1, :], bound[:], bound_hl[:, :, 0, :], ALU.subtract
                          ).then_inc(sem["lo"], 1)
        with dve.Fori(0, ET // R // 2) as i:
            for u in range(2):
                dve.wait_ge(sem["back"], i * 2 + (u + 1))
                for n in range(NT):
                    dve.tensor_scalar(ohT[:, u, n, :],
                                      st["src_row"][:, bass.ds(i * (2 * R * P) + u * R * P, R * P)],
                                      cx.part_f[:, n:n + 1], None, ALU.is_equal).then_inc(sem["ohT"], 1)
        dve.wait_ge(sem["eb"], ET // R + 2)
        dve.tensor_tensor(diff2[:], s[:], edge_bound[:, :, 0, :], ALU.subtract).then_inc(sem["d2"], 1)
        dve.wait_ge(sem["d2"], 1)
        dve.tensor_tensor(diff[:], diff2[:], edge_bound[:, :, 1, :], ALU.subtract).then_inc(sem["d3"], 1)
        dve.wait_ge(sem["p"], 1)
        dve.tensor_copy(p_hl[:, :, 0, :], p[:]).then_inc(sem["p_hl"], 1)
        dve.wait_ge(sem["p_hl"], 1)
        dve.tensor_tensor(p_hl[:, :, 1, :], p[:], p_hl[:, :, 0, :].bitcast(F32), ALU.subtract
                          ).then_inc(sem["p_hl"], 1)

        def low_part(i, u):
            dve.wait_ge(sem["pvhi"], i * G + (u + 1))
            dve.tensor_tensor(pv_lo[:, u % R, :], pv[:, u % R, :], pv_hi[:, u % R, :].bitcast(F32),
                              ALU.subtract).then_inc(sem["pvlo"], 1)

        with dve.Fori(0, ET // G) as i:
            for u in range(G):
                dve.wait_ge(sem["used"], i * G + (u + 1))
                dve.tensor_scalar(oh_r[:, u % R, :], cx.iota_h[:], cx.src_f[:, bass.ds(i * G + u, 1)], None,
                                  ALU.is_equal).then_inc(sem["ohr"], 1)
                dve.wait_ge(s_vg[u], i * 16 + 16)
                dve.tensor_tensor(pv[:, u % R, :].rearrange("p (h d) -> p h d", h=H0),
                                  vg[:, u, :].rearrange("p (h d) -> p h d", h=H0),
                                  p[:, bass.ds(i * G + u, 1), :].rearrange("p o h -> p h o").to_broadcast([P, H0, D0]),
                                  ALU.mult).then_inc(sem["pv"], 1)
                if u:
                    low_part(i, u - 1)
            low_part(i, G - 1)

    @block.scalar
    def _(act):
        for half in range(2):
            act.wait_ge(sem["arg"], M // 2 * (half + 1))
            ms = slice(half * M // 2, (half + 1) * M // 2)
            act.activation(w[:, :, ms, :].rearrange("p t m h -> p m t h"), args[half], ACT.Exp,
                           scale=1.0 / GUARD_T).then_inc(sem["w"], 1)
        with act.Fori(0, ET // R // 2) as i:
            for u in range(2):
                act.wait_ge(sem["back"], i * 2 + (u + 3))
                act.activation(edge_bound[:, bass.ds(i * (2 * R) + u * R, R)].rearrange("p t k h -> p (t k h)"),
                               ps[:, 2 + u, 0:R * 2 * H0], ACT.Copy).then_inc(sem["eb"], 1)
        act.wait_ge(sem["d3"], 1)
        act.activation(p[:], diff[:], ACT.Exp).then_inc(sem["p"], 1)
        act.wait_ge(sem["p_hl"], 2)
        with act.Fori(0, ET // R) as i:
            for u in range(R):
                act.wait_ge(sem["used"], i * R + (u + 1))
                act.activation(p_ring[:, u, 0:2 * H0],
                               p_hl[:, bass.ds(i * R + u, 1)].rearrange("p o k h -> p (o k h)"), ACT.Copy)
                act.wait_ge(sem["pv"], i * R + (u + 1))
                act.activation(pv_hi[:, u, :], pv[:, u, :], ACT.Copy).then_inc(sem["pvhi"], 1)

    @block.tensor
    def _(pe):
        pe.wait_ge(sem["pmax"], 1)
        pe.transpose(g_psum, pmax[:], cx.ident[:]).then_inc(sem["gT"], 1)
        pe.wait_ge(sem["gcol"], 1)
        pe.matmul(gb_psum, gcol[:].to_broadcast([H0, P]), cx.ident[0:H0, 0:H0], start=True, stop=True
                  ).then_inc(sem["gb"], 1)
        pe.matmul(ps[:, 1, :], cx.zero_r[:, 0:P], cx.zero_r[:], start=True, stop=False)
        pe.sem_inc(sem["oh_free"], R)
        pe.wait_ge(sem["w"], 2)
        with pe.Fori(0, ET // G) as i:
            for u in range(G):
                pe.wait_ge(sem["oh"], i * G + (u + 1))
                for n in range(NT):
                    m = pe.matmul(sum_psum[:, n, :], oh[:, u % R, n * P:(n + 1) * P],
                                  w[:, bass.ds(i * G + u, 1)].rearrange("p o m h -> p (o m h)"),
                                  start=False, stop=False)
                m.then_inc(sem["oh_free"], 1)
        pe.matmul(ps[:, 1, :], cx.zero_r[:, 0:P], cx.zero_r[:], start=False, stop=True
                  ).then_inc(sem["sum"], 1)
        pe.sem_inc(sem["back"], 2)
        pe.sem_inc(sem["eb"], 2)
        pe.wait_ge(sem["lo"], 1)
        with pe.Fori(0, ET // R // 2) as i:
            for u in range(2):
                pe.wait_ge(sem["eb"], i * 2 + (u + 1))
                pe.wait_ge(sem["ohT"], i * (2 * NT) + (u + 1) * NT)
                for t in range(R):
                    for n in range(NT):
                        m = pe.matmul(ps[:, 2 + u, t * 2 * H0:(t + 1) * 2 * H0], ohT[:, u, n, t * P:(t + 1) * P],
                                      bound_hl[:, n].rearrange("p k h -> p (k h)"),
                                      start=(n == 0), stop=(n == NT - 1))
                m.then_inc(sem["back"], 1)
        banks = [0] + [4 + n for n in range(NT)]
        for b in banks:
            pe.matmul(ps[:, b, :], cx.zero_r[:, 0:P], cx.zero_r[:], start=True, stop=False)
        pe.sem_inc(sem["used"], R)
        with pe.Fori(0, ET // G) as i:
            for u in range(G):
                pe.wait_ge(sem["ohr"], i * G + (u + 1))
                pe.wait_ge(sem["pvhi"], i * G + (u + 1))
                pe.matmul(ps[:, 0, :], p_ring[:, u % R, :], oh_r[:, u % R, :], start=False, stop=False)
                for n in range(NT):
                    pe.matmul(ps[:, 4 + n, :], oh_r[:, u % R, n * P:(n + 1) * P], pv_hi[:, u % R, :],
                              start=False, stop=False)
                pe.wait_ge(sem["pvlo"], i * G + (u + 1))
                for n in range(NT):
                    m = pe.matmul(ps[:, 4 + n, :], oh_r[:, u % R, n * P:(n + 1) * P], pv_lo[:, u % R, :],
                                  start=False, stop=False)
                m.then_inc(sem["used"], 1)
        for b in banks:
            pe.matmul(ps[:, b, :], cx.zero_r[:, 0:P], cx.zero_r[:], start=False, stop=True)

    tmp.close()
    cx.end_phase()


def gat1_weights(cx):
    return cx.wA[:, 0:2].rearrange("p a k n -> p (a k n)").rearrange("p (k n) -> p k n", k=CT)


def attention_out(cx, st):
    nc, io = cx.nc, cx.io
    tmp = ExitStack()
    den2 = cx.sb("den2", [P, NT, 2, H0], F32, tmp)
    den = cx.sb("den", [P, NT, H0], F32, tmp)
    rden = cx.sb("rden", [P, NT, H0], F32, tmp)
    att = cx.sb("att", [P, NT, C], F32, tmp)
    attT = cx.xT
    x1 = cx.sb("x1", [P, NT, C], F32, tmp)
    xb = cx.sb("xb", [P, NT, C], F32, tmp)
    z = cx.sb("z1", [P, NT, C], F32, tmp)
    zT = cx.xT
    hT = cx.sb("h0T", [P, HT, N], F32, tmp)
    denT = hT[0:2 * H0, 0, :]
    bo = cx.sb("bo_b", [P, C], F32, tmp)
    b2 = cx.sb("b20_b", [P, C], F32, tmp)
    cols = cx.sb("cols1", [P, 2, CT], F32, tmp)
    b1 = cx.sb("b10", [P, HT], F32, tmp)
    n1, n2 = Norm(cx, "n1", tmp), Norm(cx, "n2", tmp)
    ones = cx.sb("ones", [P, P], F32, tmp)
    names = ("ones", "deg", "degc", "trc", "penc", "small", "denT", "dtr", "den2", "den", "denm", "rden", "xb", "att", "tr", "attT", "wo", "x1", "tr2", "zT",
             "h", "hT", "ff", "xb2", "xb2b", "y")
    sem = {n: cx.sem("s2_" + n) for n in names}
    W1 = cx.wB[:, 0:CT * HID].rearrange("p (k n) -> p k n", k=CT)
    W2 = cx.wB[:, CT * HID:].rearrange("p (k n) -> p k n", k=HT)
    ps = cx.ps
    parts = cx.sb("parts1", [P, 16 * P * 2], F32R, tmp)
    split = Split(cx, "s2x", parts[:],
                  chunks([(attT[:, k, :], cx.wA[:, 3, k, :]) for k in range(CT)], 4)
                  + [step for half in range(2) for step in
                     chunks([(W1[:, k, half * C:(half + 1) * C], zT[:, k, :]) for k in range(CT)], 4 * (1 - half))]
                  + chunks([(hT[:, k, :], W2[:, k, :]) for k in range(HT)], 4))
    block = tmp.enter_context(nc.Block())

    @block.sync
    def _(sp):
        sp.dma_start(bo[:], row_b(io["L0_gnn_bo"])).then_inc(sem["small"], 16)
        sp.dma_start(b2[:], row_b(io["L0_gnn_b2"])).then_inc(sem["small"], 16)
        sp.dma_start(cols[:, 0, :], col(io["L0_gnn_ln2_g"], CT), allow_slow_non_contiguous=True).then_inc(sem["small"], 16)
        sp.dma_start(cols[:, 1, :], col(io["L0_gnn_ln2_b"], CT), allow_slow_non_contiguous=True).then_inc(sem["small"], 16)
        sp.dma_start(b1[:], col(io["L0_gnn_b1"], HT), allow_slow_non_contiguous=True).then_inc(sem["small"], 16)
        sp.dma_start(gat1_weights(cx), rows(io["L1_gnn_W1"])).then_inc(st["s_w2"], 16)

    @block.vector
    def _(dve):
        dve.memset(ones[:], 1.0).then_inc(sem["ones"], 1)
        dve.tensor_copy(denT, ps[0:2 * H0, 0, :]).then_inc(sem["denT"], 1)
        dve.wait_ge(sem["dtr"], 1)
        dve.tensor_copy(den2[:].rearrange("p n k h -> p (n k h)"), ps[:, 1, 0:NT * 2 * H0]).then_inc(sem["den2"], 1)
        dve.wait_ge(sem["den2"], 1)
        dve.tensor_tensor(den[:], den2[:, :, 0, :], den2[:, :, 1, :], ALU.add).then_inc(sem["den"], 1)
        dve.wait_ge(sem["den"], 1)
        dve.tensor_scalar(rden[:], den[:], 1e-37, None, ALU.max).then_inc(sem["denm"], 1)
        dve.wait_ge(sem["denm"], 1)
        dve.reciprocal(den[:], rden[:]).then_inc(sem["rden"], 1)
        dve.wait_ge(sem["rden"], 1)
        for n in range(NT):
            dve.tensor_tensor(att[:, n, :].rearrange("p (h d) -> p h d", h=H0),
                              ps[:, 4 + n, :].rearrange("p (h d) -> p h d", h=H0),
                              den[:, n, :].unsqueeze(2).to_broadcast([P, H0, D0]), ALU.mult).then_inc(sem["att"], 1)
        for c in range(1, CT, 2):
            dve.wait_ge(sem["tr"], c + 1)
            dve.tensor_copy(attT[:, c, :], ps[:, c, :]).then_inc(sem["attT"], 1)
        split.vector(dve, 0, CT)
        dve.wait_ge(sem["small"], 80)
        for n in range(NT):
            dve.tensor_tensor(xb[:, n, :], cx.x[:, n, :], bo[:], ALU.add).then_inc(sem["xb"], 1)
        dve.wait_ge(sem["xb"], NT)
        for n in range(NT):
            dve.wait_ge(sem["wo"], n + 1)
            dve.tensor_tensor(x1[:, n, :], ps[:, 4 + n, :], xb[:, n, :], ALU.add).then_inc(sem["x1"], 1)
        norm_vector(dve, n1, x1, z, sem["x1"])
        for c in range(1, CT, 2):
            dve.wait_ge(sem["tr2"], c + 1)
            dve.tensor_scalar(zT[:, c, :], ps[:, c, :], cols[:, 0, c:c + 1], cols[:, 1, c:c + 1],
                              ALU.mult, ALU.add).then_inc(sem["zT"], 1)
        dve.wait_ge(sem["penc"], NT)

        def x_plus_x1(n):
            dve.scalar_tensor_tensor(out=xb[:, n, :], in0=cx.x[:, n, :], scalar=1.0, in1=x1[:, n, :],
                                     op0=ALU.mult, op1=ALU.add).then_inc(sem["xb2"], 1)

        def plus_b2(n):
            dve.wait_ge(sem["xb2"], n + 1)
            dve.tensor_tensor(att[:, n, :], xb[:, n, :], b2[:], ALU.add).then_inc(sem["xb2b"], 1)

        def penalty(n):
            dve.tensor_scalar(cx.pen[:, n, :], cx.pen[:, n, :], 0.0, -BIG, ALU.is_equal, ALU.mult)

        split.vector(dve, CT, CT + 3)
        for n in range(NT):
            x_plus_x1(n)
            penalty(n)
            split.vector(dve, CT + 3 + n, CT + 4 + n)
        for n in range(NT):
            plus_b2(n)
            split.vector(dve, min(2 * CT + 3 + n, 3 * CT + 2), min(2 * CT + 4 + n, 3 * CT + 2))
        dve.wait_ge(sem["xb2b"], NT)
        split.vector(dve, 3 * CT + 2, 3 * CT + HT)
        for n in range(NT):
            dve.wait_ge(sem["ff"], n + 1)
            dve.tensor_tensor(x1[:, n, :], ps[:, 4 + n, :], att[:, n, :], ALU.add).then_inc(sem["y"], 1)
        norm_vector(dve, n2, x1, cx.x, sem["y"])

    @block.scalar
    def _(act):
        for c in range(0, CT, 2):
            act.wait_ge(sem["tr"], c + 1)
            act.activation(attT[:, c, :], ps[:, c, :], ACT.Copy).then_inc(sem["attT"], 1)
        act.wait_ge(sem["attT"], CT)
        split.scalar(act, 0, CT)
        act.wait_ge(sem["deg"], 1)
        act.activation(cx.rcount[:], ps[:, 0, :], ACT.Copy).then_inc(sem["degc"], 1)
        for n in range(NT):
            act.wait_ge(sem["trc"], n + 1)
            act.activation(cx.pen[:, n, :], ps[:, 1 + n, :], ACT.Copy).then_inc(sem["penc"], 1)
        norm_scalar(act, n1)
        act.wait_ge(sem["small"], 80)
        for c in range(0, CT, 2):
            act.wait_ge(sem["tr2"], c + 1)
            act.activation(zT[:, c, :], ps[:, c, :], ACT.Identity, bias=cols[:, 1, c:c + 1],
                           scale=cols[:, 0, c:c + 1]).then_inc(sem["zT"], 1)
        act.wait_ge(sem["zT"], CT)
        act.wait_ge(st["s_w1"], 32)
        split.scalar(act, CT, 2 * CT + 2)
        for m in range(HT):
            if m == NT:
                split.scalar(act, 2 * CT + 2, 3 * CT)
                act.wait_ge(sem["hT"], 2)
                split.scalar(act, 3 * CT, 3 * CT + 2)
            act.wait_ge(sem["h"], m + 1)
            act.activation(hT[:, m, :], ps[:, (4 + m) % 8, :], ACT.Silu, bias=b1[:, m:m + 1]).then_inc(sem["hT"], 1)
        act.wait_ge(sem["hT"], HT)
        split.scalar(act, 3 * CT + 2, 3 * CT + HT)
        norm_scalar(act, n2)

    @block.tensor
    def _(pe):
        pe.wait_ge(sem["denT"], 1)
        for n in range(NT):
            t = pe.transpose(ps[:, 1, n * 2 * H0:(n + 1) * 2 * H0], denT[:, n * P:(n + 1) * P],
                             cx.ident[0:2 * H0, 0:2 * H0])
        t.then_inc(sem["dtr"], 1)
        pe.wait_ge(sem["den2"], 1)
        transposes(pe, cx, att, CT, sem["att"], sem["tr"])
        split.tensor(pe, 0, CT, s_mm=sem["wo"])
        pe.wait_ge(sem["ones"], 1)
        product(pe, ps[:, 0, :], [(ones[:], cx.cnt[:, k, :]) for k in range(NT)]).then_inc(sem["deg"], 1)
        for n in range(NT):
            if n == NT - 1:
                pe.wait_ge(sem["x1"], 1)
            for c in range(NT):
                t = pe.transpose(ps[:, 1 + n, c * P:(c + 1) * P], cx.cnt[:, c, n * P:(n + 1) * P], cx.ident[:])
            t.then_inc(sem["trc"], 1)
        pe.wait_ge(sem["degc"], 1)
        pe.wait_ge(sem["penc"], NT)
        transposes(pe, cx, z, CT, n1.s_out, sem["tr2"])
        pe.wait_ge(sem["zT"], CT)
        split.tensor(pe, CT, 3 * CT, s_mm=sem["h"])
        pe.wait_ge(sem["hT"], NT)
        split.tensor(pe, 3 * CT, 3 * CT + HT, s_mm=sem["ff"])
        transposes(pe, cx, cx.x, CT, n2.s_out, st["s_xT1"])

    tmp.close()
    cx.end_phase()


def edge_sums(cx, st):
    nc, io = cx.nc, cx.io
    tmp = ExitStack()
    R, U = 4, 8
    ea = cx.sb("ea", [P, ET, EA], F32, tmp)
    ea_hl = cx.sb("ea_hl", [P, R, 2, EA], F32R, tmp)
    oh_s = cx.sb("oh_s", [P, R, N], F32R, tmp)
    oh_d = cx.sb("oh_d", [P, R, N], F32R, tmp)
    ident_b = cx.sb("ident_b", [P, P], BF16, tmp)
    names = ("ea", "const", "hi", "lo", "ohs", "ohd", "used", "tr", "eaT", "mm", "cnt")
    sem = {n: cx.sem("s3_" + n) for n in names}
    ps = cx.ps
    block = tmp.enter_context(nc.Block())

    @block.sync
    def _(sp):
        sp.dma_start(ea[:], io["edge_attr_64"].rearrange("(p t) f -> p t f", p=P)).then_inc(sem["ea"], 16)
        sp.dma_start(st["bias"][:], io["edge_attr_8"].rearrange("(p t) h -> p t h", p=P)).then_inc(st["s_bias"], 16)
        for s in st["s_st"]:
            sp.wait_ge(s, 16 * NT // 2)
        sp.dma_start(cx.wB[:, 0:CT * HID].rearrange("p (k n) -> p k n", k=CT), rows(io["L0_gnn_W1"])
                     ).then_inc(st["s_w1"], 16)
        sp.dma_start(cx.wB[:, CT * HID:].rearrange("p (k n) -> p k n", k=HT), rows(io["L0_gnn_W2"])
                     ).then_inc(st["s_w1"], 16)

    @block.gpsimd
    def _(pool):
        for s in st["s_st"]:
            pool.wait_ge(s, 16 * NT // 2)
        for t in range(ET):
            pool.indirect_dma_start(st["sg"][:, t, :], None, st["s_dram"],
                                    Offset(ap=st["pair_i"][:, t:t + 1], axis=0)).then_inc(st["s_sg"], 16)

    @block.vector
    def _(dve):
        dve.tensor_copy(ident_b[:], cx.ident[:]).then_inc(sem["const"], 1)
        dve.wait_ge(sem["ea"], 16)
        with dve.Fori(0, ET // U) as i:
            for u in range(U):
                t = i * U + u
                dve.wait_ge(sem["used"], i * U + (u + 1))
                for oh, nodes, done in ((oh_d, cx.dst_f, "ohd"), (oh_s, cx.src_f, "ohs")):
                    dve.tensor_scalar(oh[:, u % R, :], cx.iota_h[:], nodes[:, bass.ds(t, 1)], None,
                                      ALU.is_equal).then_inc(sem[done], 1)
                dve.wait_ge(sem["hi"], i * U + (u + 1))
                dve.tensor_tensor(ea_hl[:, u % R, 1, :], ea[:, bass.ds(t, 1), :].rearrange("p o f -> p (o f)"),
                                  ea_hl[:, u % R, 0, :].bitcast(F32), ALU.subtract).then_inc(sem["lo"], 1)
        dve.wait_ge(sem["mm"], 1)
        for n in range(NT):
            dve.tensor_copy(cx.cnt[:, n, :], ps[:, n, :]).then_inc(sem["cnt"], 1)
        dve.tensor_copy(cx.ea_mean[:], ps[:, 4, :])

    @block.scalar
    def _(act):
        def transposed(i, u):
            act.wait_ge(sem["tr"], i * U + (u + 1))
            act.activation(cx.eaT[:, bass.ds(i * (U * P) + u * P, P)], ps[:, 5 + u % 2, 0:P], ACT.Copy
                           ).then_inc(sem["eaT"], 1)

        act.wait_ge(sem["ea"], 16)
        with act.Fori(0, ET // U) as i:
            for u in range(U):
                act.wait_ge(sem["used"], i * U + (u + 1))
                act.activation(ea_hl[:, u % R, 0, :], ea[:, bass.ds(i * U + u, 1), :].rearrange("p o f -> p (o f)"),
                               ACT.Copy).then_inc(sem["hi"], 1)
                if u >= 1:
                    transposed(i, u - 1)
            transposed(i, U - 1)

    @block.tensor
    def _(pe):
        for b in range(NT + 1):
            pe.matmul(ps[:, b, :], cx.zero_r[:, 0:P], cx.zero_r[:], start=True, stop=False)
        pe.sem_inc(sem["eaT"], 2)
        pe.sem_inc(sem["used"], R)
        with pe.Fori(0, ET // U) as i:
            for u in range(U):
                pe.wait_ge(sem["lo"], i * U + (u + 1))
                pe.wait_ge(sem["eaT"], i * U + (u + 1))
                pe.transpose(ps[:, 5 + u % 2, 0:P], ea_hl[:, u % R].rearrange("p k f -> p (k f)").bitcast(F32),
                             cx.ident[:]).then_inc(sem["tr"], 1)
                pe.matmul(ps[:, 4, :], ea_hl[:, u % R].rearrange("p k f -> p (k f)"), oh_d[:, u % R, :],
                          start=False, stop=False)
                for n in range(NT):
                    m = pe.matmul(ps[:, n, :], oh_s[:, u % R, n * P:(n + 1) * P], oh_d[:, u % R, :],
                                  start=False, stop=False)
                m.then_inc(sem["used"], 1)
        pe.wait_ge(sem["const"], 1)
        for n in range(NT):
            pe.matmul(ps[:, n, n * P:(n + 1) * P], ident_b[:], ident_b[:], start=False, stop=False)
        for b in range(NT + 1):
            m = pe.matmul(ps[:, b, :], cx.zero_r[:, 0:P], cx.zero_r[:], start=False, stop=True)
        m.then_inc(sem["mm"], 1)

    tmp.close()
    cx.end_phase()


W_ = C1 + 4


def gat_output(h_mem):
    return h_mem[:, 0:HT * N].rearrange("p (k n) -> p k n", k=HT)


def gat(cx, st, tag, W, kt, xT, h_mem, spare, a_src, a_dst, b, s_w, w_count, x_in):
    nc, io = cx.nc, cx.io
    tmp = ExitStack()
    h = h_mem[:].rearrange("p (n q c) -> p n q c", n=NT, q=H1)
    outT = gat_output(h_mem)
    al_b = spare[:, 0:H1 * N].rearrange("p (q n) -> p q n", q=H1)
    o = W.rearrange("p k n -> p (k n)")[:, 0:NT * HID].rearrange("p (n c) -> p n c", n=NT)
    b_c = cx.sb(tag + "b_c", [P, HT], F32, tmp)
    al = cx.sb(tag + "al", [P, NT, 2, H1], F32, tmp)
    als2 = cx.sb(tag + "als2", [P, NT, H1], F32, tmp)
    junk_al = cx.sb(tag + "junk_al", [P, 2, C1], F32, tmp)
    junk = cx.sb(tag + "junk", [P, 2, N], F32, tmp)
    mx = cx.sb(tag + "mx", [P, NT, H1], F32, tmp)
    zmax = cx.sb(tag + "zmax", [P, NT, H1], F32, tmp)
    emax = cx.sb(tag + "emax", [P, NT, H1], F32, tmp)
    dd = cx.sb(tag + "dd", [P, 2, NT, H1], F32, tmp)
    first = ExitStack()
    parts = cx.sb(tag + "parts", [P, 8 * C], F32R, first)
    first.close()
    ex = cx.sb(tag + "ex", [P, 2, 2, N], F32, tmp)
    pm = cx.sb(tag + "pm", [P, 2, N], F32, tmp)
    pr = cx.sb(tag + "pr", [P, 2, NT, N], F32, tmp)
    a_b = pr[:, 1].rearrange("p (a k) c -> p a (k c)", a=2)
    rd = cx.sb(tag + "rd", [P, NT * H1], F32, tmp)
    split = Split(cx, tag + "x", parts[:], [
        step for half in range(2) for step in
        chunks([(xT[:, k, :], W[:, k, half * C:(half + 1) * C]) for k in range(kt)], 4 * half)])
    names = ("small", "count", "ones", "xT", "mm", "h", "al", "als2", "asb", "asc", "mx", "z", "emax", "dd", "db",
             "ex1", "ex2", "pm", "p", "agg", "rd", "o", "tr2", "oT")
    sem = {n: cx.sem(tag + "_" + n) for n in names}
    ps = cx.ps
    block = tmp.enter_context(nc.Block())

    @block.sync
    def _(sp):
        sp.dma_start(a_b[:, 0, :], row_b(a_src.rearrange("h c -> (h c)"))).then_inc(sem["small"], 16)
        sp.dma_start(a_b[:, 1, :], row_b(a_dst.rearrange("h c -> (h c)"))).then_inc(sem["small"], 16)
        sp.dma_start(b_c[:], col(b, HT), allow_slow_non_contiguous=True).then_inc(sem["small"], 16)
        if x_in is not None:
            sp.dma_start(cx.wB[:].rearrange("p (k n) -> p k n", k=HT), rows(io["L1_gnn_W2"])
                         ).then_inc(st["s_w3"], 16)
            sp.dma_start(cx.wA[:, 2:4].rearrange("p a k n -> p (a k) n"), rows(io["L1_gnn_Wfc"])
                         ).then_inc(st["s_w4"], 16)

    @block.vector
    def _(dve):
        dve.memset(h[:, :, :, C1:W_], 1.0).then_inc(sem["ones"], 1)
        if x_in is not None:
            for c in range(1, kt, 2):
                dve.wait_ge(st["s_xT1"], c + 1)
                dve.tensor_copy(xT[:, c, :], ps[:, c, :]).then_inc(sem["xT"], 1)
        split.vector(dve, 0, kt + 2)
        dve.wait_ge(sem["small"], 48)

        def logits(half, tiles=range(NT)):
            for n in tiles:
                if half == 0 and n:
                    split.vector(dve, min(kt + 1 + n, 2 * kt), min(kt + 2 + n, 2 * kt))
                dve.wait_ge(sem["h"], half * NT + n + 1)
                for q in (2 * half, 2 * half + 1):
                    for k in range(2):
                        i = ((half * NT + n) * 2 + q % 2) * 2 + k
                        if i >= 2:
                            dve.wait_ge(sem["al"], i - 1)
                        dve.tensor_tensor_reduce(out=junk_al[:, i % 2, :], in0=h[:, n, q, 0:C1],
                                                 in1=a_b[:, k, q * C1:(q + 1) * C1], scale=1.0, scalar=0.0,
                                                 op0=ALU.mult, op1=ALU.add, accum_out=al[:, n, k, q:q + 1]
                                                 ).then_inc(sem["al"], 1)
            if NT - 1 not in tiles:
                return
            heads = slice(2 * half, 2 * half + 2)
            dve.wait_ge(sem["al"], 2 * NT * 2 * (half + 1))
            dve.tensor_scalar(als2[:, :, heads], al[:, :, 0, heads], 0.2, None, ALU.mult).then_inc(sem["als2"], 1)

        def largest(q):
            dve.wait_ge(sem["asc"], q + 1)
            for n in range(NT):
                i = q * NT + n
                if i >= 2:
                    dve.wait_ge(sem["mx"], i - 1)
                dve.tensor_tensor_reduce(out=junk[:, i % 2, :], in0=cx.pen[:, n, :], in1=al_b[:, q, :], scale=1.0,
                                         scalar=-BIG, op0=ALU.add, op1=ALU.max,
                                         accum_out=mx[:, n, q:q + 1]).then_inc(sem["mx"], 1)
            dve.wait_ge(sem["mx"], NT * (q + 1))
            dve.tensor_tensor(zmax[:, :, q], mx[:, :, q], al[:, :, 1, q], ALU.add).then_inc(sem["z"], 1)
            dve.wait_ge(sem["z"], q + 1)
            dve.scalar_tensor_tensor(out=emax[:, :, q], in0=zmax[:, :, q], scalar=0.2, in1=zmax[:, :, q],
                                     op0=ALU.mult, op1=ALU.max).then_inc(sem["emax"], 1)
            dve.wait_ge(sem["emax"], q + 1)
            dve.tensor_tensor(dd[:, 0, :, q], al[:, :, 1, q], emax[:, :, q], ALU.subtract).then_inc(sem["dd"], 1)
            dve.scalar_tensor_tensor(out=dd[:, 1, :, q], in0=al[:, :, 1, q], scalar=0.2, in1=emax[:, :, q],
                                     op0=ALU.mult, op1=ALU.subtract).then_inc(sem["dd"], 1)

        def numerators(q, s):
            i = q * NT + s
            dve.wait_ge(sem["ex2"], i + 1)
            if i >= 2:
                dve.wait_ge(sem["p"], i - 1)
            dve.scalar_tensor_tensor(out=pm[:, i % 2, :], in0=ex[:, i % 2, 0, :], scalar=1.0,
                                     in1=ex[:, i % 2, 1, :], op0=ALU.min, op1=ALU.max).then_inc(sem["pm"], 1)
            if q >= 2 and s == 0:
                dve.wait_ge(sem["agg"], NT * (q - 1))
            dve.wait_ge(sem["pm"], i + 1)
            dve.scalar_tensor_tensor(out=pr[:, q % 2, s, :], in0=pm[:, i % 2, :], scalar=1.0,
                                     in1=cx.cnt[:, s, :], op0=ALU.min, op1=ALU.mult).then_inc(sem["p"], 1)

        def outputs(q, n):
            i = q * NT + n
            dve.wait_ge(sem["agg"], i + 1)
            dve.reciprocal(rd[:, i:i + 1], ps[:, n, C1:C1 + 1]).then_inc(sem["rd"], 1)

        logits(0)
        split.vector(dve, min(kt + 1 + NT, 2 * kt), 2 * kt)
        logits(1, range(2))
        largest(0)
        logits(1, range(2, NT))
        for q in range(H1):
            if q + 1 < H1:
                largest(q + 1)
            for s in range(NT):
                numerators(q, s)
            if q:
                for n in range(NT):
                    outputs(q - 1, n)
        if x_in is None:
            dve.wait_ge(sem["mx"], NT * H1)
            dve.tensor_scalar(junk[:, 0, :], cx.rcount[:], -1.0, 1.0, ALU.add, ALU.max).then_inc(sem["count"], 1)
            dve.wait_ge(sem["count"], 1)
            dve.reciprocal(cx.rcount[:], junk[:, 0, :]).then_inc(sem["count"], 1)
            dve.wait_ge(sem["count"], 2)
            dve.tensor_tensor(cx.ea_mean[:], cx.ea_mean[:], cx.rcount[:], ALU.mult)
        for n in range(NT):
            outputs(H1 - 1, n)
        for c in range(1, HT, 2):
            dve.wait_ge(sem["tr2"], c + 1)
            dve.tensor_scalar(outT[:, c, :], ps[:, c, :], b_c[:, c:c + 1], 0.0, ALU.add, ALU.max
                              ).then_inc(sem["oT"], 1)

    @block.scalar
    def _(act):
        act.wait_ge(s_w, w_count)
        if x_in is not None:
            for c in range(0, kt, 2):
                act.wait_ge(st["s_xT1"], c + 1)
                act.activation(xT[:, c, :], ps[:, c, :], ACT.Copy).then_inc(sem["xT"], 1)
            act.wait_ge(sem["xT"], kt)
        split.scalar(act, 0, kt + 2)
        for i in range(NT * 2):
            half, n = i // NT, i % NT
            if i == NT:
                split.scalar(act, kt + 2, 2 * kt)
            act.wait_ge(sem["mm"], i + 1)
            act.activation(h[:, n, 2 * half:2 * half + 2, 0:C1],
                           ps[:, i, :].rearrange("p (q c) -> p q c", q=2), ACT.Copy).then_inc(sem["h"], 1)

        def al_src(q):
            act.wait_ge(sem["asb"], q + 1)
            act.activation(al_b[:, q, :], ps[:, q, :], ACT.Copy).then_inc(sem["asc"], 1)

        al_src(0)
        al_src(1)

        def outputs(q):
            for n in range(NT):
                i = q * NT + n
                act.wait_ge(sem["rd"], i + 1)
                act.activation(o[:, n, q * C1:(q + 1) * C1], ps[:, n, 0:C1], ACT.Copy, scale=rd[:, i:i + 1]
                               ).then_inc(sem["o"], 1)

        for q in range(H1):
            act.wait_ge(sem["als2"], q // 2 + 1)
            if q >= 2:
                outputs(q - 2)
            if q == 1:
                al_src(2)
                al_src(3)
            for s in range(NT):
                i = q * NT + s
                bank = 4 + 2 * (q % 2)
                act.wait_ge(sem["db"], 2 * (q + 1))
                if i >= 2:
                    act.wait_ge(sem["pm"], i - 1)
                act.activation(ex[:, i % 2, 0, :], ps[:, bank, :], ACT.Exp, bias=al[:, s, 0, q:q + 1]
                               ).then_inc(sem["ex1"], 1)
                act.wait_ge(sem["ex1"], i + 1)
                act.activation(ex[:, i % 2, 1, :], ps[:, bank + 1, :], ACT.Exp, bias=als2[:, s, q:q + 1]
                               ).then_inc(sem["ex2"], 1)
        outputs(H1 - 2)
        outputs(H1 - 1)
        act.wait_ge(sem["small"], 48)
        for c in range(0, HT, 2):
            act.wait_ge(sem["tr2"], c + 1)
            act.activation(outT[:, c, :], ps[:, c, :], ACT.Relu, bias=b_c[:, c:c + 1]).then_inc(sem["oT"], 1)

    @block.tensor
    def _(pe):
        if x_in is not None:
            pe.wait_ge(sem["xT"], kt)
        split.tensor(pe, 0, 2 * kt, s_mm=sem["mm"])

        def spread(bank, column, done):
            for n in range(NT):
                m = pe.matmul(ps[:, bank, n * P:(n + 1) * P], column(n).to_broadcast([P, P]), cx.ident[:],
                              start=True, stop=True)
            m.then_inc(done, 1)

        pe.wait_ge(sem["als2"], 1)
        for q in range(2):
            spread(q, lambda n: al[:, n, 0, q:q + 1], sem["asb"])

        def spread_dst(q):
            if q >= 2:
                pe.wait_ge(sem["ex2"], NT * (q - 1))
            pe.wait_ge(sem["dd"], 2 * (q + 1))
            for k in range(2):
                spread(4 + 2 * (q % 2) + k, lambda n: dd[:, k, n, q:q + 1], sem["db"])

        pe.wait_ge(sem["ones"], 1)
        spread_dst(0)
        pe.wait_ge(sem["als2"], 2)
        for q in range(2, H1):
            spread(q, lambda n: al[:, n, 0, q:q + 1], sem["asb"])
        pe.wait_ge(sem["asc"], H1)
        for q in range(H1):
            if q + 1 < H1:
                spread_dst(q + 1)
            pe.wait_ge(sem["p"], NT * (q + 1))
            for n in range(NT):
                if q:
                    pe.wait_ge(sem["o"], NT * (q - 1) + n + 1)
                product(pe, ps[:, n, 0:C1 + 2],
                        [(pr[:, q % 2, s, n * P:(n + 1) * P], h[:, s, q, 0:C1 + 2]) for s in range(NT)]
                        ).then_inc(sem["agg"], 1)
        pe.wait_ge(sem["o"], NT * H1)
        transposes(pe, cx, o, HT, None, sem["tr2"])

    tmp.close()
    cx.end_phase()


def gat_out(cx, st, hT):
    nc, io = cx.nc, cx.io
    tmp = ExitStack()
    bfc = cx.sb("bfc_b", [P, C], F32, tmp)
    xb = cx.sb("xb1", [P, NT, C], F32, tmp)
    y = cx.sb("y1", [P, NT, C], F32, tmp)
    norm = Norm(cx, "n3", tmp)
    s_small, s_xb, s_mm, s_y = (cx.sem("s5_" + n) for n in ("small", "xb", "mm", "y"))
    Wfc = cx.wA[:, 2:4].rearrange("p a k n -> p (a k) n")
    ps = cx.ps
    parts = cx.sb("parts5", [P, 8 * C], F32R, tmp)
    split = Split(cx, "s5x", parts[:], chunks([(hT[:, k, :], Wfc[:, k, :]) for k in range(HT)], 4))
    block = tmp.enter_context(nc.Block())

    @block.sync
    def _(sp):
        sp.dma_start(bfc[:], row_b(io["L1_gnn_bfc"])).then_inc(s_small, 16)
        sp.dma_start(cx.wB[:, 0:CT * HID].rearrange("p (k n) -> p k n", k=CT), rows(io["L2_gnn_W1"][0:C, :])
                     ).then_inc(st["s_w5"], 16)
        sp.dma_start(cx.wB[:, CT * HID:].rearrange("p (k n) -> p k n", k=HT), rows(io["L2_gnn_W2"])
                     ).then_inc(st["s_w5"], 16)

    @block.vector
    def _(dve):
        split.vector(dve, 0, 4)
        dve.wait_ge(s_small, 16)
        for n in range(NT):
            dve.tensor_tensor(xb[:, n, :], cx.x[:, n, :], bfc[:], ALU.add).then_inc(s_xb, 1)
        split.vector(dve, 4, HT)
        dve.wait_ge(s_xb, NT)
        for n in range(NT):
            dve.wait_ge(s_mm, n + 1)
            dve.tensor_tensor(y[:, n, :], ps[:, 4 + n, :], xb[:, n, :], ALU.add).then_inc(s_y, 1)
        norm_vector(dve, norm, y, cx.x, s_y)

    @block.scalar
    def _(act):
        act.wait_ge(st["s_w4"], 16)
        split.scalar(act, 0, HT)
        norm_scalar(act, norm)

    @block.tensor
    def _(pe):
        split.tensor(pe, 0, HT, s_mm=s_mm)
        transposes(pe, cx, cx.x, CT, norm.s_out, st["s_xT2"])

    tmp.close()
    cx.end_phase()


def residual_layer(cx, st):
    nc, io = cx.nc, cx.io
    tmp = ExitStack()
    W1e = cx.sb("W1e", [P, HID], F32, tmp)
    b1 = cx.sb("b12", [P, HT], F32, tmp)
    b2 = cx.sb("b22_b", [P, C], F32, tmp)
    hT = cx.sb("h2T", [P, HT, N], F32, tmp)
    xb = cx.sb("xb2", [P, NT, C], F32, tmp)
    y = cx.sb("y2", [P, NT, C], F32, tmp)
    norm = Norm(cx, "n4", tmp)
    names = ("small", "w", "xT", "h", "hT", "xb", "mm", "y")
    sem = {n: cx.sem("s6_" + n) for n in names}
    W1 = cx.wB[:, 0:CT * HID].rearrange("p (k n) -> p k n", k=CT)
    W2 = cx.wB[:, CT * HID:].rearrange("p (k n) -> p k n", k=HT)
    ps = cx.ps
    parts = cx.sb("parts6", [P, 8 * C], F32R, tmp)
    split = Split(cx, "s6x", parts[:],
                  [step for half in range(2) for step in
                   chunks([(W1[:, k, half * C:(half + 1) * C], cx.xT[:, k, :]) for k in range(CT)]
                          + [(W1e[:, half * C:(half + 1) * C], cx.ea_mean[:])], 4 * (1 - half))]
                  + chunks([(hT[:, k, :], W2[:, k, :]) for k in range(HT)], 4))
    n1 = 2 * (CT + 1)
    block = tmp.enter_context(nc.Block())

    @block.sync
    def _(sp):
        for k in range(2):
            sp.dma_start(W1e[k * EA:(k + 1) * EA, :], io["L2_gnn_W1"][C:C + EA, :]).then_inc(sem["w"], 16)
        sp.dma_start(b1[:], col(io["L2_gnn_b1"], HT), allow_slow_non_contiguous=True).then_inc(sem["small"], 16)
        sp.dma_start(b2[:], row_b(io["L2_gnn_b2"])).then_inc(sem["small"], 16)
        sp.dma_start(cx.wA[:].rearrange("p a k n -> p (a k) n")[:, 0:2 * CT, :],
                     rows(io["L3_gnn_W1"][0:C * 2, :])).then_inc(st["s_w6"], 16)

    @block.vector
    def _(dve):
        for c in range(1, CT, 2):
            dve.wait_ge(st["s_xT2"], c + 1)
            dve.tensor_copy(cx.xT[:, c, :], ps[:, c, :]).then_inc(sem["xT"], 1)
        split.vector(dve, 0, 4)
        dve.wait_ge(sem["small"], 32)
        for n in range(NT):
            dve.scalar_tensor_tensor(out=xb[:, n, :], in0=cx.x[:, n, :], scalar=2.0, in1=b2[:], op0=ALU.mult,
                                     op1=ALU.add).then_inc(sem["xb"], 1)
        split.vector(dve, 4, n1 + 2)
        dve.wait_ge(sem["xb"], NT)
        split.vector(dve, n1 + 2, n1 + HT)
        for n in range(NT):
            dve.wait_ge(sem["mm"], n + 1)
            dve.tensor_tensor(y[:, n, :], ps[:, 4 + n, :], xb[:, n, :], ALU.add).then_inc(sem["y"], 1)
        norm_vector(dve, norm, y, cx.x, sem["y"])

    @block.scalar
    def _(act):
        for c in range(0, CT, 2):
            act.wait_ge(st["s_xT2"], c + 1)
            act.activation(cx.xT[:, c, :], ps[:, c, :], ACT.Copy).then_inc(sem["xT"], 1)
        act.wait_ge(sem["xT"], CT)
        act.wait_ge(sem["w"], 32)
        act.wait_ge(st["s_w5"], 32)
        split.scalar(act, 0, CT + 3)
        act.wait_ge(sem["small"], 32)
        for m in range(HT):
            if m == NT:
                split.scalar(act, CT + 3, n1)
                act.wait_ge(sem["hT"], 2)
                split.scalar(act, n1, n1 + 2)
            act.wait_ge(sem["h"], m + 1)
            act.activation(hT[:, m, :], ps[:, (4 + m) % 8, :], ACT.Relu, bias=b1[:, m:m + 1]).then_inc(sem["hT"], 1)
        act.wait_ge(sem["hT"], HT)
        split.scalar(act, n1 + 2, n1 + HT)
        norm_scalar(act, norm)

    @block.tensor
    def _(pe):
        pe.wait_ge(sem["xT"], CT)
        split.tensor(pe, 0, n1, s_mm=sem["h"])
        pe.wait_ge(sem["hT"], NT)
        split.tensor(pe, n1, n1 + HT, s_mm=sem["mm"])
        transposes(pe, cx, cx.x, CT, norm.s_out, st["s_xT3"])

    tmp.close()
    cx.end_phase()


def edge_weights(cx):
    return (cx.wB[:, 0:CT * C].rearrange("p (k n) -> p k n", k=CT), cx.wB[:, CT * C:(CT + 1) * C])


def edge_mlp_nodes(cx, st):
    nc, io = cx.nc, cx.io
    tmp = ExitStack()
    W = cx.wA[:].rearrange("p a k n -> p (a k) n")
    b1 = cx.sb("b13_b", [P, C], F32, tmp)
    out = cx.sb("xab", [P, 2, NT, C], F32, tmp)
    names = ("small", "xT", "mm", "out", "dram")
    sem = {n: cx.sem("s7_" + n) for n in names}
    ps = cx.ps
    parts = cx.sb("parts7", [P, 8 * C], F32R, tmp)
    split = Split(cx, "s7x", parts[:], [step for k in range(2) for step in
                                        chunks([(cx.xT[:, c, :], W[:, k * CT + c, :]) for c in range(CT)], 4 * (1 - k))])
    block = tmp.enter_context(nc.Block())

    @block.sync
    def _(sp):
        sp.dma_start(b1[:], row_b(io["L3_gnn_b1"])).then_inc(sem["small"], 16)
        sp.dma_start(edge_weights(cx)[0], rows(io["L3_gnn_W2"])).then_inc(st["s_w7"], 16)
        for k in range(2):
            sp.dma_start(edge_weights(cx)[1][k * EA:(k + 1) * EA, :], io["L3_gnn_W1"][2 * C:2 * C + EA, :]
                         ).then_inc(st["s_w7"], 16)
        for k, dram in enumerate((st["xa_dram"], st["xb_dram"])):
            sp.wait_ge(sem["out"], NT * (k + 1))
            sp.dma_start(dram.rearrange("(n p) c -> p n c", p=P), out[:, k]).then_inc(sem["dram"], 16)
        sp.wait_ge(sem["dram"], 32)

    @block.vector
    def _(dve):
        for c in range(1, CT, 2):
            dve.wait_ge(st["s_xT3"], c + 1)
            dve.tensor_copy(cx.xT[:, c, :], ps[:, c, :]).then_inc(sem["xT"], 1)
        split.vector(dve, 0, CT + 2)
        dve.wait_ge(sem["small"], 16)
        for i in range(2 * NT):
            k, n = i // NT, i % NT
            if i == NT:
                split.vector(dve, CT + 2, 2 * CT)
            dve.wait_ge(sem["mm"], i + 1)
            if k == 0:
                dve.tensor_tensor(out[:, k, n, :], ps[:, (4 + i) % 8, :], b1[:], ALU.add).then_inc(sem["out"], 1)
            else:
                dve.tensor_copy(out[:, k, n, :], ps[:, (4 + i) % 8, :]).then_inc(sem["out"], 1)

    @block.scalar
    def _(act):
        for c in range(0, CT, 2):
            act.wait_ge(st["s_xT3"], c + 1)
            act.activation(cx.xT[:, c, :], ps[:, c, :], ACT.Copy).then_inc(sem["xT"], 1)
        act.wait_ge(sem["xT"], CT)
        act.wait_ge(st["s_w6"], 16)
        split.scalar(act, 0, 2 * CT)

    @block.tensor
    def _(pe):
        pe.wait_ge(sem["xT"], CT)
        split.tensor(pe, 0, 2 * CT, s_mm=sem["mm"])

    tmp.close()
    cx.end_phase()


def edge_mlp(cx, st):
    nc, io = cx.nc, cx.io
    tmp = ExitStack()
    B = 2
    NB = ET // B
    W2h = cx.sb("W2h", [P, CT, C], F32R, tmp)
    W2l = cx.sb("W2l", [P, CT, C], F32R, tmp)
    Wch = cx.sb("Wch", [P, C], F32R, tmp)
    Wcl = cx.sb("Wcl", [P, C], F32R, tmp)
    b2 = cx.sb("b23_b", [P, C], F32, tmp)
    g = cx.sb("g", [P, 2, B, 2, C], F32, tmp)
    x1 = cx.wB[:, 0:2048].rearrange("p (r c e) -> p r c e", r=2, c=CT)
    x2 = cx.wB[:, 2048:4096].rearrange("p (r u c) -> p r u c", r=2, u=B)
    q = cx.sb("q", [P, 2, CT * B * P], F32, tmp)
    t = cx.wB[:, 4096:8192].rearrange("p (r k e) -> p r k e", r=2, k=2)
    f = cx.wA[:, 3].rearrange("p k c -> p (k c)").rearrange("p (a e) -> p a e", a=2)
    W2f, Wcf = edge_weights(cx)
    hh = cx.sb("hh", [P, 2, CT, B * P], F32R, tmp)
    hl = cx.sb("hl", [P, 2, CT, B * P], F32R, tmp)
    mh = cx.sb("mh", [P, 2, B, C], F32R, tmp)
    ml = cx.sb("ml", [P, 2, B, C], F32R, tmp)
    oh = cx.sb("oh3", [P, 2, B, N], F32R, tmp)
    names = ("w", "gsum", "wch", "wcl", "wh", "wl", "pre", "x1", "w2", "x2", "q1", "q2", "a1", "a2", "t1", "t2", "h", "m", "hh", "mh",
             "hl", "ml", "oh", "sum")
    sem = {n: cx.sem("s8_" + n) for n in names}
    s_g = [cx.sem(f"s8_g{i}") for i in range(2 * B * 2)]
    ps = cx.ps
    block = tmp.enter_context(nc.Block())

    def rounds(engine, body):
        for k in range(-3, 1):
            body(k, k % 2, lambda a, c: a * k + c, {s for s, (lo, hi) in SPAN.items() if lo <= k <= hi})
        first, last = 1, NB - 4
        assert (last - first + 1) % 2 == 0
        with engine.Fori(0, (last - first + 1) // 2) as j:
            for v in range(2):
                k0 = first + v
                body(k0, k0 % 2, lambda a, c, k0=k0: j * (2 * a) + (a * k0 + c), set(SPAN))
        for k in range(last + 1, NB + 1):
            body(k, k % 2, lambda a, c: a * k + c, {s for s, (lo, hi) in SPAN.items() if lo <= k <= hi})

    SPAN = {"pre": (-3, NB - 4), "mish1": (-2, NB - 3), "second": (-1, NB - 2), "mish2": (0, NB - 1),
            "sum": (1, NB)}

    @block.sync
    def _(sp):
        sp.dma_start(b2[:], row_b(io["L3_gnn_b2"])).then_inc(sem["w"], 16)
        sp.wait_ge(sem["h"], 1)
        sp.dma_start(cx.wA[:].rearrange("p a k n -> p (a k) n")[:, 0:2 * CT, :], rows(io["L3_gnn_W3"])
                     ).then_inc(st["s_w8"], 16)
        sp.dma_start(cx.wA[:].rearrange("p a k n -> p (a k) n")[:, 2 * CT:3 * CT, :], rows(io["L3_gnn_W4"])
                     ).then_inc(st["s_w8"], 16)

    @block.gpsimd
    def _(pool):
        def add(b):
            for u in range(B):
                for k in range(2):
                    pool.wait_ge(s_g[((b % 2) * B + u) * 2 + k], 16 * (b // 2 + 1))
                pool.tensor_tensor(g[:, b % 2, u, 0, :], g[:, b % 2, u, 0, :], g[:, b % 2, u, 1, :], ALU.add
                                   ).then_inc(sem["gsum"], 1)

        for b in range(NB):
            if b >= 2:
                pool.wait_ge(sem["pre"], 2 * (b - 1))
            for u in range(B):
                for k, (dram, idx) in enumerate(((st["xa_dram"], cx.src_i), (st["xb_dram"], cx.dst_i))):
                    tile = b * B + u
                    pool.indirect_dma_start(g[:, b % 2, u, k, :], None, dram,
                                            Offset(ap=idx[:, tile:tile + 1], axis=0)
                                            ).then_inc(s_g[((b % 2) * B + u) * 2 + k], 16)
            if b:
                add(b - 1)
        add(NB - 1)

    @block.vector
    def _(dve):
        dve.wait_ge(st["s_w7"], 48)
        dve.tensor_copy(Wch[:], Wcf[:]).then_inc(sem["wch"], 1)
        dve.wait_ge(sem["wch"], 1)
        dve.tensor_tensor(Wcl[:], Wcf[:], Wch[:].bitcast(F32), ALU.subtract).then_inc(sem["wcl"], 1)
        dve.wait_ge(sem["wh"], 1)
        dve.tensor_tensor(W2l[:], W2f[:], W2h[:].bitcast(F32), ALU.subtract).then_inc(sem["wl"], 1)
        dve.wait_ge(sem["wl"], 1)
        dve.wait_ge(sem["wcl"], 1)
        dve.wait_ge(sem["w"], 16)
        dve.sem_inc(sem["sum"], 2)

        def body(k, r, at, on):
            if "second" in on:
                for u in range(B):
                    dve.wait_ge(sem["w2"], at(B, B + u + 1))
                    if k >= 1 and u == 0:
                        dve.wait_ge(sem["m"], at(1, 0))
                    dve.tensor_tensor(x2[:, 1 - r, u, :], ps[:, 2 + u, :], b2[:], ALU.add).then_inc(sem["x2"], 1)
            if "mish2" in on:
                dve.wait_ge(sem["sum"], at(1, 1))
                for u in range(B):
                    dve.tensor_scalar(oh[:, r, u, :], cx.iota_h[:], cx.dst_f[:, bass.ds(at(B, u), 1)],
                                      None, ALU.is_equal).then_inc(sem["oh"], 1)
            if "mish1" in on:
                dve.wait_ge(sem["t1"], at(1, 3))
                if k >= -1:
                    dve.wait_ge(sem["hl"], at(1, 2))
                dve.tensor_tensor(f[:, 0], x1[:, r].rearrange("p c e -> p (c e)"), t[:, r, 0], ALU.mult
                                  ).then_inc(sem["h"], 1)
                dve.wait_ge(sem["h"], at(1, 3))
                if k >= 0:
                    dve.wait_ge(sem["w2"], at(B, B))
                dve.tensor_copy(hh[:, r].rearrange("p c e -> p (c e)"), f[:, 0]).then_inc(sem["hh"], 1)
                dve.wait_ge(sem["hh"], at(1, 3))
                dve.tensor_tensor(hl[:, r].rearrange("p c e -> p (c e)"), f[:, 0],
                                  hh[:, r].rearrange("p c e -> p (c e)").bitcast(F32), ALU.subtract
                                  ).then_inc(sem["hl"], 1)
            if "pre" in on:
                for h in range(2):
                    dve.wait_ge(sem["pre"], at(2, 7 + h))
                    if k >= -1 and h == 0:
                        dve.wait_ge(sem["h"], at(1, 2))
                    dve.tensor_copy(x1[:, 1 - r, 2 * h:2 * h + 2, :].rearrange("p c e -> p (c e)"),
                                    ps[:, h, :]).then_inc(sem["x1"], 1)
            if "mish2" in on:
                dve.wait_ge(sem["t2"], at(1, 1))
                if k >= 1:
                    dve.wait_ge(sem["ml"], at(1, 0))
                dve.tensor_tensor(f[:, 1], x2[:, r].rearrange("p u c -> p (u c)"), t[:, r, 1], ALU.mult
                                  ).then_inc(sem["m"], 1)
                dve.wait_ge(sem["m"], at(1, 1))
                dve.tensor_copy(mh[:, r].rearrange("p u c -> p (u c)"), f[:, 1]).then_inc(sem["mh"], 1)
                dve.wait_ge(sem["mh"], at(1, 1))
                dve.tensor_tensor(ml[:, r].rearrange("p u c -> p (u c)"), f[:, 1],
                                  mh[:, r].rearrange("p u c -> p (u c)").bitcast(F32), ALU.subtract
                                  ).then_inc(sem["ml"], 1)

        rounds(dve, body)

    @block.scalar
    def _(act):
        act.wait_ge(st["s_w7"], 48)
        act.activation(W2h[:], W2f[:], ACT.Copy).then_inc(sem["wh"], 1)

        def body(k, r, at, on):
            if "mish2" in on:
                act.wait_ge(sem["x2"], at(B, B))
                if k >= 1:
                    act.wait_ge(sem["t2"], at(1, 0))
                act.activation(q[:, 1], x2[:, r].rearrange("p u c -> p (u c)"), ACT.Sigmoid, scale=-1.0
                               ).then_inc(sem["q2"], 1)
            if "mish1" in on:
                act.wait_ge(sem["x1"], at(2, 6))
                if k >= -1:
                    act.wait_ge(sem["t1"], at(1, 2))
                act.activation(q[:, 0], x1[:, r].rearrange("p c e -> p (c e)"), ACT.Sigmoid, scale=-1.0
                               ).then_inc(sem["q1"], 1)
            if "mish1" in on:
                act.wait_ge(sem["q1"], at(1, 3))
                act.activation(q[:, 0], q[:, 0], ACT.Arctan).then_inc(sem["a1"], 1)
            if "mish2" in on:
                act.wait_ge(sem["q2"], at(1, 1))
                act.activation(q[:, 1], q[:, 1], ACT.Arctan).then_inc(sem["a2"], 1)
            if "mish1" in on:
                act.wait_ge(sem["a1"], at(1, 3))
                if k >= 0:
                    act.wait_ge(sem["h"], at(1, 1))
                act.activation(t[:, r, 0], q[:, 0], ACT.Sin, bias=cx.half_pi[:], scale=-2.0).then_inc(sem["t1"], 1)
            if "mish2" in on:
                act.wait_ge(sem["a2"], at(1, 1))
                if k >= 2:
                    act.wait_ge(sem["m"], at(1, -1))
                act.activation(t[:, r, 1], q[:, 1], ACT.Sin, bias=cx.half_pi[:], scale=-2.0).then_inc(sem["t2"], 1)

        rounds(act, body)

    @block.tensor
    def _(pe):
        for c in range(CT):
            pe.matmul(ps[:, 4 + c, :], cx.zero_r[:, 0:P], cx.zero_r[:], start=True, stop=False)
        pe.wait_ge(sem["wcl"], 1)

        def body(k, r, at, on):
            if "second" in on:
                if k == -1:
                    pe.wait_ge(sem["wl"], 1)
                pe.wait_ge(sem["hl"], at(1, 2))
                for u in range(B):
                    if k >= 0:
                        pe.wait_ge(sem["x2"], at(B, u + 1))
                    cols = slice(u * P, (u + 1) * P)
                    product(pe, ps[:, 2 + u, :],
                            [(a[:, 1 - r, c, cols], w[:, c, :]) for c in range(CT)
                             for a, w in ((hh, W2h), (hh, W2l), (hl, W2h))]).then_inc(sem["w2"], 1)
            if "sum" in on:
                pe.wait_ge(sem["ml"], at(1, 0))
                pe.wait_ge(sem["oh"], at(B, 0))
                for u in range(B):
                    for c in range(CT):
                        for a in (mh, ml):
                            m = pe.matmul(ps[:, 4 + c, :], a[:, 1 - r, u, c * P:(c + 1) * P], oh[:, 1 - r, u, :],
                                          start=False, stop=False)
                m.then_inc(sem["sum"], 1)
            if "pre" in on:
                for h in range(2):
                    if k >= -2:
                        pe.wait_ge(sem["x1"], at(2, 5 + h))
                    if h == 0:
                        pe.wait_ge(sem["gsum"], at(B, 4 * B))
                    for c in (2 * h, 2 * h + 1):
                        out = ps[:, h, (c % 2) * B * P:(c % 2 + 1) * B * P]
                        edges = cx.eaT[:, bass.ds(at(B * P, 3 * B * P), B * P)]
                        pe.matmul(out, Wch[:, c * P:(c + 1) * P], edges, start=True, stop=False)
                        for u in range(B):
                            pe.matmul(out[:, u * P:(u + 1) * P], g[:, 1 - r, u, 0, c * P:(c + 1) * P],
                                      cx.ident[:], is_transpose=True, start=False, stop=False)
                        m = pe.matmul(out, Wcl[:, c * P:(c + 1) * P], edges, start=False, stop=True)
                    m.then_inc(sem["pre"], 1)

        rounds(pe, body)
        for c in range(CT):
            pe.matmul(ps[:, 4 + c, :], cx.zero_r[:, 0:P], cx.zero_r[:], start=False, stop=True)

    tmp.close()
    cx.end_phase()


def edge_mlp_out(cx, st):
    nc, io = cx.nc, cx.io
    tmp = ExitStack()
    aggT = cx.sb("aggT", [P, CT, N], F32, tmp)
    b3 = cx.sb("b33", [P, CT], F32, tmp)
    xu = cx.sb("xu", [P, CT, N], F32, tmp)
    qu = cx.sb("qu", [P, CT, N], F32, tmp)
    uT = cx.sb("uT", [P, CT, N], F32, tmp)
    rowsb = cx.sb("rows3", [P, 3, C], F32, tmp)
    xb = cx.sb("xb3", [P, NT, C], F32, tmp)
    y = cx.sb("y3", [P, NT, C], F32, tmp)
    z = cx.sb("z3", [P, NT, C], F32, tmp)
    x_beta = cx.sb("x_beta", [P, NT, C], F32, tmp)
    n5, n6 = Norm(cx, "n5", tmp), Norm(cx, "n6", tmp)
    names = ("small", "aggT", "mm", "xu", "q", "a", "t", "u", "xb", "mm2", "y", "g", "xbeta", "r", "store")
    sem = {n: cx.sem("s9_" + n) for n in names}
    W = cx.wA[:].rearrange("p a k n -> p (a k) n")
    W3, W4 = W[:, 0:2 * CT, :], W[:, 2 * CT:3 * CT, :]
    ps = cx.ps
    parts = cx.sb("parts9", [P, 8 * C], F32R, tmp)
    split = Split(cx, "s9x", parts[:],
                  chunks([(W3[:, k, :], cx.xT[:, k, :]) for k in range(CT)]
                         + [(W3[:, CT + k, :], aggT[:, k, :]) for k in range(CT)], 0)
                  + chunks([(uT[:, k, :], W4[:, k, :]) for k in range(CT)], 4))
    block = tmp.enter_context(nc.Block())

    @block.sync
    def _(sp):
        sp.dma_start(b3[:], col(io["L3_gnn_b3"], CT), allow_slow_non_contiguous=True).then_inc(sem["small"], 16)
        for i, name in enumerate(("L3_gnn_b4", "L3_gnn_gamma", "L3_gnn_beta")):
            sp.dma_start(rowsb[:, i, :], row_b(io[name])).then_inc(sem["small"], 16)
        for n in range(NT):
            sp.wait_ge(n6.s_out, n + 1)
            sp.dma_start(rows(io["out"])[:, n], y[:, n, :]).then_inc(sem["store"], 16)
        sp.wait_ge(sem["store"], 16 * NT)

    @block.gpsimd
    def _(pool):
        pool.wait_ge(sem["small"], 64)
        for n in range(NT):
            pool.tensor_tensor(x_beta[:, n, :], cx.x[:, n, :], rowsb[:, 2, :], ALU.add).then_inc(sem["xbeta"], 1)

    @block.vector
    def _(dve):
        for c in range(1, CT, 2):
            dve.tensor_copy(aggT[:, c, :], ps[:, 4 + c, :]).then_inc(sem["aggT"], 1)
        split.vector(dve, 0, 4)
        dve.wait_ge(sem["small"], 64)
        for n in range(NT):
            dve.tensor_tensor(xb[:, n, :], cx.x[:, n, :], rowsb[:, 0, :], ALU.add).then_inc(sem["xb"], 1)
        split.vector(dve, 4, 2 * CT)
        for c in range(CT):
            dve.wait_ge(sem["mm"], c + 1)
            dve.tensor_scalar(xu[:, c, :], ps[:, c, :], b3[:, c:c + 1], None, ALU.add).then_inc(sem["xu"], 1)
        dve.wait_ge(sem["xu"], CT)
        for c in range(CT):
            dve.wait_ge(sem["t"], c + 1)
            dve.tensor_tensor(uT[:, c, :], xu[:, c, :], qu[:, c, :], ALU.mult).then_inc(sem["u"], 1)
        dve.wait_ge(sem["xb"], NT)
        split.vector(dve, 2 * CT, 3 * CT)
        for n in range(NT):
            dve.wait_ge(sem["mm2"], n + 1)
            dve.tensor_tensor(y[:, n, :], ps[:, 4 + n, :], xb[:, n, :], ALU.add).then_inc(sem["y"], 1)
        norm_vector(dve, n5, y, None, sem["y"])
        for n in range(NT):
            dve.scalar_tensor_tensor(out=xb[:, n, :], in0=y[:, n, :], scalar=n5.mv[:, n, 0:1],
                                     in1=rowsb[:, 1, :], op0=ALU.subtract, op1=ALU.mult).then_inc(sem["g"], 1)
        dve.wait_ge(sem["xbeta"], NT)
        for n in range(NT):
            dve.wait_ge(sem["g"], n + 1)
            dve.scalar_tensor_tensor(out=z[:, n, :], in0=xb[:, n, :], scalar=n5.rstd[:, n:n + 1],
                                     in1=x_beta[:, n, :], op0=ALU.mult, op1=ALU.add).then_inc(sem["r"], 1)
        norm_vector(dve, n6, z, y, sem["r"])

    @block.scalar
    def _(act):
        for c in range(0, CT, 2):
            act.activation(aggT[:, c, :], ps[:, 4 + c, :], ACT.Copy).then_inc(sem["aggT"], 1)
        act.wait_ge(st["s_w8"], 32)
        split.scalar(act, 0, CT)
        act.wait_ge(sem["aggT"], CT)
        split.scalar(act, CT, 2 * CT)
        for c in range(CT):
            act.wait_ge(sem["xu"], c + 1)
            act.activation(qu[:, c, :], xu[:, c, :], ACT.Sigmoid, scale=-1.0).then_inc(sem["q"], 1)
            act.wait_ge(sem["q"], c + 1)
            act.activation(qu[:, c, :], qu[:, c, :], ACT.Arctan).then_inc(sem["a"], 1)
        act.wait_ge(sem["a"], CT)
        for c in range(CT):
            act.activation(qu[:, c, :], qu[:, c, :], ACT.Sin, bias=cx.half_pi[:], scale=-2.0).then_inc(sem["t"], 1)
        for k in range(CT):
            act.wait_ge(sem["u"], k + 1)
            split.scalar(act, 2 * CT + k, 2 * CT + k + 1)
        norm_scalar(act, n5)
        norm_scalar(act, n6)

    @block.tensor
    def _(pe):
        split.tensor(pe, 0, 2 * CT, s_mm=sem["mm"])
        split.tensor(pe, 2 * CT, 3 * CT, s_mm=sem["mm2"])

    tmp.close()
    cx.end_phase()


def build_program(nc, io):
    with ExitStack() as stack:
        cx = Ctx(nc, io, stack)
        cx.ps = stack.enter_context(nc.psum_tensor("ps", [P, 8, 512], F32))
        cx.ident = cx.sb("ident", [P, P])
        cx.zero_r = cx.sb("zero_r", [P, C], F32R)
        cx.iota_h = cx.sb("iota_h", [P, N], FP16)
        cx.half_pi = cx.sb("half_pi", [P, 1])
        cx.ident_h = cx.sb("ident_h", [P, P], FP16)
        cx.src_h = cx.sb("src_h", [P, ET], FP16)
        cx.part_f = cx.sb("part_f", [P, NT])
        cx.x = cx.sb("x", [P, NT, C])
        cx.xT = cx.sb("xT", [P, CT, N])
        cx.src_i = cx.sb("src_i", [P, ET], I32)
        cx.dst_i = cx.sb("dst_i", [P, ET], I32)
        cx.src_f = cx.sb("src_f", [P, ET])
        cx.dst_f = cx.sb("dst_f", [P, ET])
        cx.wA = cx.sb("wA", [P, 4, CT, C])
        cx.wB = cx.sb("wB", [P, HT * HID])
        st = {"pair_i": cx.sb("pair_i", [P, ET], I32)}
        st["s_st"] = [stack.enter_context(nc.semaphore(f"s_st{i}")) for i in range(2)]
        for name in ("s_xT1", "s_xT2", "s_xT3", "s_x0", "s_vout", "s_bias", "s_sg", *(f"s_w{i}" for i in range(9))):
            st[name] = stack.enter_context(nc.semaphore(name))
        for name, shape in (("v_dram", [N, C]), ("s_dram", [N * N, H0]), ("xa_dram", [N, C]), ("xb_dram", [N, C])):
            st[name] = nc.dram_tensor(name, shape, F32).ap()
        st["weights0"] = [(cx.wA[:, i], f"L0_gnn_{n}") for i, n in enumerate(("Wq", "Wk", "Wv", "Wo"))]
        cx.eaT = cx.sb("eaT", [P, E], F32R)
        with ExitStack() as graph:
            cx.cnt = cx.sb("cnt", [P, NT, N], F32, graph)
            cx.pen = cx.sb("pen", [P, NT, N], F32, graph)
            cx.rcount = cx.sb("rcount", [P, N], F32, graph)
            cx.ea_mean = cx.sb("ea_mean", [P, N], F32, graph)
            with ExitStack() as layer0:
                st["src_row"] = cx.sb("src_row", [P, E], FP16, layer0)
                st["bias"] = cx.sb("bias", [P, ET, H0], F32, layer0)
                st["sg"] = cx.sb("sg", [P, ET, H0], F32, layer0)
                setup(cx, st)
                attention_scores(cx, st)
                edge_sums(cx, st)
                attention_edges(cx, st)
            attention_out(cx, st)
            with ExitStack() as layer1:
                h1 = cx.sb("h1", [P, NT * H1 * W_], F32, layer1)
                h2 = cx.sb("h2", [P, NT * H1 * W_], F32, layer1)
                gat(cx, st, "g1", gat1_weights(cx), CT, cx.xT, h1, h2, io["L1_gnn_a_src1"], io["L1_gnn_a_dst1"],
                    io["L1_gnn_b1"], st["s_w2"], 16, cx.x)
                gat(cx, st, "g2", cx.wB[:].rearrange("p (k n) -> p k n", k=HT), HT, gat_output(h1), h2, h1,
                    io["L1_gnn_a_src2"], io["L1_gnn_a_dst2"], io["L1_gnn_b2"], st["s_w3"], 16, None)
                gat_out(cx, st, gat_output(h2))
            residual_layer(cx, st)
        edge_mlp_nodes(cx, st)
        edge_mlp(cx, st)
        edge_mlp_out(cx, st)


USED = ("x", "src", "dst", "edge_attr_64", "edge_attr_8",
        *(f"L0_gnn_{n}" for n in ("Wq", "bq", "Wk", "bk", "Wv", "bv", "Wo", "bo", "ln1_g", "ln1_b", "ln2_g",
                                  "ln2_b", "W1", "b1", "W2", "b2")),
        *(f"L1_gnn_{n}" for n in ("W1", "a_src1", "a_dst1", "b1", "W2", "a_src2", "a_dst2", "b2", "Wfc", "bfc")),
        *(f"L2_gnn_{n}" for n in ("W1", "b1", "W2", "b2")),
        *(f"L3_gnn_{n}" for n in ("W1", "b1", "W2", "b2", "W3", "b3", "W4", "b4", "gamma", "beta")))


def kernel(**inputs):
    import numpy as np
    import concourse.bacc as bacc
    from concourse.bass_utils import run_bass_kernel_spmd

    nc = bacc.Bacc("TRN2", target_bir_lowering=False, num_devices=1)
    arrays, io = {}, {}
    for name in USED:
        a = np.ascontiguousarray(inputs[name])
        arrays[f"in_{name}_dram"] = a
        io[name] = nc.dram_tensor(f"in_{name}_dram", a.shape, mybir.dt.from_np(a.dtype), kind="ExternalInput").ap()
    io["out"] = nc.dram_tensor("out_0_dram", [N, C], F32, kind="ExternalOutput").ap()
    build_program(nc, io)
    r = run_bass_kernel_spmd(nc, [arrays], core_ids=[0])
    return r.results[0]["out_0_dram"]
```
